# Optimizing a Trainium2 kernel written in Bass

```python
import numpy as np
import jax
import jax.numpy as jnp

def _softmax(x, axis=-1):
    return jax.nn.softmax(x, axis=axis)

def _gelu(x):
    return jax.nn.gelu(x, approximate=True)

def _silu(x):
    return jax.nn.silu(x)

def _sigmoid(x):
    return jax.nn.sigmoid(x)

def _layernorm(x, axis=-1, eps=1e-05):
    m = jnp.mean(x, axis=axis, keepdims=True)
    v = jnp.var(x, axis=axis, keepdims=True)
    return (x - m) / jnp.sqrt(v + eps)

def _scatter_add(tgt, idx, src, axis=0):
    return tgt.at[idx].add(src)

def _segment_sum(src, seg, n):
    return jax.ops.segment_sum(src, seg, n)
kernel_name = 'mk_gnn_ffn_d1_gnn_r8_6ff0ff'

def setup_inputs(seed: int=0):
    np.random.seed(seed)
    _w = jnp.asarray

    def _rec_inputs():
        import jax
        import jax.numpy as jnp
        _gk = jax.random.key(seed)
        x = -0.0002117 + 1 * jax.random.normal(jax.random.fold_in(_gk, 1), (6250, 512), jnp.float32)
        src = jax.random.randint(jax.random.fold_in(_gk, 2), (100000,), 0, 6250, jnp.int32)
        dst = jnp.minimum((6250 * jax.random.uniform(jax.random.fold_in(_gk, 3), (100000,)) ** 2.0).astype(jnp.int32), 49999)
        _o = jnp.argsort(dst, stable=True)
        src = src[_o]
        dst = dst[_o]
        edge_attr_8 = jax.random.uniform(jax.random.fold_in(_gk, 12), (100000, 8), jnp.float32, 0.0, 1)
        return (x, src, dst, edge_attr_8)
    x, src, dst, edge_attr_8 = _rec_inputs()

    def _L0_gnn_setup():
        import jax, jax.numpy as jnp
        import numpy as np
        N = 6250
        E = 100000
        IN_DIM = 512
        OUT_DIM = 64
        NUM_HEADS = 8
        NEG_SLOPE = 0.2
        key = jax.random.key(seed)
        ks = jax.random.split(key, 8)
        feat = jax.random.normal(ks[0], (N, IN_DIM), dtype=jnp.float32)
        dist = jax.random.uniform(ks[1], (E, NUM_HEADS), dtype=jnp.float32)
        src = jax.random.randint(ks[2], (E,), 0, N, dtype=jnp.int32)
        dst = jax.random.randint(ks[3], (E,), 0, N, dtype=jnp.int32)
        W = jax.random.normal(ks[4], (NUM_HEADS * OUT_DIM, IN_DIM), dtype=jnp.float32) / np.sqrt(IN_DIM)
        b = jax.random.normal(ks[5], (NUM_HEADS * OUT_DIM,), dtype=jnp.float32) * 0.01
        w_att_src = jax.random.normal(ks[6], (NUM_HEADS, OUT_DIM), dtype=jnp.float32)
        w_att_dst = jax.random.normal(ks[7], (NUM_HEADS, OUT_DIM), dtype=jnp.float32)
        return {'feat': feat, 'dist': dist, 'src': src, 'dst': dst, 'W': W, 'b': b, 'w_att_src': w_att_src, 'w_att_dst': w_att_dst}
    _L0_gnn_all = _L0_gnn_setup()
    _L0_gnn_in = {k: v for k, v in _L0_gnn_all.items() if k in ('W', 'b', 'w_att_src', 'w_att_dst')}
    del _L0_gnn_all

    def _L0_ffn_setup():
        import jax, jax.numpy as jnp
        import numpy as np
        MARK_AX, OP_ADD, OP_SUB = (0, 1, 2)
        ALU_LO, ALU_HI = (16, 32)
        AX_CARRY_LO, AX_CARRY_HI = (48, 64)
        OPCODE_BASE = 80
        OUTPUT_LO, OUTPUT_HI, CARRY = (128, 144, 160)
        NIB_A, NIB_B, OP_START = (0, 1, 10)
        RESULT, CARRY_OUT = (100, 101)
        GE_POS, GE_DIM = (8, 160)
        OPC_ADD, OPC_SUB = (25, 26)
        B, S, D = (8, 512, 512)

        def _decode_nibble(x, base):
            return jnp.argmax(x[..., base:base + 16] > 0.5, axis=-1).astype(x.dtype)

        def _pipeline(h, W, b):
            for i in range(3):
                h = jnp.einsum('bspd,od->bspo', h, W[i]) + b[i]
                if i < 2:
                    h = jax.nn.relu(h)
            return h
        key = jax.random.key(seed)
        kx, k1, k2, k3, k4 = jax.random.split(key, 5)
        x_bd = jax.random.uniform(kx, (B, S, D), dtype=jnp.float32)
        Wa = jax.random.normal(k1, (3, GE_DIM, GE_DIM), dtype=jnp.float32) * 0.05
        ba = jax.random.normal(k2, (3, GE_DIM), dtype=jnp.float32) * 0.05
        Ws = jax.random.normal(k3, (3, GE_DIM, GE_DIM), dtype=jnp.float32) * 0.05
        bs = jax.random.normal(k4, (3, GE_DIM), dtype=jnp.float32) * 0.05
        return {'x_bd': x_bd, 'Wa': Wa, 'ba': ba, 'Ws': Ws, 'bs': bs}
    _L0_ffn_all = _L0_ffn_setup()
    _L0_ffn_in = {k: v for k, v in _L0_ffn_all.items() if k in ('Wa', 'ba', 'Ws', 'bs')}
    del _L0_ffn_all
    return {'x': x, 'src': src, 'dst': dst, 'edge_attr_8': edge_attr_8, 'L0_gnn_W': _L0_gnn_in['W'], 'L0_gnn_b': _L0_gnn_in['b'], 'L0_gnn_w_att_src': _L0_gnn_in['w_att_src'], 'L0_gnn_w_att_dst': _L0_gnn_in['w_att_dst'], 'L0_ffn_Wa': _L0_ffn_in['Wa'], 'L0_ffn_ba': _L0_ffn_in['ba'], 'L0_ffn_Ws': _L0_ffn_in['Ws'], 'L0_ffn_bs': _L0_ffn_in['bs']}

def reference(x, src, dst, edge_attr_8, L0_gnn_W, L0_gnn_b, L0_gnn_w_att_src, L0_gnn_w_att_dst, L0_ffn_Wa, L0_ffn_ba, L0_ffn_Ws, L0_ffn_bs):
    import jax
    import jax.numpy as jnp

    def _L0_gnn_ref(feat, dist, src, dst, W, b, w_att_src, w_att_dst):
        import jax, jax.numpy as jnp
        import numpy as np
        N = 6250
        E = 100000
        IN_DIM = 512
        OUT_DIM = 64
        NUM_HEADS = 8
        NEG_SLOPE = 0.2
        h = jax.nn.leaky_relu(feat @ W.T + b, negative_slope=NEG_SLOPE)
        h = h.reshape(N, NUM_HEADS, OUT_DIM)
        e_src = jnp.sum(h * w_att_src, axis=-1)
        e_dst = jnp.sum(h * w_att_dst, axis=-1)
        e = jax.nn.leaky_relu(e_src[src] + e_dst[dst], negative_slope=NEG_SLOPE)
        m = jax.ops.segment_max(e, dst, num_segments=N)
        ex = jnp.exp(e - m[dst])
        s = jax.ops.segment_sum(ex, dst, num_segments=N)
        a = ex / s[dst] * dist
        msg = h[src] * a[:, :, None]
        out = jax.ops.segment_sum(msg, dst, num_segments=N)
        return out.reshape(N, NUM_HEADS * OUT_DIM)

    def _L0_ffn_ref(x_bd, Wa, ba, Ws, bs):
        import jax, jax.numpy as jnp
        import numpy as np
        MARK_AX, OP_ADD, OP_SUB = (0, 1, 2)
        ALU_LO, ALU_HI = (16, 32)
        AX_CARRY_LO, AX_CARRY_HI = (48, 64)
        OPCODE_BASE = 80
        OUTPUT_LO, OUTPUT_HI, CARRY = (128, 144, 160)
        NIB_A, NIB_B, OP_START = (0, 1, 10)
        RESULT, CARRY_OUT = (100, 101)
        GE_POS, GE_DIM = (8, 160)
        OPC_ADD, OPC_SUB = (25, 26)
        B, S, D = (8, 512, 512)

        def _decode_nibble(x, base):
            return jnp.argmax(x[..., base:base + 16] > 0.5, axis=-1).astype(x.dtype)

        def _pipeline(h, W, b):
            for i in range(3):
                h = jnp.einsum('bspd,od->bspo', h, W[i]) + b[i]
                if i < 2:
                    h = jax.nn.relu(h)
            return h
        x = x_bd
        Bsz, seq, _ = x.shape
        x_ge = jnp.zeros((Bsz, seq, GE_POS, GE_DIM), dtype=x.dtype)
        x_ge = x_ge.at[..., 0, NIB_A].set(_decode_nibble(x, ALU_LO))
        x_ge = x_ge.at[..., 1, NIB_A].set(_decode_nibble(x, ALU_HI))
        x_ge = x_ge.at[..., 0, NIB_B].set(_decode_nibble(x, AX_CARRY_LO))
        x_ge = x_ge.at[..., 1, NIB_B].set(_decode_nibble(x, AX_CARRY_HI))
        x_ge = x_ge.at[..., :, OP_START + OPC_ADD].set(x[..., OPCODE_BASE + OPC_ADD][..., None])
        x_ge = x_ge.at[..., :, OP_START + OPC_SUB].set(x[..., OPCODE_BASE + OPC_SUB][..., None])
        mark = x[..., MARK_AX] > 0.5
        m_add = mark & (x[..., OP_ADD] > 0.5)
        m_sub = mark & ~(x[..., OP_ADD] > 0.5) & (x[..., OP_SUB] > 0.5)
        active = (m_add | m_sub).astype(x.dtype)
        y_add = _pipeline(x_ge, Wa, ba)
        y_sub = _pipeline(x_ge, Ws, bs)
        y = jnp.where(m_add[..., None, None], y_add, jnp.where(m_sub[..., None, None], y_sub, x_ge))
        res_lo = jnp.clip(jnp.round(y[..., 0, RESULT]), 0, 15).astype(jnp.int32)
        res_hi = jnp.clip(jnp.round(y[..., 1, RESULT]), 0, 15).astype(jnp.int32)
        oh_lo = jax.nn.one_hot(res_lo, 16, dtype=x.dtype) * active[..., None]
        oh_hi = jax.nn.one_hot(res_hi, 16, dtype=x.dtype) * active[..., None]
        carry = (jnp.round(y[..., 1, CARRY_OUT]) > 0.5).astype(x.dtype) * active
        out = x
        out = out.at[..., OUTPUT_LO:OUTPUT_LO + 16].add(2.0 * oh_lo)
        out = out.at[..., OUTPUT_HI:OUTPUT_HI + 16].add(2.0 * oh_hi)
        out = out.at[..., CARRY].add(carry)
        return out
    x = x + _L0_gnn_ref(_layernorm(x, axis=-1), edge_attr_8, src, dst, L0_gnn_W, L0_gnn_b, L0_gnn_w_att_src, L0_gnn_w_att_dst)
    x = x + _L0_ffn_ref(_layernorm(x, axis=-1)[None], L0_ffn_Wa, L0_ffn_ba, L0_ffn_Ws, L0_ffn_bs)[0]
    return x

_drawn_inputs = setup_inputs


def setup_inputs(seed=0):
    import zlib

    import numpy as np

    out = dict(_drawn_inputs(seed))
    spreads = {}
    factors = {'L0_gnn_b': 8.0}
    for name, (base, spread) in spreads.items():
        noise = np.random.default_rng([zlib.crc32(name.encode()), seed]).standard_normal(out[name].shape)
        drawn = base * np.exp(spread * noise) if base else spread * noise
        out[name] = jnp.asarray(drawn.astype(out[name].dtype))
    for name, factor in factors.items():
        out[name] = (out[name] * factor).astype(out[name].dtype)
    return out
```

```python
from contextlib import ExitStack

import concourse.bass as bass
import numpy as np
from concourse import mybir

F32 = mybir.dt.float32
I32 = mybir.dt.int32
ALU = mybir.AluOpType
ACT = mybir.ActivationFunctionType
AX = mybir.AxisListType.X

P = 128
N, D, HEADS, E = 6250, 512, 8, 100000
HD = D // HEADS
SLOPE = 0.2
EPS = 1e-5
NODE_TILES = -(-N // P)
NODES = NODE_TILES * P
ROWS = NODES + P
NOWHERE = NODES
DC = D // P
ROW = D + HEADS
EDGE_TILES = -(-E // P)
TINY = 1e-30
FAR = 1 << 20
LOWEST = -3e38

GE = 160
REM = GE - P
RESULT, CARRY_OUT = 100, 101
NIB_A, NIB_B, OP_ADD_IN, OP_SUB_IN = 0, 1, 35, 36
X_OP_ADD, X_OP_SUB = 105, 106
FEATS = 8
COMBOS = [(0, 0), (0, 1), (1, 0), (1, 1)]
OUTS = 6
CHUNK = 4
CHUNKS = NODE_TILES // CHUNK


def turns(eng, total):
    yield 0, 0
    yield 1, 1
    with eng.Fori(1, total // 2) as i:
        yield 2 * i, 0
        yield 2 * i + 1, 1
    if total % 2:
        yield total - 1, 0


def reused(turn, slots=2):
    return not (isinstance(turn, int) and turn < slots)


def dma_count(turn, slot, slots=2):
    if isinstance(turn, int):
        return 16 * ((turn - slot) // slots + 1)
    return (turn - slot) * (16 // slots) + 16


def wait_alone(eng, semaphore, value, went_on):
    eng.wait_ge(semaphore, value)
    eng.sem_inc(went_on, 1)


def edge_turns(eng):
    yield 0
    with eng.Fori(1, EDGE_TILES) as n:
        yield n


def project(nc, top, banks, t, keep):
    with ExitStack() as ctx:
        def sb(name, shape, dt=F32):
            return ctx.enter_context(nc.sbuf_tensor(name, shape, dt))

        def sem(name):
            return top.enter_context(nc.semaphore(name))

        wt = sb("wt", [P, DC, D])
        bias_row = sb("bias_row", [1, D])
        ones_row = sb("ones_row", [1, P])
        w_src = sb("w_src", [P, D])
        w_dst = sb("w_dst", [P, D])
        zeros = sb("zeros", [P, ROW])
        xt = sb("xt", [P, 2, D])
        xn = sb("xn", [P, 2, D])
        xnT = sb("xnT", [P, 2, D])
        stats = sb("stats", [P, 2, 6])
        mean_var = sb("mean_var", [P, 2, 2])
        var_eps = sb("var_eps", [P, 2, 1])
        std = sb("std", [P, 2, 1])
        rstd = sb("rstd", [P, 2, 1])
        leak = sb("leak", [P, 2, D])
        hrow = sb("hrow", [P, 2, ROW])
        prod_src = sb("prod_src", [P, D])
        prod_dst = sb("prod_dst", [P, 2, D])
        ps_t, ps_h = banks[0:2], banks[2:4]

        s_const = sem("const_loaded")
        s_set = sem("const_set")
        s_zero = sem("zeros_set")
        s_ztab = sem("zeros_stored")
        s_dve_on = sem("dve_went_on")
        s_x = [sem("x_loaded0"), sem("x_loaded1")]
        s_stats, s_mv, s_ve = sem("stats_ready"), sem("meanvar_ready"), sem("vareps_ready")
        s_std, s_rstd, s_xn = sem("std_ready"), sem("rstd_ready"), sem("xn_ready")
        s_tr, s_xnT = sem("transposed"), sem("xnT_ready")
        s_h, s_leak, s_row = sem("h_ready"), sem("leak_ready"), sem("hrow_ready")
        s_psrc, s_esrc = sem("prod_src_ready"), sem("esrc_ready")
        s_pdst, s_edst = sem("prod_dst_ready"), sem("edst_ready")
        s_out = [sem("hrow_stored0"), sem("hrow_stored1")]

        with nc.Block() as block:
            @block.sync
            def _(sp):
                sp.dma_start(wt[:, :, :], t["wt"].rearrange("(c p) n -> p c n", p=P)).then_inc(s_const, 16)
                sp.dma_start(bias_row[:, :], t["bias"]).then_inc(s_const, 16)
                sp.dma_start(w_src[:, :], t["w_src"]).then_inc(s_const, 16)
                sp.dma_start(w_dst[:, :], t["w_dst"]).then_inc(s_const, 16)
                sp.dma_start(keep["ident"][:, :], t["ident"]).then_inc(s_const, 16)
                for n, s in turns(sp, NODE_TILES):
                    if reused(n):
                        sp.wait_ge(s_xn, n - 1)
                    sp.dma_start(xt[:, s, :], t["x"][bass.ds(n * P, P), :]).then_inc(s_x[s], 16)

            @block.gpsimd
            def _(pool):
                nc.gpsimd.memset(zeros[:, :], 0.0).then_inc(s_zero, 1)
                nc.gpsimd.memset(ones_row[:, :], 1.0).then_inc(s_set, 1)
                pool.wait_ge(s_const, 5 * 16)
                for n, s in turns(pool, NODE_TILES):
                    pool.wait_ge(s_row, n + 1)
                    if reused(n):
                        pool.wait_ge(s_edst, n - 1)
                    nc.gpsimd.tensor_tensor(prod_dst[:, s, :], hrow[:, s, 0:D], w_dst[:, :],
                                            ALU.mult).then_inc(s_pdst, 1)

            def scores(dve, n, s):
                dve.wait_ge(s_leak, n + 1)
                dve.wait_ge(s_h, n + 1)
                if reused(n):
                    dve.wait_ge(s_out[s], dma_count(n - 2, s))
                    dve.wait_ge(s_pdst, n - 1)
                nc.vector.tensor_tensor(hrow[:, s, 0:D], leak[:, s, :], ps_h[s][:, :], ALU.max).then_inc(s_row, 1)
                dve.wait_ge(s_row, n + 1)
                if reused(n, 1):
                    dve.wait_ge(s_esrc, 2 * n)
                nc.vector.tensor_tensor(prod_src[:, :], hrow[:, s, 0:D], w_src[:, :], ALU.mult).then_inc(s_psrc, 1)
                dve.wait_ge(s_psrc, n + 1)
                src_heads = prod_src[:, :].rearrange("p (h d) -> p h d", h=HEADS)
                nc.vector.tensor_reduce(hrow[:, s, D:ROW], src_heads, AX, ALU.add).then_inc(s_esrc, 1)
                nc.vector.tensor_reduce(keep["esrc"][:, bass.ds(n * HEADS, HEADS)], src_heads, AX,
                                        ALU.add).then_inc(s_esrc, 1)
                dve.wait_ge(s_pdst, n + 1)
                dst_heads = prod_dst[:, s, :].rearrange("p (h d) -> p h d", h=HEADS)
                nc.vector.tensor_reduce(keep["edst"][:, bass.ds(n * HEADS, HEADS)], dst_heads, AX,
                                        ALU.add).then_inc(s_edst, 1)

            @block.vector
            def _(dve):
                dve.wait_ge(s_const, 5 * 16)
                for n, s in turns(dve, NODE_TILES):
                    dve.wait_ge(s_x[s], dma_count(n, s))
                    nc.vector.bn_stats(stats[:, s, :], xt[:, s, :]).then_inc(s_stats, 1)
                    wait_alone(dve, s_stats, n + 1, s_dve_on)
                    nc.vector.bn_aggr(mean_var[:, s, :], stats[:, s, :]).then_inc(s_mv, 1)
                    dve.wait_ge(s_mv, n + 1)
                    if reused(n):
                        dve.wait_ge(s_std, n - 1)
                    nc.vector.tensor_scalar_add(var_eps[:, s, :], mean_var[:, s, 1:2], EPS).then_inc(s_ve, 1)
                    dve.wait_ge(s_std, n + 1)
                    nc.vector.reciprocal(rstd[:, s, :], std[:, s, :]).then_inc(s_rstd, 1)
                    dve.wait_ge(s_rstd, n + 1)
                    if reused(n):
                        dve.wait_ge(s_tr, n - 1)
                    nc.vector.tensor_scalar(xn[:, s, :], xt[:, s, :], mean_var[:, s, 0:1], rstd[:, s, :],
                                            ALU.subtract, ALU.mult).then_inc(s_xn, 1)
                    if isinstance(n, int) and n == 0:
                        continue
                    scores(dve, n - 1, 1 - s)
                scores(dve, NODE_TILES - 1, (NODE_TILES - 1) % 2)

            @block.tensor
            def _(pe):
                pe.wait_ge(s_const, 5 * 16)
                pe.wait_ge(s_set, 1)

                def gemm(n, s):
                    pe.wait_ge(s_xnT, n + 1)
                    if reused(n):
                        pe.wait_ge(s_row, n - 1)
                    nc.tensor.matmul(ps_h[s][:, :], ones_row[:, :], bias_row[:, :], start=True, stop=False)
                    for c in range(DC):
                        last = nc.tensor.matmul(ps_h[s][:, :], xnT[:, s, c * P:(c + 1) * P], wt[:, c, :],
                                                start=False, stop=(c == DC - 1))
                    last.then_inc(s_h, 1)

                for n, s in turns(pe, NODE_TILES):
                    pe.wait_ge(s_xn, n + 1)
                    if reused(n):
                        pe.wait_ge(s_xnT, n - 1)
                    for c in range(DC):
                        last = nc.tensor.transpose(ps_t[s][:, c * P:(c + 1) * P], xn[:, s, c * P:(c + 1) * P],
                                                   keep["ident"][:, :])
                    last.then_inc(s_tr, 1)
                    if isinstance(n, int) and n == 0:
                        continue
                    gemm(n - 1, 1 - s)
                gemm(NODE_TILES - 1, (NODE_TILES - 1) % 2)

            @block.scalar
            def _(act):
                def leaky(n, s):
                    act.wait_ge(s_h, n + 1)
                    if reused(n):
                        act.wait_ge(s_row, n - 1)
                    nc.scalar.activation(leak[:, s, :], ps_h[s][:, :], ACT.Copy, scale=SLOPE).then_inc(s_leak, 1)

                def store(n, s):
                    act.wait_ge(s_esrc, 2 * (n + 1))
                    act.dma_start(t["h"][bass.ds(n * P, P), :], hrow[:, s, :]).then_inc(s_out[s], 16)

                act.wait_ge(s_zero, 1)
                act.dma_start(t["h"][NODES:ROWS, :], zeros[:, :]).then_inc(s_ztab, 16)
                act.dma_start(t["agg"][NODES:ROWS, :], zeros[:, :]).then_inc(s_ztab, 16)
                for n, s in turns(act, NODE_TILES):
                    act.dma_start(t["agg"][bass.ds(n * P, P), :], zeros[:, :]).then_inc(s_ztab, 16)
                    act.wait_ge(s_ve, n + 1)
                    if reused(n):
                        act.wait_ge(s_rstd, n - 1)
                    nc.scalar.activation(std[:, s, :], var_eps[:, s, :], ACT.Sqrt).then_inc(s_std, 1)
                    act.wait_ge(s_tr, n + 1)
                    if reused(n):
                        act.wait_ge(s_h, n - 1)
                    nc.scalar.activation(xnT[:, s, :], ps_t[s][:, :], ACT.Copy).then_inc(s_xnT, 1)
                    if isinstance(n, int) and n == 0:
                        continue
                    leaky(n - 1, 1 - s)
                    if isinstance(n, int) and n == 1:
                        continue
                    store(n - 2, s)
                leaky(NODE_TILES - 1, 0)
                store(NODE_TILES - 2, 1)
                store(NODE_TILES - 1, 0)
                act.wait_ge(s_out[0], dma_count(NODE_TILES - 1, 0))
                act.wait_ge(s_out[1], dma_count(NODE_TILES - 2, 1))
                act.wait_ge(s_ztab, 16 * (NODE_TILES + 2))


def attend_any(nc, top, banks, t, keep):
    with ExitStack() as ctx:
        def sb(name, shape, dt=F32):
            return ctx.enter_context(nc.sbuf_tensor(name, shape, dt))

        def sem(name):
            return top.enter_context(nc.semaphore(name))

        pairs = sb("pairs", [P, EDGE_TILES, 2], I32)
        dist = sb("dist", [P, EDGE_TILES, HEADS])
        before = sb("before", [P, P])
        med = sb("med", [P, NODE_TILES + 1, 2 * HEADS])
        src_idx = sb("src_idx", [P, 1], I32)
        dst_idx = sb("dst_idx", [P, 1], I32)
        put_idx = sb("put_idx", [P, 1], I32)
        dcol = sb("dcol", [P, 1])
        dst_wide = sb("dst_wide", [P, P])
        e_wide = sb("e_wide", [P, HEADS, P])
        same = sb("same", [P, P])
        penalty = sb("penalty", [P, P])
        masked = sb("masked", [P, HEADS, P])
        earlier = sb("earlier", [P, P])
        n_earlier = sb("n_earlier", [P, 1])
        grow = sb("grow", [P, ROW])
        arow = sb("arow", [P, ROW])
        anew = sb("anew", [P, ROW])
        mrow = sb("mrow", [P, 2 * HEADS])
        mnew = sb("mnew", [P, 2 * HEADS])
        score = sb("score", [P, HEADS])
        e = sb("e", [P, HEADS])
        tile_max = sb("tile_max", [P, HEADS])
        diffs = sb("diffs", [P, 2 * HEADS])
        exps = sb("exps", [P, 2 * HEADS])
        coef = sb("coef", [P, HEADS])
        msg = sb("msg", [P, D])
        put_f = sb("put_f", [P, 1])
        wide_t = banks[0]
        e_t = [banks[1], banks[2]]
        sums, weights = banks[3], banks[4]

        s_load = sem("edges_loaded")
        s_set = sem("med_set")
        s_med = sem("med_stored")
        s_src, s_dst, s_dc, s_put = sem("src_idx_set"), sem("dst_idx_set"), sem("dcol_set"), sem("put_idx_set")
        s_pool_on = sem("pool_went_on")
        s_g, s_a, s_m = sem("g_gathered"), sem("a_gathered"), sem("m_gathered")
        s_ap, s_mp = sem("a_put"), sem("m_put")
        names = ("dst_wide dstT same penalty earlier n_earlier put_f score e e_wide eT masked tile_max "
                 "mnew diffs exps coef msg sums anew").split()
        done = {k: sem("any_" + k) for k in names}
        s_scaled = sem("any_scaled")

        with nc.Block() as block:
            @block.sync
            def _(sp):
                sp.dma_start(pairs[:, :, :], t["pairs"]).then_inc(s_load, 16)
                sp.dma_start(dist[:, :, :], t["dist"]).then_inc(s_load, 16)
                sp.dma_start(before[:, :], t["before"]).then_inc(s_load, 16)
                sp.wait_ge(s_set, 3)
                sp.dma_start(t["med"].rearrange("(n p) c -> p n c", p=P), med[:, :, :]).then_inc(s_med, 16)
                sp.wait_ge(s_med, 16)

            @block.gpsimd
            def _(pool):
                pool.wait_ge(s_med, 16)

                def gather(out, table, idx, semaphore):
                    pool.indirect_dma_start(out=out[:, :], out_offset=None, in_=table[:, :],
                                            in_offset=bass.IndirectOffsetOnAxis(ap=idx[:, :], axis=0)
                                            ).then_inc(semaphore, 16)

                def scatter(table, row, semaphore):
                    pool.indirect_dma_start(out=table[:, :],
                                            out_offset=bass.IndirectOffsetOnAxis(ap=put_idx[:, :], axis=0),
                                            in_=row[:, :], in_offset=None, bounds_check=ROWS - 1,
                                            oob_is_err=False).then_inc(semaphore, 16)

                for n in edge_turns(pool):
                    wait_alone(pool, s_src, n + 1, s_pool_on)
                    gather(grow, t["h"], src_idx, s_g)
                    wait_alone(pool, s_dst, n + 1, s_pool_on)
                    gather(arow, t["agg"], dst_idx, s_a)
                    gather(mrow, t["med"], dst_idx, s_m)
                    pool.wait_ge(s_put, n + 1)
                    wait_alone(pool, done["anew"], 2 * (n + 1), s_pool_on)
                    scatter(t["agg"], anew, s_ap)
                    scatter(t["med"], mnew, s_mp)
                    pool.wait_ge(s_ap, 16 * (n + 1))
                    pool.wait_ge(s_mp, 16 * (n + 1))

            @block.vector
            def _(dve):
                dve.wait_ge(s_load, 3 * 16)
                nc.vector.memset(med[:, :, 0:HEADS], LOWEST).then_inc(s_set, 1)
                nc.vector.memset(med[:, NODE_TILES, HEADS:2 * HEADS], 0.0).then_inc(s_set, 1)
                nc.vector.tensor_copy(med[:, 0:NODE_TILES, HEADS:2 * HEADS],
                                      keep["edst"][:, :].rearrange("p (n h) -> p n h", h=HEADS)).then_inc(s_set, 1)

                def heads(ap):
                    return ap.rearrange("p (h d) -> p h d", h=HEADS)

                for n in edge_turns(dve):
                    def step(name, ins):
                        ins.then_inc(done[name], 1)
                        dve.wait_ge(done[name], n + 1)

                    if reused(n, 1):
                        dve.wait_ge(s_mp, 16 * n)
                        dve.wait_ge(s_ap, 16 * n)
                    nc.vector.tensor_copy(src_idx[:, :], pairs[:, bass.ds(n, 1), 0]).then_inc(s_src, 1)
                    nc.vector.tensor_copy(dst_idx[:, :], pairs[:, bass.ds(n, 1), 1]).then_inc(s_dst, 1)
                    nc.vector.tensor_copy(dcol[:, :], pairs[:, bass.ds(n, 1), 1]).then_inc(s_dc, 1)
                    dve.wait_ge(s_dc, n + 1)
                    step("dst_wide", nc.vector.tensor_copy(dst_wide[:, :], dcol[:, 0:1].to_broadcast([P, P])))
                    dve.wait_ge(done["dstT"], n + 1)
                    step("same", nc.vector.tensor_scalar(same[:, :], wide_t[:, 0:P], dcol[:, 0:1], None,
                                                         ALU.is_equal))
                    nc.vector.tensor_scalar(penalty[:, :], same[:, :], -1.0, -LOWEST, ALU.add,
                                            ALU.mult).then_inc(done["penalty"], 1)
                    step("earlier", nc.vector.tensor_tensor(earlier[:, :], same[:, :], before[:, :], ALU.mult))
                    step("n_earlier", nc.vector.tensor_reduce(n_earlier[:, :], earlier[:, :], AX, ALU.max))
                    step("put_f", nc.vector.scalar_tensor_tensor(put_f[:, :], n_earlier[:, :], float(FAR),
                                                                 dcol[:, :], ALU.mult, ALU.add))
                    nc.vector.tensor_copy(put_idx[:, :], put_f[:, :]).then_inc(s_put, 1)

                    dve.wait_ge(s_g, 16 * (n + 1))
                    dve.wait_ge(s_m, 16 * (n + 1))
                    step("score", nc.vector.tensor_tensor(score[:, :], grow[:, D:ROW], mrow[:, HEADS:2 * HEADS],
                                                          ALU.add))
                    step("e", nc.vector.scalar_tensor_tensor(e[:, :], score[:, :], SLOPE, score[:, :], ALU.mult,
                                                             ALU.max))
                    step("e_wide", nc.vector.tensor_copy(e_wide[:, :, :], e[:, :].unsqueeze(2)
                                                         .to_broadcast([P, HEADS, P])))
                    dve.wait_ge(done["eT"], n + 1)
                    dve.wait_ge(done["penalty"], n + 1)
                    half = HEADS // 2
                    for b in range(2):
                        last = nc.vector.tensor_tensor(
                            masked[:, b * half:(b + 1) * half, :],
                            e_t[b][:, :].rearrange("p (h c) -> p h c", h=half),
                            penalty[:, :].unsqueeze(1).to_broadcast([P, half, P]), ALU.add)
                        if b == 0:
                            last.then_inc(done["masked"], 1)
                    last.then_inc(done["masked"], 1)
                    dve.wait_ge(done["masked"], 2 * (n + 1))
                    step("tile_max", nc.vector.tensor_reduce(tile_max[:, :], masked[:, :, :], AX, ALU.max))
                    nc.vector.tensor_copy(mnew[:, HEADS:2 * HEADS], mrow[:, HEADS:2 * HEADS]
                                          ).then_inc(done["mnew"], 1)
                    nc.vector.tensor_tensor(mnew[:, 0:HEADS], mrow[:, 0:HEADS], tile_max[:, :], ALU.max
                                            ).then_inc(done["mnew"], 1)
                    dve.wait_ge(done["mnew"], 2 * (n + 1))
                    nc.vector.tensor_tensor(diffs[:, 0:HEADS], mrow[:, 0:HEADS], mnew[:, 0:HEADS],
                                            ALU.subtract).then_inc(done["diffs"], 1)
                    nc.vector.tensor_tensor(diffs[:, HEADS:2 * HEADS], e[:, :], mnew[:, 0:HEADS],
                                            ALU.subtract).then_inc(done["diffs"], 1)
                    dve.wait_ge(done["exps"], n + 1)
                    step("coef", nc.vector.tensor_tensor(
                        coef[:, :], exps[:, HEADS:2 * HEADS],
                        dist[:, bass.ds(n, 1), :].rearrange("p o h -> p (o h)"), ALU.mult))
                    nc.vector.tensor_tensor(heads(msg[:, :]), heads(grow[:, 0:D]),
                                            coef[:, :].unsqueeze(2).to_broadcast([P, HEADS, HD]), ALU.mult
                                            ).then_inc(done["msg"], 1)
                    dve.wait_ge(s_a, 16 * (n + 1))
                    nc.vector.tensor_tensor(heads(arow[:, 0:D]), heads(arow[:, 0:D]),
                                            exps[:, 0:HEADS].unsqueeze(2).to_broadcast([P, HEADS, HD]),
                                            ALU.mult).then_inc(s_scaled, 1)
                    nc.vector.tensor_tensor(arow[:, D:ROW], arow[:, D:ROW], exps[:, 0:HEADS],
                                            ALU.mult).then_inc(s_scaled, 1)
                    dve.wait_ge(s_scaled, 2 * (n + 1))
                    dve.wait_ge(done["sums"], n + 1)
                    nc.vector.tensor_tensor(anew[:, 0:D], arow[:, 0:D], sums[:, :], ALU.add
                                            ).then_inc(done["anew"], 1)
                    nc.vector.tensor_tensor(anew[:, D:ROW], arow[:, D:ROW], weights[:, 0:HEADS], ALU.add
                                            ).then_inc(done["anew"], 1)

            @block.scalar
            def _(act):
                for n in edge_turns(act):
                    act.wait_ge(done["diffs"], 2 * (n + 1))
                    nc.scalar.activation(exps[:, :], diffs[:, :], ACT.Exp).then_inc(done["exps"], 1)

            @block.tensor
            def _(pe):
                for n in edge_turns(pe):
                    pe.wait_ge(done["dst_wide"], n + 1)
                    nc.tensor.transpose(wide_t[:, 0:P], dst_wide[:, :], keep["ident"][:, :]
                                        ).then_inc(done["dstT"], 1)
                    pe.wait_ge(done["e_wide"], n + 1)
                    for h in range(HEADS):
                        k = h % (HEADS // 2)
                        last = nc.tensor.transpose(e_t[h // (HEADS // 2)][:, k * P:(k + 1) * P], e_wide[:, h, :],
                                                   keep["ident"][:, :])
                    last.then_inc(done["eT"], 1)
                    pe.wait_ge(done["msg"], n + 1)
                    nc.tensor.matmul(sums[:, :], same[:, :], msg[:, :], start=True, stop=True)
                    nc.tensor.matmul(weights[:, 0:HEADS], same[:, :], exps[:, HEADS:2 * HEADS], start=True,
                                     stop=True).then_inc(done["sums"], 1)


def finish(nc, top, banks, t, keep):
    with ExitStack() as ctx:
        def sb(name, shape, dt=F32):
            return ctx.enter_context(nc.sbuf_tensor(name, shape, dt))

        def sem(name):
            return top.enter_context(nc.semaphore(name))

        C = CHUNK
        w1 = sb("w1", [FEATS, 5, P])
        w2 = sb("w2", [P, 13, P])
        w3 = sb("w3", [P, 5, 8])
        b2 = sb("b2", [P, 5])
        b3 = sb("b3", [P, 8])
        countdown = sb("countdown", [P, 64])
        digits = sb("digits", [P, 2, 16])
        x = sb("x_in", [P, 2, C, D])
        agg = sb("agg_in", [P, 2, C, ROW])
        y = sb("y", [P, C, D])
        res = sb("res", [P, 2, C, D])
        wsum = sb("wsum", [P, C, HEADS])
        rsum = sb("rsum", [P, C, HEADS])
        stats = sb("fstats", [P, C, 6])
        mean_var = sb("fmean_var", [P, C, 2])
        var_eps = sb("fvar_eps", [P, C])
        std = sb("fstd", [P, C])
        rstd = sb("frstd", [P, C])
        hits = sb("hits", [P, C, 64])
        best = sb("best", [P, C, 4])
        first = sb("first", [P, C, 4])
        feats = sb("feats", [P, 2, C, FEATS])
        flags = sb("flags", [P, C, 3])
        both = sb("both", [P, 2, C, 2])
        picks = sb("picks", [P, 2, C, 2])
        active = sb("active", [P, 2, C])
        active2 = sb("active2", [P, 2, C])
        featsT = sb("featsT", [FEATS, C * P])
        h1 = sb("h1", [P, 5, C * P])
        h2 = sb("h2", [P, 5, C * P])
        v3 = sb("v3", [P, C, 8])
        added = sb("added", [P, C, 3])
        subbed = sb("subbed", [P, C, 3])
        value = sb("value", [P, C, 3])
        clipped = sb("clipped", [P, C, 3])
        shifted = sb("shifted", [P, C, 3])
        rounded = sb("rounded", [P, C, 3])
        hot = sb("hot", [P, C, 2, 16])
        carry = sb("carry", [P, C])
        feats_t = banks[0]
        layer = banks[1:7]
        y3 = banks[7]

        s_dve_on = sem("fin_dve_went_on")
        s_w = sem("mlp_weights_loaded")
        s_ones = sem("feats_ones_set")
        s_in = [sem("chunk_loaded0"), sem("chunk_loaded1")]
        s_out = [sem("out_stored0"), sem("out_stored1")]
        per_chunk = ("wsum rsum x1 var_eps std rstd res best first feats_ops feats_nibbles flags both m_add all "
                     "m_sub active active2 feats_t featsT mm h1 h2 y3 v3 added subbed value clipped shifted "
                     "rounded carry carried").split()
        per_tile = "scaled stats mean_var y hits hot placed".split()
        d = {k: sem("fin_" + k) for k in per_chunk + per_tile}

        def chunks(eng):
            yield 0, 0, C
            yield 1, 1, C
            with eng.Fori(1, CHUNKS // 2) as i:
                yield 2 * i, 0, C
                yield 2 * i + 1, 1, C
            yield CHUNKS, 0, NODE_TILES - CHUNKS * C

        with nc.Block() as block:
            @block.sync
            def _(sp):
                for name, tile in (("w1", w1), ("w2", w2), ("w3", w3), ("b2", b2), ("b3", b3),
                                   ("countdown", countdown), ("digits", digits)):
                    whole = tile[:, :, :] if len(tile.shape) == 3 else tile[:, :]
                    sp.dma_start(whole, t[name]).then_inc(s_w, 16)

                def store(c, s, k):
                    sp.wait_ge(d["placed"], c * C + k)
                    sp.wait_ge(d["carried"], c + 1)
                    if k == C:
                        sp.dma_start(t["out"][bass.ds(c * (C * P), C * P), :].rearrange("(k p) n -> p k n", p=P),
                                     res[:, s, :, :]).then_inc(s_out[s], 16)
                    else:
                        rows = N - CHUNKS * C * P
                        sp.dma_start(t["out"][N - rows:N, :], res[0:rows, s, 0, :]).then_inc(s_out[s], 16)

                for c, s, k in chunks(sp):
                    if reused(c):
                        sp.wait_ge(d["res"], c - 1)
                    rows = bass.ds(c * (C * P), k * P)
                    sp.dma_start(x[:, s, 0:k, :], t["x"][rows, :].rearrange("(k p) n -> p k n", p=P)
                                 ).then_inc(s_in[s], 16)
                    sp.dma_start(agg[:, s, 0:k, :], t["agg"][rows, :].rearrange("(k p) n -> p k n", p=P)
                                 ).then_inc(s_in[s], 16)
                    if reused(c):
                        store(c - 2, s, C)
                store(CHUNKS - 1, 1, C)
                store(CHUNKS, 0, NODE_TILES - CHUNKS * C)
                sp.wait_ge(s_out[0], dma_count(CHUNKS, 0))
                sp.wait_ge(s_out[1], dma_count(CHUNKS - 1, 1))

            @block.gpsimd
            def _(pool):
                for c, s, k in chunks(pool):
                    pool.wait_ge(d["y"], c * C + k)
                    if reused(c):
                        pool.wait_ge(s_out[s], dma_count(c - 2, s))
                    nc.gpsimd.tensor_tensor(res[:, s, 0:k, :], x[:, s, 0:k, :], y[:, 0:k, :], ALU.add
                                            ).then_inc(d["res"], 1)

            @block.scalar
            def _(act):
                def relus(c, k):
                    w = k * P
                    act.wait_ge(d["feats_t"], c + 1)
                    if reused(c, 1):
                        act.wait_ge(d["mm"], 10 * c)
                    nc.scalar.activation(featsT[:, 0:w], feats_t[0:FEATS, 0:w], ACT.Copy).then_inc(d["featsT"], 1)
                    for g in range(5):
                        act.wait_ge(d["mm"], 10 * c + g + 1)
                        nc.scalar.activation(h1[:, g, 0:w], layer[g][:, 0:w], ACT.Relu).then_inc(d["h1"], 1)
                    for g in range(5):
                        act.wait_ge(d["mm"], 10 * c + 5 + g + 1)
                        if reused(c, 1):
                            act.wait_ge(d["y3"], c)
                        nc.scalar.activation(h2[:, g, 0:w], layer[(5 + g) % 6][:, 0:w], ACT.Relu,
                                             bias=b2[:, g:g + 1]).then_inc(d["h2"], 1)

                act.wait_ge(s_w, 7 * 16)
                for c, s, k in chunks(act):
                    act.wait_ge(d["var_eps"], c + 1)
                    nc.scalar.activation(std[:, 0:k], var_eps[:, 0:k], ACT.Sqrt).then_inc(d["std"], 1)
                    if isinstance(c, int) and c == 0:
                        continue
                    relus(c - 1, C)
                relus(CHUNKS, NODE_TILES - CHUNKS * C)

            @block.tensor
            def _(pe):
                pe.wait_ge(s_w, 7 * 16)
                for c, s, k in chunks(pe):
                    w = k * P
                    pe.wait_ge(s_ones, 2)
                    pe.wait_ge(d["feats_ops"], c + 1)
                    pe.wait_ge(d["feats_nibbles"], c + 1)
                    if reused(c, 1):
                        pe.wait_ge(d["featsT"], c)
                    for j in range(k):
                        last = nc.tensor.transpose(feats_t[0:FEATS, j * P:(j + 1) * P], feats[:, s, j, :],
                                                   keep["ident"][:, :])
                    last.then_inc(d["feats_t"], 1)
                    pe.wait_ge(d["featsT"], c + 1)
                    if reused(c, 1):
                        pe.wait_ge(d["h2"], 5 * c)
                    for g in range(5):
                        nc.tensor.matmul(layer[g][:, 0:w], w1[:, g, :], featsT[:, 0:w], start=True,
                                         stop=True).then_inc(d["mm"], 1)
                    pe.wait_ge(d["h1"], 5 * (c + 1))
                    for g in range(4):
                        bank = layer[(5 + g) % 6]
                        nc.tensor.matmul(bank[:, 0:w], w2[:, g, :], h1[:, g, 0:w], start=True, stop=False)
                        nc.tensor.matmul(bank[:, 0:w], w2[:, 4 + g, :], h1[:, 4, 0:w], start=False,
                                         stop=True).then_inc(d["mm"], 1)
                    bank = layer[9 % 6]
                    for g in range(5):
                        last = nc.tensor.matmul(bank[:, 0:w], w2[:, 8 + g, :], h1[:, g, 0:w], start=(g == 0),
                                                stop=(g == 4))
                    last.then_inc(d["mm"], 1)
                    pe.wait_ge(d["h2"], 5 * (c + 1))
                    if reused(c, 1):
                        pe.wait_ge(d["v3"], c)
                    for j in range(k):
                        for g in range(5):
                            last = nc.tensor.matmul(y3[:, 8 * j:8 * j + 8], h2[:, g, j * P:(j + 1) * P],
                                                    w3[:, g, :], start=(g == 0), stop=(g == 4))
                    last.then_inc(d["y3"], 1)

            @block.vector
            def _(dve):
                def front(c, s, k):
                    def need(name):
                        dve.wait_ge(d[name], c + 1)

                    def need_tiles(name):
                        dve.wait_ge(d[name], c * C + k)

                    loaded = 2 * dma_count(c, s) if isinstance(c, int) else (c - s) * 16 + 32
                    dve.wait_ge(s_in[s], loaded)
                    xk, ak = x[:, s, 0:k, :], agg[:, s, 0:k, :]
                    nc.vector.tensor_scalar_max(wsum[:, 0:k, :], ak[:, :, D:ROW], TINY).then_inc(d["wsum"], 1)
                    need("wsum")
                    nc.vector.reciprocal(rsum[:, 0:k, :], wsum[:, 0:k, :]).then_inc(d["rsum"], 1)
                    need("rsum")
                    for j in range(k):
                        heads = agg[:, s, j, 0:D].rearrange("p (h d) -> p h d", h=HEADS)
                        nc.vector.tensor_tensor(heads, heads, rsum[:, j, :].unsqueeze(2)
                                                .to_broadcast([P, HEADS, HD]), ALU.mult).then_inc(d["scaled"], 1)
                    need_tiles("scaled")
                    nc.vector.tensor_tensor(xk, xk, ak[:, :, 0:D], ALU.add).then_inc(d["x1"], 1)
                    need("x1")
                    for j in range(k):
                        nc.vector.bn_stats(stats[:, j, :], x[:, s, j, :]).then_inc(d["stats"], 1)
                    wait_alone(dve, d["stats"], c * C + k, s_dve_on)
                    for j in range(k):
                        nc.vector.bn_aggr(mean_var[:, j, :], stats[:, j, :]).then_inc(d["mean_var"], 1)
                    need_tiles("mean_var")
                    nc.vector.tensor_scalar_add(var_eps[:, 0:k], mean_var[:, 0:k, 1], EPS).then_inc(d["var_eps"], 1)
                    need("std")
                    nc.vector.reciprocal(rstd[:, 0:k], std[:, 0:k]).then_inc(d["rstd"], 1)
                    need("rstd")
                    if reused(c, 1):
                        dve.wait_ge(d["res"], c)
                    for j in range(k):
                        nc.vector.tensor_scalar(y[:, j, :], x[:, s, j, :], mean_var[:, j, 0:1], rstd[:, j:j + 1],
                                                ALU.subtract, ALU.mult).then_inc(d["y"], 1)
                    need_tiles("y")
                    if reused(c):
                        dve.wait_ge(d["feats_t"], c - 1)
                    nc.vector.tensor_copy(feats[:, s, 0:k, 4:6], y[:, 0:k, X_OP_ADD:X_OP_SUB + 1]
                                          ).then_inc(d["feats_ops"], 1)
                    for j in range(k):
                        nc.vector.scalar_tensor_tensor(hits[:, j, :], y[:, j, 16:80], 0.5, countdown[:, :],
                                                       ALU.is_gt, ALU.mult).then_inc(d["hits"], 1)
                    nc.vector.tensor_scalar(flags[:, 0:k, :], y[:, 0:k, 0:3], 0.5, None, ALU.is_gt
                                            ).then_inc(d["flags"], 1)
                    need_tiles("hits")
                    nc.vector.tensor_reduce(best[:, 0:k, :], hits[:, 0:k, :].rearrange("p k (f j) -> p k f j", j=16),
                                            AX, ALU.max).then_inc(d["best"], 1)
                    need("best")
                    nc.vector.tensor_scalar(first[:, 0:k, :], best[:, 0:k, :], -1.0, 16.0, ALU.mult, ALU.add
                                            ).then_inc(d["first"], 1)
                    need("first")
                    nc.vector.scalar_tensor_tensor(feats[:, s, 0:k, 0:4], best[:, 0:k, :], 0.0, first[:, 0:k, :],
                                                   ALU.is_gt, ALU.mult).then_inc(d["feats_nibbles"], 1)
                    need("flags")
                    mark, add, sub = (flags[:, 0:k, i] for i in range(3))
                    nc.vector.tensor_tensor(picks[:, s, 0:k, 0], mark, add, ALU.mult).then_inc(d["m_add"], 1)
                    nc.vector.tensor_tensor(both[:, s, 0:k, 0], mark, sub, ALU.mult).then_inc(d["both"], 1)
                    need("both")
                    nc.vector.tensor_tensor(both[:, s, 0:k, 1], both[:, s, 0:k, 0], add, ALU.mult
                                            ).then_inc(d["all"], 1)
                    need("all")
                    nc.vector.tensor_tensor(picks[:, s, 0:k, 1], both[:, s, 0:k, 0], both[:, s, 0:k, 1],
                                            ALU.subtract).then_inc(d["m_sub"], 1)
                    need("m_sub")
                    need("m_add")
                    nc.vector.tensor_tensor(active[:, s, 0:k], picks[:, s, 0:k, 0], picks[:, s, 0:k, 1], ALU.add
                                            ).then_inc(d["active"], 1)
                    need("active")
                    nc.vector.tensor_scalar_mul(active2[:, s, 0:k], active[:, s, 0:k], 2.0).then_inc(d["active2"], 1)

                def tail(c, s, k):
                    def need(name):
                        dve.wait_ge(d[name], c + 1)

                    need("y3")
                    nc.vector.tensor_tensor(v3[:, 0:k, :], y3[:, 0:8 * k].rearrange("p (k o) -> p k o", o=8),
                                            b3[:, :].unsqueeze(1).to_broadcast([P, k, 8]), ALU.add
                                            ).then_inc(d["v3"], 1)
                    need("v3")
                    nc.vector.tensor_tensor(added[:, 0:k, :], v3[:, 0:k, 0:3],
                                            picks[:, s, 0:k, 0:1].to_broadcast([P, k, 3]), ALU.mult
                                            ).then_inc(d["added"], 1)
                    nc.vector.tensor_tensor(subbed[:, 0:k, :], v3[:, 0:k, 3:6],
                                            picks[:, s, 0:k, 1:2].to_broadcast([P, k, 3]), ALU.mult
                                            ).then_inc(d["subbed"], 1)
                    need("added")
                    need("subbed")
                    nc.vector.tensor_tensor(value[:, 0:k, :], added[:, 0:k, :], subbed[:, 0:k, :], ALU.add
                                            ).then_inc(d["value"], 1)
                    need("value")
                    nc.vector.tensor_scalar(clipped[:, 0:k, :], value[:, 0:k, :], 0.0, 15.0, ALU.max, ALU.min
                                            ).then_inc(d["clipped"], 1)
                    need("clipped")
                    nc.vector.tensor_scalar_add(shifted[:, 0:k, :], clipped[:, 0:k, :], ROUNDER
                                                ).then_inc(d["shifted"], 1)
                    need("shifted")
                    nc.vector.tensor_scalar_add(rounded[:, 0:k, :], shifted[:, 0:k, :], -ROUNDER
                                                ).then_inc(d["rounded"], 1)
                    need("rounded")
                    need("res")
                    for j in range(k):
                        nc.vector.tensor_tensor(hot[:, j, :, :], digits[:, :, :],
                                                rounded[:, j, 0:2].unsqueeze(2).to_broadcast([P, 2, 16]),
                                                ALU.is_equal).then_inc(d["hot"], 1)
                    nc.vector.scalar_tensor_tensor(carry[:, 0:k], rounded[:, 0:k, 2], 0.5, active[:, s, 0:k],
                                                   ALU.is_gt, ALU.mult).then_inc(d["carry"], 1)
                    dve.wait_ge(d["hot"], c * C + k)
                    for j in range(k):
                        place = res[:, s, j, 128:160]
                        nc.vector.scalar_tensor_tensor(place, hot[:, j, :, :].rearrange("p a b -> p (a b)"),
                                                       active2[:, s, j:j + 1], place, ALU.mult, ALU.add
                                                       ).then_inc(d["placed"], 1)
                    need("carry")
                    nc.vector.tensor_tensor(res[:, s, 0:k, 160], res[:, s, 0:k, 160], carry[:, 0:k], ALU.add
                                            ).then_inc(d["carried"], 1)

                dve.wait_ge(s_w, 7 * 16)
                nc.vector.memset(feats[:, :, :, 6:7], 1.0).then_inc(s_ones, 1)
                nc.vector.memset(feats[:, :, :, 7:8], 0.0).then_inc(s_ones, 1)
                for c, s, k in chunks(dve):
                    front(c, s, k)
                    if isinstance(c, int) and c == 0:
                        continue
                    tail(c - 1, 1 - s, C)
                tail(CHUNKS, 0, NODE_TILES - CHUNKS * C)


ROUNDER = 1.5 * 2.0 ** 23

SHAPES = {
    "x": (NODES, D), "wt": (D, D), "bias": (1, D), "w_src": (P, D), "w_dst": (P, D), "ident": (P, P),
    "pairs": (P, EDGE_TILES, 2), "dist": (P, EDGE_TILES, HEADS), "before": (P, P),
    "w1": (FEATS, 5, P), "w2": (P, 13, P), "w3": (P, 5, 8), "b2": (P, 5), "b3": (P, 8),
    "countdown": (P, 64), "digits": (P, 2, 16),
}


def program(nc, t):
    with ExitStack() as top:
        keep = {
            "ident": top.enter_context(nc.sbuf_tensor("ident", [P, P], F32)),
            "esrc": top.enter_context(nc.sbuf_tensor("esrc", [P, NODE_TILES * HEADS], F32)),
            "edst": top.enter_context(nc.sbuf_tensor("edst", [P, NODE_TILES * HEADS], F32)),
        }
        banks = [top.enter_context(nc.psum_tensor(f"bank{i}", [P, 512], F32)) for i in range(8)]
        t["h"] = nc.dram_tensor("table_h", (ROWS, ROW), F32).ap()
        t["agg"] = nc.dram_tensor("table_agg", (ROWS, ROW), F32).ap()
        t["med"] = nc.dram_tensor("table_med", (ROWS, 2 * HEADS), F32).ap()
        project(nc, top, banks, t, keep)
        attend_any(nc, top, banks, t, keep)
        finish(nc, top, banks, t, keep)


def layout(x, src, dst, edge_attr_8, L0_gnn_W, L0_gnn_b, L0_gnn_w_att_src, L0_gnn_w_att_dst,
           L0_ffn_Wa, L0_ffn_ba, L0_ffn_Ws, L0_ffn_bs):
    a = {}
    a["x"] = np.zeros((NODES, D), np.float32)
    a["x"][:N] = x
    a["wt"] = L0_gnn_W.T
    a["bias"] = L0_gnn_b[None]
    a["w_src"] = np.broadcast_to(L0_gnn_w_att_src.reshape(1, D), (P, D))
    a["w_dst"] = np.broadcast_to(L0_gnn_w_att_dst.reshape(1, D), (P, D))
    a["ident"] = np.eye(P, dtype=np.float32)
    a["before"] = np.tril(np.ones((P, P), np.float32), -1)
    pairs = np.full((EDGE_TILES * P, 2), NOWHERE, np.int32)
    pairs[:E, 0] = src
    pairs[:E, 1] = dst
    a["pairs"] = pairs.reshape(EDGE_TILES, P, 2).transpose(1, 0, 2)
    dist = np.zeros((EDGE_TILES * P, HEADS), np.float32)
    dist[:E] = edge_attr_8
    a["dist"] = dist.reshape(EDGE_TILES, P, HEADS).transpose(1, 0, 2)

    w1 = np.zeros((FEATS, 5, P), np.float32)
    w2 = np.zeros((P, 13, P), np.float32)
    w3 = np.zeros((P, 5, 8), np.float32)
    b2 = np.zeros((P, 5), np.float32)
    b3 = np.zeros((P, 8), np.float32)
    nets = [(L0_ffn_Wa, L0_ffn_ba), (L0_ffn_Ws, L0_ffn_bs)]
    for g, (net, pos) in enumerate(COMBOS):
        w, b = nets[net]
        last = slice(REM * g, REM * (g + 1))
        rows = [(pos, NIB_A), (2 + pos, NIB_B), (4, OP_ADD_IN), (5, OP_SUB_IN)]
        for row, col in rows:
            w1[row, g] = w[0][:P, col]
            w1[row, 4, last] = w[0][P:, col]
        w1[6, g] = b[0][:P]
        w1[6, 4, last] = b[0][P:]
        w2[:, g] = w[1][:P, :P].T
        w2[last, 4 + g] = w[1][:P, P:].T
        w2[:, 8 + g, last] = w[1][P:, :P].T
        w2[last, 12, last] = w[1][P:, P:].T
        b2[:, g] = b[1][:P]
        b2[last, 4] = b[1][P:]
        outs = [(3 * net + pos, RESULT)] + [(3 * net + 2, CARRY_OUT)] * pos
        for out, row in outs:
            w3[:, g, out] = w[2][row, :P]
            w3[last, 4, out] = w[2][row, P:]
            b3[:, out] = b[2][row]
    a.update(w1=w1, w2=w2, w3=w3, b2=b2, b3=b3)
    a["countdown"] = np.broadcast_to(np.tile(16.0 - np.arange(16), 4).astype(np.float32), (P, 64))
    a["digits"] = np.broadcast_to(np.arange(16).astype(np.float32), (P, 2, 16))
    return a


def kernel(**inputs):
    import concourse.bacc as bacc
    from concourse.bass_utils import run_bass_kernel_spmd

    arrays = {"in_" + k: np.ascontiguousarray(v) for k, v in layout(**{k: np.asarray(v) for k, v in inputs.items()}
                                                                     ).items()}
    nc = bacc.Bacc("TRN2", target_bir_lowering=False, num_devices=1)
    t = {}
    for name, shape in SHAPES.items():
        assert arrays["in_" + name].shape == shape, name
        dt = mybir.dt.from_np(arrays["in_" + name].dtype)
        t[name] = nc.dram_tensor("in_" + name, shape, dt, kind="ExternalInput").ap()
    t["out"] = nc.dram_tensor("out", (N, D), F32, kind="ExternalOutput").ap()
    program(nc, t)
    return run_bass_kernel_spmd(nc, [arrays], core_ids=[0]).results[0]["out"]
```

```python
from contextlib import ExitStack

import concourse.bass as bass
import numpy as np
from concourse import mybir

F32 = mybir.dt.float32
I32 = mybir.dt.int32
ALU = mybir.AluOpType
ACT = mybir.ActivationFunctionType
AX = mybir.AxisListType.X

P = 128
N, D, HEADS, E = 6250, 512, 8, 100000
HD = D // HEADS
SLOPE = 0.2
EPS = 1e-5
NODE_TILES = -(-N // P)
NODES = NODE_TILES * P
ROWS = NODES + P
NOWHERE = NODES
DC = D // P
ROW = D + HEADS
GROUP = 6
GROUPS = -(-E // (P * GROUP))
EDGE_TILES = GROUPS * GROUP
TINY = 1e-30
FAR = 1 << 20
LOWEST = -3e38
SAFE_WIDTH = 64.0
RMAX = bass.bass_isa.ReduceOp.max

GE = 160
REM = GE - P
RESULT, CARRY_OUT = 100, 101
NIB_A, NIB_B, OP_ADD_IN, OP_SUB_IN = 0, 1, 35, 36
X_OP_ADD, X_OP_SUB = 105, 106
FEATS = 8
COMBOS = [(0, 0), (0, 1), (1, 0), (1, 1)]
OUTS = 6
CHUNK = 4
CHUNKS = NODE_TILES // CHUNK


def turns(eng, total):
    yield 0, 0
    yield 1, 1
    with eng.Fori(1, total // 2) as i:
        yield 2 * i, 0
        yield 2 * i + 1, 1
    if total % 2:
        yield total - 1, 0


def reused(turn, slots=2):
    return not (isinstance(turn, int) and turn < slots)


def dma_count(turn, slot, slots=2):
    if isinstance(turn, int):
        return 16 * ((turn - slot) // slots + 1)
    return (turn - slot) * (16 // slots) + 16


def wait_alone(eng, semaphore, value, went_on):
    eng.wait_ge(semaphore, value)
    eng.sem_inc(went_on, 1)


def edge_turns(eng):
    yield 0
    with eng.Fori(1, EDGE_TILES) as n:
        yield n


def project(nc, top, banks, t, keep):
    with ExitStack() as ctx:
        def sb(name, shape, dt=F32):
            return ctx.enter_context(nc.sbuf_tensor(name, shape, dt))

        def sem(name):
            return top.enter_context(nc.semaphore(name))

        wt = sb("wt", [P, DC, D])
        bias_row = sb("bias_row", [1, D])
        ones_row = sb("ones_row", [1, P])
        w_src = sb("w_src", [P, D])
        w_dst = sb("w_dst", [P, D])
        zeros = sb("zeros", [P, ROW])
        xt = sb("xt", [P, 2, D])
        xn = sb("xn", [P, 2, D])
        xnT = sb("xnT", [P, 2, D])
        stats = sb("stats", [P, 2, 6])
        mean_var = sb("mean_var", [P, 2, 2])
        var_eps = sb("var_eps", [P, 2, 1])
        std = sb("std", [P, 2, 1])
        rstd = sb("rstd", [P, 2, 1])
        leak = sb("leak", [P, 2, D])
        hrow = sb("hrow", [P, 2, ROW])
        prod_src = sb("prod_src", [P, D])
        prod_dst = sb("prod_dst", [P, 2, D])
        ps_t, ps_h = banks[0:2], banks[2:4]

        s_const = sem("const_loaded")
        s_set = sem("const_set")
        s_zero = sem("zeros_set")
        s_ztab = sem("zeros_stored")
        s_dve_on = sem("dve_went_on")
        s_x = [sem("x_loaded0"), sem("x_loaded1")]
        s_stats, s_mv, s_ve = sem("stats_ready"), sem("meanvar_ready"), sem("vareps_ready")
        s_std, s_rstd, s_xn = sem("std_ready"), sem("rstd_ready"), sem("xn_ready")
        s_tr, s_xnT = sem("transposed"), sem("xnT_ready")
        s_h, s_leak, s_row = sem("h_ready"), sem("leak_ready"), sem("hrow_ready")
        s_psrc, s_esrc = sem("prod_src_ready"), sem("esrc_ready")
        s_pdst, s_edst = sem("prod_dst_ready"), sem("edst_ready")
        s_out = [sem("hrow_stored0"), sem("hrow_stored1")]

        with nc.Block() as block:
            @block.sync
            def _(sp):
                sp.dma_start(wt[:, :, :], t["wt"].rearrange("(c p) n -> p c n", p=P)).then_inc(s_const, 16)
                sp.dma_start(bias_row[:, :], t["bias"]).then_inc(s_const, 16)
                sp.dma_start(w_src[:, :], t["w_src"]).then_inc(s_const, 16)
                sp.dma_start(w_dst[:, :], t["w_dst"]).then_inc(s_const, 16)
                sp.dma_start(keep["ident"][:, :], t["ident"]).then_inc(s_const, 16)
                for n, s in turns(sp, NODE_TILES):
                    if reused(n):
                        sp.wait_ge(s_xn, n - 1)
                    sp.dma_start(xt[:, s, :], t["x"][bass.ds(n * P, P), :]).then_inc(s_x[s], 16)

            @block.gpsimd
            def _(pool):
                nc.gpsimd.memset(zeros[:, :], 0.0).then_inc(s_zero, 1)
                nc.gpsimd.memset(ones_row[:, :], 1.0).then_inc(s_set, 1)
                pool.wait_ge(s_const, 5 * 16)
                for n, s in turns(pool, NODE_TILES):
                    pool.wait_ge(s_row, n + 1)
                    if reused(n):
                        pool.wait_ge(s_edst, n - 1)
                    nc.gpsimd.tensor_tensor(prod_dst[:, s, :], hrow[:, s, 0:D], w_dst[:, :],
                                            ALU.mult).then_inc(s_pdst, 1)

            def scores(dve, n, s):
                dve.wait_ge(s_leak, n + 1)
                dve.wait_ge(s_h, n + 1)
                if reused(n):
                    dve.wait_ge(s_out[s], dma_count(n - 2, s))
                    dve.wait_ge(s_pdst, n - 1)
                nc.vector.tensor_tensor(hrow[:, s, 0:D], leak[:, s, :], ps_h[s][:, :], ALU.max).then_inc(s_row, 1)
                dve.wait_ge(s_row, n + 1)
                if reused(n, 1):
                    dve.wait_ge(s_esrc, 2 * n)
                nc.vector.tensor_tensor(prod_src[:, :], hrow[:, s, 0:D], w_src[:, :], ALU.mult).then_inc(s_psrc, 1)
                dve.wait_ge(s_psrc, n + 1)
                src_heads = prod_src[:, :].rearrange("p (h d) -> p h d", h=HEADS)
                nc.vector.tensor_reduce(hrow[:, s, D:ROW], src_heads, AX, ALU.add).then_inc(s_esrc, 1)
                nc.vector.tensor_reduce(keep["esrc"][:, bass.ds(n * HEADS, HEADS)], src_heads, AX,
                                        ALU.add).then_inc(s_esrc, 1)
                dve.wait_ge(s_pdst, n + 1)
                dst_heads = prod_dst[:, s, :].rearrange("p (h d) -> p h d", h=HEADS)
                nc.vector.tensor_reduce(keep["edst"][:, bass.ds(n * HEADS, HEADS)], dst_heads, AX,
                                        ALU.add).then_inc(s_edst, 1)

            @block.vector
            def _(dve):
                dve.wait_ge(s_const, 5 * 16)
                for n, s in turns(dve, NODE_TILES):
                    dve.wait_ge(s_x[s], dma_count(n, s))
                    nc.vector.bn_stats(stats[:, s, :], xt[:, s, :]).then_inc(s_stats, 1)
                    wait_alone(dve, s_stats, n + 1, s_dve_on)
                    nc.vector.bn_aggr(mean_var[:, s, :], stats[:, s, :]).then_inc(s_mv, 1)
                    dve.wait_ge(s_mv, n + 1)
                    if reused(n):
                        dve.wait_ge(s_std, n - 1)
                    nc.vector.tensor_scalar_add(var_eps[:, s, :], mean_var[:, s, 1:2], EPS).then_inc(s_ve, 1)
                    dve.wait_ge(s_std, n + 1)
                    nc.vector.reciprocal(rstd[:, s, :], std[:, s, :]).then_inc(s_rstd, 1)
                    dve.wait_ge(s_rstd, n + 1)
                    if reused(n):
                        dve.wait_ge(s_tr, n - 1)
                    nc.vector.tensor_scalar(xn[:, s, :], xt[:, s, :], mean_var[:, s, 0:1], rstd[:, s, :],
                                            ALU.subtract, ALU.mult).then_inc(s_xn, 1)
                    if isinstance(n, int) and n == 0:
                        continue
                    scores(dve, n - 1, 1 - s)
                scores(dve, NODE_TILES - 1, (NODE_TILES - 1) % 2)

            @block.tensor
            def _(pe):
                pe.wait_ge(s_const, 5 * 16)
                pe.wait_ge(s_set, 1)

                def gemm(n, s):
                    pe.wait_ge(s_xnT, n + 1)
                    if reused(n):
                        pe.wait_ge(s_row, n - 1)
                    nc.tensor.matmul(ps_h[s][:, :], ones_row[:, :], bias_row[:, :], start=True, stop=False)
                    for c in range(DC):
                        last = nc.tensor.matmul(ps_h[s][:, :], xnT[:, s, c * P:(c + 1) * P], wt[:, c, :],
                                                start=False, stop=(c == DC - 1))
                    last.then_inc(s_h, 1)

                for n, s in turns(pe, NODE_TILES):
                    pe.wait_ge(s_xn, n + 1)
                    if reused(n):
                        pe.wait_ge(s_xnT, n - 1)
                    for c in range(DC):
                        last = nc.tensor.transpose(ps_t[s][:, c * P:(c + 1) * P], xn[:, s, c * P:(c + 1) * P],
                                                   keep["ident"][:, :])
                    last.then_inc(s_tr, 1)
                    if isinstance(n, int) and n == 0:
                        continue
                    gemm(n - 1, 1 - s)
                gemm(NODE_TILES - 1, (NODE_TILES - 1) % 2)

            @block.scalar
            def _(act):
                def leaky(n, s):
                    act.wait_ge(s_h, n + 1)
                    if reused(n):
                        act.wait_ge(s_row, n - 1)
                    nc.scalar.activation(leak[:, s, :], ps_h[s][:, :], ACT.Copy, scale=SLOPE).then_inc(s_leak, 1)

                def store(n, s):
                    act.wait_ge(s_esrc, 2 * (n + 1))
                    act.dma_start(t["h"][bass.ds(n * P, P), :], hrow[:, s, :]).then_inc(s_out[s], 16)

                act.wait_ge(s_zero, 1)
                act.dma_start(t["h"][NODES:ROWS, :], zeros[:, :]).then_inc(s_ztab, 16)
                act.dma_start(t["agg"][NODES:ROWS, :], zeros[:, :]).then_inc(s_ztab, 16)
                for n, s in turns(act, NODE_TILES):
                    act.dma_start(t["agg"][bass.ds(n * P, P), :], zeros[:, :]).then_inc(s_ztab, 16)
                    act.wait_ge(s_ve, n + 1)
                    if reused(n):
                        act.wait_ge(s_rstd, n - 1)
                    nc.scalar.activation(std[:, s, :], var_eps[:, s, :], ACT.Sqrt).then_inc(s_std, 1)
                    act.wait_ge(s_tr, n + 1)
                    if reused(n):
                        act.wait_ge(s_h, n - 1)
                    nc.scalar.activation(xnT[:, s, :], ps_t[s][:, :], ACT.Copy).then_inc(s_xnT, 1)
                    if isinstance(n, int) and n == 0:
                        continue
                    leaky(n - 1, 1 - s)
                    if isinstance(n, int) and n == 1:
                        continue
                    store(n - 2, s)
                leaky(NODE_TILES - 1, 0)
                store(NODE_TILES - 2, 1)
                store(NODE_TILES - 1, 0)
                act.wait_ge(s_out[0], dma_count(NODE_TILES - 1, 0))
                act.wait_ge(s_out[1], dma_count(NODE_TILES - 2, 1))
                act.wait_ge(s_ztab, 16 * (NODE_TILES + 2))


def attend_any(nc, top, banks, t, keep):
    with ExitStack() as ctx:
        def sb(name, shape, dt=F32):
            return ctx.enter_context(nc.sbuf_tensor(name, shape, dt))

        def sem(name):
            return top.enter_context(nc.semaphore(name))

        before = sb("before", [P, P])
        src_idx = sb("src_idx", [P, 1], I32)
        dst_idx = sb("dst_idx", [P, 1], I32)
        put_idx = sb("put_idx", [P, 1], I32)
        dcol = sb("dcol", [P, 1])
        dst_wide = sb("dst_wide", [P, P])
        e_wide = sb("e_wide", [P, HEADS, P])
        same = sb("same", [P, P])
        penalty = sb("penalty", [P, P])
        masked = sb("masked", [P, HEADS, P])
        earlier = sb("earlier", [P, P])
        n_earlier = sb("n_earlier", [P, 1])
        grow = sb("grow", [P, ROW])
        arow = sb("arow", [P, ROW])
        anew = sb("anew", [P, ROW])
        mrow = sb("mrow", [P, 2 * HEADS])
        mnew = sb("mnew", [P, 2 * HEADS])
        score = sb("score", [P, HEADS])
        e = sb("e", [P, HEADS])
        tile_max = sb("tile_max", [P, HEADS])
        diffs = sb("diffs", [P, 2 * HEADS])
        exps = sb("exps", [P, 2 * HEADS])
        coef = sb("coef", [P, HEADS])
        msg = sb("msg", [P, D])
        put_f = sb("put_f", [P, 1])
        src = keep["src"][:, :, :].rearrange("p g j -> p (g j)")
        dst = keep["dst"][:, :, :].rearrange("p g j -> p (g j)")
        dist = keep["dist"]
        wide_t = banks[0]
        e_t = [banks[1], banks[2]]
        sums, weights = banks[3], banks[4]

        s_load = sem("edges_loaded")
        s_src, s_dst, s_dc, s_put = sem("src_idx_set"), sem("dst_idx_set"), sem("dcol_set"), sem("put_idx_set")
        s_pool_on = sem("pool_went_on")
        s_g, s_a, s_m = sem("g_gathered"), sem("a_gathered"), sem("m_gathered")
        s_ap, s_mp = sem("a_put"), sem("m_put")
        names = ("dst_wide dstT same penalty earlier n_earlier put_f score e e_wide eT masked tile_max "
                 "mnew diffs exps coef msg sums anew").split()
        done = {k: sem("any_" + k) for k in names}
        s_scaled = sem("any_scaled")

        with nc.Block() as block:
            @block.sync
            def _(sp):
                sp.dma_start(before[:, :], t["before"]).then_inc(s_load, 16)

            @block.gpsimd
            def _(pool):
                def gather(out, table, idx, semaphore):
                    pool.indirect_dma_start(out=out[:, :], out_offset=None, in_=table[:, :],
                                            in_offset=bass.IndirectOffsetOnAxis(ap=idx[:, :], axis=0)
                                            ).then_inc(semaphore, 16)

                def scatter(table, row, semaphore):
                    pool.indirect_dma_start(out=table[:, :],
                                            out_offset=bass.IndirectOffsetOnAxis(ap=put_idx[:, :], axis=0),
                                            in_=row[:, :], in_offset=None, bounds_check=ROWS - 1,
                                            oob_is_err=False).then_inc(semaphore, 16)

                for n in edge_turns(pool):
                    wait_alone(pool, s_src, n + 1, s_pool_on)
                    gather(grow, t["h"], src_idx, s_g)
                    wait_alone(pool, s_dst, n + 1, s_pool_on)
                    gather(arow, t["agg"], dst_idx, s_a)
                    gather(mrow, t["maxima"], dst_idx, s_m)
                    pool.wait_ge(s_put, n + 1)
                    wait_alone(pool, done["anew"], 2 * (n + 1), s_pool_on)
                    scatter(t["agg"], anew, s_ap)
                    scatter(t["maxima"], mnew, s_mp)
                    pool.wait_ge(s_ap, 16 * (n + 1))
                    pool.wait_ge(s_mp, 16 * (n + 1))

            @block.vector
            def _(dve):
                dve.wait_ge(s_load, 16)

                def heads(ap):
                    return ap.rearrange("p (h d) -> p h d", h=HEADS)

                for n in edge_turns(dve):
                    def step(name, ins):
                        ins.then_inc(done[name], 1)
                        dve.wait_ge(done[name], n + 1)

                    if reused(n, 1):
                        dve.wait_ge(s_mp, 16 * n)
                        dve.wait_ge(s_ap, 16 * n)
                    nc.vector.tensor_copy(src_idx[:, :], src[:, bass.ds(n, 1)]).then_inc(s_src, 1)
                    nc.vector.tensor_copy(dst_idx[:, :], dst[:, bass.ds(n, 1)]).then_inc(s_dst, 1)
                    nc.vector.tensor_copy(dcol[:, :], dst[:, bass.ds(n, 1)]).then_inc(s_dc, 1)
                    dve.wait_ge(s_dc, n + 1)
                    step("dst_wide", nc.vector.tensor_copy(dst_wide[:, :], dcol[:, 0:1].to_broadcast([P, P])))
                    dve.wait_ge(done["dstT"], n + 1)
                    step("same", nc.vector.tensor_scalar(same[:, :], wide_t[:, 0:P], dcol[:, 0:1], None,
                                                         ALU.is_equal))
                    nc.vector.tensor_scalar(penalty[:, :], same[:, :], -1.0, -LOWEST, ALU.add,
                                            ALU.mult).then_inc(done["penalty"], 1)
                    step("earlier", nc.vector.tensor_tensor(earlier[:, :], same[:, :], before[:, :], ALU.mult))
                    step("n_earlier", nc.vector.tensor_reduce(n_earlier[:, :], earlier[:, :], AX, ALU.max))
                    step("put_f", nc.vector.scalar_tensor_tensor(put_f[:, :], n_earlier[:, :], float(FAR),
                                                                 dcol[:, :], ALU.mult, ALU.add))
                    nc.vector.tensor_copy(put_idx[:, :], put_f[:, :]).then_inc(s_put, 1)

                    dve.wait_ge(s_g, 16 * (n + 1))
                    dve.wait_ge(s_m, 16 * (n + 1))
                    step("score", nc.vector.tensor_tensor(score[:, :], grow[:, D:ROW], mrow[:, HEADS:2 * HEADS],
                                                          ALU.add))
                    step("e", nc.vector.scalar_tensor_tensor(e[:, :], score[:, :], SLOPE, score[:, :], ALU.mult,
                                                             ALU.max))
                    step("e_wide", nc.vector.tensor_copy(e_wide[:, :, :], e[:, :].unsqueeze(2)
                                                         .to_broadcast([P, HEADS, P])))
                    dve.wait_ge(done["eT"], n + 1)
                    dve.wait_ge(done["penalty"], n + 1)
                    half = HEADS // 2
                    for b in range(2):
                        last = nc.vector.tensor_tensor(
                            masked[:, b * half:(b + 1) * half, :],
                            e_t[b][:, :].rearrange("p (h c) -> p h c", h=half),
                            penalty[:, :].unsqueeze(1).to_broadcast([P, half, P]), ALU.add)
                        if b == 0:
                            last.then_inc(done["masked"], 1)
                    last.then_inc(done["masked"], 1)
                    dve.wait_ge(done["masked"], 2 * (n + 1))
                    step("tile_max", nc.vector.tensor_reduce(tile_max[:, :], masked[:, :, :], AX, ALU.max))
                    nc.vector.tensor_copy(mnew[:, HEADS:2 * HEADS], mrow[:, HEADS:2 * HEADS]
                                          ).then_inc(done["mnew"], 1)
                    nc.vector.tensor_tensor(mnew[:, 0:HEADS], mrow[:, 0:HEADS], tile_max[:, :], ALU.max
                                            ).then_inc(done["mnew"], 1)
                    dve.wait_ge(done["mnew"], 2 * (n + 1))
                    nc.vector.tensor_tensor(diffs[:, 0:HEADS], mrow[:, 0:HEADS], mnew[:, 0:HEADS],
                                            ALU.subtract).then_inc(done["diffs"], 1)
                    nc.vector.tensor_tensor(diffs[:, HEADS:2 * HEADS], e[:, :], mnew[:, 0:HEADS],
                                            ALU.subtract).then_inc(done["diffs"], 1)
                    dve.wait_ge(done["exps"], n + 1)
                    step("coef", nc.vector.tensor_tensor(
                        coef[:, :], exps[:, HEADS:2 * HEADS],
                        dist[:, bass.ds(n, 1), :].rearrange("p o h -> p (o h)"), ALU.mult))
                    nc.vector.tensor_tensor(heads(msg[:, :]), heads(grow[:, 0:D]),
                                            coef[:, :].unsqueeze(2).to_broadcast([P, HEADS, HD]), ALU.mult
                                            ).then_inc(done["msg"], 1)
                    dve.wait_ge(s_a, 16 * (n + 1))
                    nc.vector.tensor_tensor(heads(arow[:, 0:D]), heads(arow[:, 0:D]),
                                            exps[:, 0:HEADS].unsqueeze(2).to_broadcast([P, HEADS, HD]),
                                            ALU.mult).then_inc(s_scaled, 1)
                    nc.vector.tensor_tensor(arow[:, D:ROW], arow[:, D:ROW], exps[:, 0:HEADS],
                                            ALU.mult).then_inc(s_scaled, 1)
                    dve.wait_ge(s_scaled, 2 * (n + 1))
                    dve.wait_ge(done["sums"], n + 1)
                    nc.vector.tensor_tensor(anew[:, 0:D], arow[:, 0:D], sums[:, :], ALU.add
                                            ).then_inc(done["anew"], 1)
                    nc.vector.tensor_tensor(anew[:, D:ROW], arow[:, D:ROW], weights[:, 0:HEADS], ALU.add
                                            ).then_inc(done["anew"], 1)

            @block.scalar
            def _(act):
                for n in edge_turns(act):
                    act.wait_ge(done["diffs"], 2 * (n + 1))
                    nc.scalar.activation(exps[:, :], diffs[:, :], ACT.Exp).then_inc(done["exps"], 1)

            @block.tensor
            def _(pe):
                for n in edge_turns(pe):
                    pe.wait_ge(done["dst_wide"], n + 1)
                    nc.tensor.transpose(wide_t[:, 0:P], dst_wide[:, :], keep["ident"][:, :]
                                        ).then_inc(done["dstT"], 1)
                    pe.wait_ge(done["e_wide"], n + 1)
                    for h in range(HEADS):
                        k = h % (HEADS // 2)
                        last = nc.tensor.transpose(e_t[h // (HEADS // 2)][:, k * P:(k + 1) * P], e_wide[:, h, :],
                                                   keep["ident"][:, :])
                    last.then_inc(done["eT"], 1)
                    pe.wait_ge(done["msg"], n + 1)
                    nc.tensor.matmul(sums[:, :], same[:, :], msg[:, :], start=True, stop=True)
                    nc.tensor.matmul(weights[:, 0:HEADS], same[:, :], exps[:, HEADS:2 * HEADS], start=True,
                                     stop=True).then_inc(done["sums"], 1)


def finish(nc, top, banks, t, keep):
    with ExitStack() as ctx:
        def sb(name, shape, dt=F32):
            return ctx.enter_context(nc.sbuf_tensor(name, shape, dt))

        def sem(name):
            return top.enter_context(nc.semaphore(name))

        C = CHUNK
        w1 = sb("w1", [FEATS, 5, P])
        w2 = sb("w2", [P, 13, P])
        w3 = sb("w3", [P, 5, 8])
        b2 = sb("b2", [P, 5])
        b3 = sb("b3", [P, 8])
        countdown = sb("countdown", [P, 64])
        digits = sb("digits", [P, 16])
        x = sb("fx", [P, 2, C, D])
        agg = sb("fagg", [P, 2, C, ROW])
        y = sb("fy", [P, C, D])
        res = sb("fres", [P, 2, C, D])
        wsum = sb("fwsum", [P, C, HEADS])
        rsum = sb("frsum", [P, C, HEADS])
        stats = sb("fstats", [P, C, 6])
        mv = sb("fmv", [P, C, 2])
        ve = sb("fve", [P, C])
        std = sb("fstd", [P, C])
        rstd = sb("frstd", [P, C])
        hits = sb("fhits", [P, C, 64])
        best = sb("fbest", [P, C, 4])
        first = sb("ffirst", [P, C, 4])
        feats = sb("ffeats", [P, C, FEATS])
        flags = sb("fflags", [P, C, 3])
        marked = sb("fmarked", [P, C, 4])
        featsT = sb("ffeatsT", [FEATS, C * P])
        h1 = sb("fh1", [P, 5, C * P])
        h2 = sb("fh2", [P, 5, C * P])
        v3 = sb("fv3", [P, C, 8])
        picked = sb("fpicked", [P, C, 3])
        other = sb("fother", [P, C, 3])
        clipped = sb("fclipped", [P, C, 3])
        shifted = sb("fshifted", [P, C, 3])
        rounded = sb("frounded", [P, C, 3])
        hot = sb("fhot", [P, C, 2, 16])
        act2 = sb("fact2", [P, C])
        carry = sb("fcarry", [P, C])
        ftp = banks[0]
        rot = banks[1:7]
        yp = banks[7]

        s_w = sem("mlp_weights_loaded")
        s_in = [sem("fin_loaded0"), sem("fin_loaded1")]
        s_out = [sem("out_stored0"), sem("out_stored1")]
        names = ("wsum rsum scaled x1 stats mv ve std rstd y res hits best first feats flags marked active "
                 "ftp featsT mm h1 h2 y3 v3 other picked clipped shifted rounded act2 hot hot2 carry final").split()
        d = {k: sem("fin_" + k) for k in names}
        LAST_ROWS = N - CHUNKS * C * P

        def chunks(eng):
            yield 0, 0, C
            yield 1, 1, C
            with eng.Fori(1, CHUNKS // 2) as i:
                yield 2 * i, 0, C
                yield 2 * i + 1, 1, C
            yield CHUNKS, 0, NODE_TILES - CHUNKS * C

        def vec_relu(k):
            return k % 2 == 1

        with nc.Block() as block:
            @block.sync
            def _(sp):
                for name, tile in (("w1", w1), ("w2", w2), ("w3", w3), ("b2", b2), ("b3", b3),
                                   ("countdown", countdown), ("digits", digits)):
                    dst = tile[:, :, :] if len(tile.shape) == 3 else tile[:, :]
                    sp.dma_start(dst, t[name]).then_inc(s_w, 16)
                for c, s, k in chunks(sp):
                    if reused(c):
                        sp.wait_ge(d["x1"], c - 1)
                    rows = bass.ds(c * (C * P), k * P)
                    sp.dma_start(x[:, s, 0:k, :], t["x"][rows, :].rearrange("(k p) n -> p k n", p=P)
                                 ).then_inc(s_in[s], 16)
                    sp.dma_start(agg[:, s, 0:k, :], t["agg"][rows, :].rearrange("(k p) n -> p k n", p=P)
                                 ).then_inc(s_in[s], 16)

            @block.gpsimd
            def _(pool):
                for c, s, k in chunks(pool):
                    pool.wait_ge(d["y"], c + 1)
                    if reused(c):
                        pool.wait_ge(s_out[s], dma_count(c - 2, s))
                    nc.gpsimd.tensor_tensor(res[:, s, 0:k, :], x[:, s, 0:k, :], y[:, 0:k, :], ALU.add
                                            ).then_inc(d["res"], 1)

            @block.scalar
            def _(act):
                act.wait_ge(s_w, 7 * 16)
                for c, s, k in chunks(act):
                    w = k * P
                    act.wait_ge(d["ve"], c + 1)
                    nc.scalar.activation(std[:, 0:k], ve[:, 0:k], ACT.Sqrt).then_inc(d["std"], 1)
                    act.wait_ge(d["ftp"], c + 1)
                    if reused(c, 1):
                        act.wait_ge(d["mm"], 10 * c)
                    nc.scalar.activation(featsT[:, 0:w], ftp[0:FEATS, 0:w], ACT.Copy).then_inc(d["featsT"], 1)
                    for g in (0, 2, 4):
                        act.wait_ge(d["mm"], 10 * c + g + 1)
                        nc.scalar.activation(h1[:, g, 0:w], rot[g % 6][:, 0:w], ACT.Relu).then_inc(d["h1"], 1)
                    for g in (0, 2, 4):
                        act.wait_ge(d["mm"], 10 * c + 5 + g + 1)
                        nc.scalar.activation(h2[:, g, 0:w], rot[(5 + g) % 6][:, 0:w], ACT.Relu,
                                             bias=b2[:, g:g + 1]).then_inc(d["h2"], 1)
                    act.wait_ge(d["final"], c + 1)
                    act.wait_ge(d["carry"], 2 * (c + 1))
                    if k == C:
                        act.dma_start(t["out"][bass.ds(c * (C * P), w), :].rearrange("(k p) n -> p k n", p=P),
                                      res[:, s, :, :]).then_inc(s_out[s], 16)
                    else:
                        act.dma_start(t["out"][N - LAST_ROWS:N, :], res[0:LAST_ROWS, s, 0, :]
                                      ).then_inc(s_out[s], 16)
                act.wait_ge(s_out[0], dma_count(CHUNKS, 0))
                act.wait_ge(s_out[1], dma_count(CHUNKS - 1, 1))

            @block.tensor
            def _(pe):
                pe.wait_ge(s_w, 7 * 16)
                for c, s, k in chunks(pe):
                    w = k * P
                    pe.wait_ge(d["feats"], 3 * (c + 1))
                    if reused(c, 1):
                        pe.wait_ge(d["featsT"], c)
                    for j in range(k):
                        last = nc.tensor.transpose(ftp[0:FEATS, j * P:(j + 1) * P], feats[:, j, :],
                                                   keep["ident"][:, :])
                    last.then_inc(d["ftp"], 1)
                    pe.wait_ge(d["featsT"], c + 1)
                    if reused(c, 1):
                        pe.wait_ge(d["h2"], 5 * c)
                    for g in range(5):
                        nc.tensor.matmul(rot[g][:, 0:w], w1[:, g, :], featsT[:, 0:w], start=True,
                                         stop=True).then_inc(d["mm"], 1)
                    pe.wait_ge(d["h1"], 5 * (c + 1))
                    for g in range(4):
                        bank = rot[(5 + g) % 6]
                        nc.tensor.matmul(bank[:, 0:w], w2[:, g, :], h1[:, g, 0:w], start=True, stop=False)
                        nc.tensor.matmul(bank[:, 0:w], w2[:, 4 + g, :], h1[:, 4, 0:w], start=False,
                                         stop=True).then_inc(d["mm"], 1)
                    bank = rot[9 % 6]
                    for g in range(5):
                        last = nc.tensor.matmul(bank[:, 0:w], w2[:, 8 + g, :], h1[:, g, 0:w], start=(g == 0),
                                                stop=(g == 4))
                    last.then_inc(d["mm"], 1)
                    pe.wait_ge(d["h2"], 5 * (c + 1))
                    if reused(c, 1):
                        pe.wait_ge(d["v3"], c)
                    for j in range(k):
                        for g in range(5):
                            last = nc.tensor.matmul(yp[:, 8 * j:8 * j + 8], h2[:, g, j * P:(j + 1) * P],
                                                    w3[:, g, :], start=(g == 0), stop=(g == 4))
                    last.then_inc(d["y3"], 1)

            @block.vector
            def _(dve):
                dve.wait_ge(s_w, 7 * 16)
                nc.vector.memset(feats[:, :, 6:7], 1.0).then_inc(d["mv"], 1)
                nc.vector.memset(feats[:, :, 7:8], 0.0).then_inc(d["mv"], 1)
                for c, s, k in chunks(dve):
                    def done(name, ins, per=1):
                        ins.then_inc(d[name], 1)

                    def need(name, per=1):
                        dve.wait_ge(d[name], per * (c + 1))

                    w = k * P
                    if isinstance(c, int):
                        dve.wait_ge(s_in[s], 2 * dma_count(c, s))
                    else:
                        dve.wait_ge(s_in[s], (c - s) * 16 + 32)
                    xk, ak = x[:, s, 0:k, :], agg[:, s, 0:k, :]
                    done("wsum", nc.vector.tensor_scalar_max(wsum[:, 0:k, :], ak[:, :, D:ROW], TINY))
                    need("wsum")
                    done("rsum", nc.vector.reciprocal(rsum[:, 0:k, :], wsum[:, 0:k, :]))
                    need("rsum")
                    for j in range(k):
                        heads = agg[:, s, j, 0:D].rearrange("p (h d) -> p h d", h=HEADS)
                        last = nc.vector.tensor_tensor(heads, heads, rsum[:, j, :].unsqueeze(2)
                                                       .to_broadcast([P, HEADS, HD]), ALU.mult)
                        last.then_inc(d["scaled"], 1)
                    dve.wait_ge(d["scaled"], c * C + k)
                    done("x1", nc.vector.tensor_tensor(xk, xk, ak[:, :, 0:D], ALU.add))
                    need("x1")
                    for j in range(k):
                        done("stats", nc.vector.bn_stats(stats[:, j, :], x[:, s, j, :]))
                    dve.wait_ge(d["stats"], c * C + k)
                    for j in range(k):
                        done("mv", nc.vector.bn_aggr(mv[:, j, :], stats[:, j, :]))
                    dve.wait_ge(d["mv"], c * C + k + 2)
                    done("ve", nc.vector.tensor_scalar_add(ve[:, 0:k], mv[:, 0:k, 1], EPS))
                    need("std")
                    done("rstd", nc.vector.reciprocal(rstd[:, 0:k], std[:, 0:k]))
                    need("rstd")
                    if reused(c, 1):
                        dve.wait_ge(d["res"], c)
                    for j in range(k):
                        last = nc.vector.tensor_scalar(y[:, j, :], x[:, s, j, :], mv[:, j, 0:1],
                                                       rstd[:, j:j + 1], ALU.subtract, ALU.mult)
                        last.then_inc(d["flags"], 1)
                    dve.wait_ge(d["flags"], c * C + k)
                    nc.vector.tensor_copy(feats[:, 0:k, 4:6], y[:, 0:k, X_OP_ADD:X_OP_SUB + 1]
                                          ).then_inc(d["feats"], 1)
                    for j in range(k):
                        nc.vector.scalar_tensor_tensor(hits[:, j, :], y[:, j, 16:80], 0.5, countdown[:, :],
                                                       ALU.is_gt, ALU.mult).then_inc(d["hits"], 1)
                    dve.wait_ge(d["hits"], c * C + k)
                    done("best", nc.vector.tensor_reduce(
                        best[:, 0:k, :], hits[:, 0:k, :].rearrange("p k (f j) -> p k f j", j=16), AX, ALU.max))
                    need("best")
                    done("first", nc.vector.tensor_scalar(first[:, 0:k, :], best[:, 0:k, :], -1.0, 16.0,
                                                          ALU.mult, ALU.add))
                    need("first")
                    nc.vector.scalar_tensor_tensor(feats[:, 0:k, 0:4], best[:, 0:k, :], 0.0, first[:, 0:k, :],
                                                   ALU.is_gt, ALU.mult).then_inc(d["feats"], 1)
                    fl = hot[:, 0:k, 0, 0:3]
                    nc.vector.tensor_scalar(flags[:, 0:k, :], y[:, 0:k, 0:3], 0.5, None, ALU.is_gt
                                            ).then_inc(d["feats"], 1)
                    need("feats", 3)
                    done("marked", nc.vector.tensor_tensor(marked[:, 0:k, 1], flags[:, 0:k, 0], flags[:, 0:k, 1],
                                                           ALU.mult))
                    done("marked", nc.vector.tensor_tensor(marked[:, 0:k, 0], flags[:, 0:k, 0], flags[:, 0:k, 2],
                                                           ALU.mult))
                    need("marked", 2)
                    done("active", nc.vector.tensor_tensor(marked[:, 0:k, 3], marked[:, 0:k, 0],
                                                           flags[:, 0:k, 1], ALU.mult))
                    need("active", 1)
                    done("wide_sub", nc.vector.tensor_tensor(marked[:, 0:k, 2], marked[:, 0:k, 0],
                                                             marked[:, 0:k, 3], ALU.subtract))
                    need("wide_sub")
                    done("act2", nc.vector.tensor_tensor(act2[:, 0:k], marked[:, 0:k, 1], marked[:, 0:k, 2],
                                                         ALU.add))

                    for g in (1, 3):
                        dve.wait_ge(d["mm"], 10 * c + g + 1)
                        nc.vector.tensor_scalar_max(h1[:, g, 0:w], rot[g][:, 0:w], 0.0).then_inc(d["h1"], 1)
                    for g in (1, 3):
                        dve.wait_ge(d["mm"], 10 * c + 5 + g + 1)
                        nc.vector.tensor_scalar(h2[:, g, 0:w], rot[(5 + g) % 6][:, 0:w], b2[:, g:g + 1], 0.0,
                                                ALU.add, ALU.max).then_inc(d["h2"], 1)
                    need("y3")
                    done("v3", nc.vector.tensor_tensor(
                        v3[:, 0:k, :], yp[:, 0:8 * k].rearrange("p (k o) -> p k o", o=8),
                        b3[:, :].unsqueeze(1).to_broadcast([P, k, 8]), ALU.add))
                    need("v3")
                    need("act2")
                    done("picked", nc.vector.tensor_tensor(
                        picked[:, 0:k, :], v3[:, 0:k, 0:3],
                        marked[:, 0:k, 1:2].to_broadcast([P, k, 3]), ALU.mult))
                    done("other", nc.vector.tensor_tensor(
                        other[:, 0:k, :], v3[:, 0:k, 3:6],
                        marked[:, 0:k, 2:3].to_broadcast([P, k, 3]), ALU.mult))
                    need("picked")
                    need("other")
                    done("hot2", nc.vector.tensor_tensor(picked[:, 0:k, :], picked[:, 0:k, :], other[:, 0:k, :],
                                                         ALU.add))
                    need("hot2")
                    done("clipped", nc.vector.tensor_scalar(clipped[:, 0:k, :], picked[:, 0:k, :], 0.0, 15.0,
                                                            ALU.max, ALU.min))
                    need("clipped")
                    done("shifted", nc.vector.tensor_scalar_add(shifted[:, 0:k, :], clipped[:, 0:k, :],
                                                                12582912.0))
                    need("shifted")
                    done("rounded", nc.vector.tensor_scalar_add(rounded[:, 0:k, :], shifted[:, 0:k, :],
                                                                -12582912.0))
                    need("rounded")
                    need("res")
                    for j in range(k):
                        nc.vector.tensor_tensor(hot[:, j, :, :], digits[:, :].unsqueeze(1).to_broadcast([P, 2, 16]),
                                                rounded[:, j, 0:2].unsqueeze(2).to_broadcast([P, 2, 16]),
                                                ALU.is_equal).then_inc(d["hot"], 1)
                    dve.wait_ge(d["hot"], c * C + k)
                    done("twice", nc.vector.tensor_scalar_mul(ve2[:, 0:k], act2[:, 0:k], 2.0))
                    need("twice")
                    for j in range(k):
                        out32 = res[:, s, j, 128:160]
                        nc.vector.scalar_tensor_tensor(out32, hot[:, j, :, :].rearrange("p a b -> p (a b)"),
                                                       ve2[:, j:j + 1], out32, ALU.mult, ALU.add
                                                       ).then_inc(d["hot3"], 1)
                    done("carry", nc.vector.scalar_tensor_tensor(carry[:, 0:k], rounded[:, 0:k, 2], 0.5,
                                                                 act2[:, 0:k], ALU.is_gt, ALU.mult))
                    need("carry_only") if False else dve.wait_ge(d["carry"], 2 * c + 1)
                    done("carry", nc.vector.tensor_tensor(res[:, s, 0:k, 160], res[:, s, 0:k, 160],
                                                          carry[:, 0:k], ALU.add))
                    dve.wait_ge(d["hot3"], c * C + k)
                    nc.vector.tensor_copy(flags[:, 0:k, 0], flags[:, 0:k, 0]).then_inc(d["final"], 1)


def prepare(nc, top, banks, t, keep):
    with ExitStack() as ctx:
        def sb(name, shape, dt=F32):
            return ctx.enter_context(nc.sbuf_tensor(name, shape, dt))

        def sem(name):
            return top.enter_context(nc.semaphore(name))

        group_dst = [P, GROUPS, GROUP]
        row_no = sb("row_no", [P, 1])
        base_row = sb("base_row", [1, GROUPS])
        spread = sb("spread", [P, 2 * GROUPS + 2 * HEADS])
        reach = sb("reach", [P, 2 * GROUPS + 2 * HEADS])
        least = sb("least", [P, GROUPS + HEADS])
        row_in_window = sb("row_in_window", [P, GROUPS])
        beyond = sb("beyond", [P, GROUPS])
        put_f = sb("put_rows", [P, GROUPS])
        width = sb("score_width", [P, HEADS])
        excess = sb("excess", [P, 3])
        worst = sb("worst", [P, 1])
        far_flag = sb("far_flag", [P, 1])
        raised = sb("raised", [P, NODE_TILES, HEADS])
        shifts = sb("shifts", [P, NODE_TILES + 1, 2 * HEADS])
        maxima = sb("maxima", [P, NODE_TILES + 1, 2 * HEADS])

        s_load, s_all, s_tab = sem("prep_loaded"), sem("prep_reached"), sem("prep_tables_stored")
        s_bases = sem("bases_spread")
        names = ("base dstf rel rel_max rel_min esrc_max esrc_min negated row_in beyond put put_int base_int "
                 "width excess worst far flag raised shift ed_copies zero_rows").split()
        d = {k: sem("prep_" + k) for k in names}
        esrc = keep["esrc"][:, :].rearrange("p (n h) -> p h n", h=HEADS)
        edst = keep["edst"][:, :].rearrange("p (n h) -> p n h", h=HEADS)
        rel = keep["rel"][:, :].rearrange("p (g j) -> p g j", j=GROUP)

        with nc.Block() as block:
            @block.sync
            def _(sp):
                sp.dma_start(keep["src"][:, :, :], t["src"]).then_inc(s_load, 16)
                sp.dma_start(keep["dst"][:, :, :], t["dst"]).then_inc(s_load, 16)
                sp.dma_start(keep["dist"][:, :, :], t["dist"]).then_inc(s_load, 16)
                sp.dma_start(row_no[:, :], t["row_no"]).then_inc(s_load, 16)
                sp.wait_ge(d["ed_copies"], 2)
                sp.wait_ge(d["zero_rows"], 3)
                sp.dma_start(t["maxima"].rearrange("(n p) c -> p n c", p=P), maxima[:, :, :]).then_inc(s_tab, 16)
                sp.wait_ge(d["shift"], 1)
                sp.dma_start(t["shifts"].rearrange("(n p) c -> p n c", p=P), shifts[:, :, :]).then_inc(s_tab, 16)
                sp.wait_ge(s_tab, 32)

            @block.gpsimd
            def _(pool):
                pool.wait_ge(d["base"], 1)
                nc.gpsimd.partition_broadcast(keep["bases"][:, :], base_row[:, :]).then_inc(s_bases, 1)
                pool.wait_ge(d["rel_max"], 1)
                pool.wait_ge(d["esrc_max"], 1)
                pool.wait_ge(d["negated"], 2)
                nc.gpsimd.partition_all_reduce(reach[:, :], spread[:, :], P, RMAX).then_inc(s_all, 1)

            @block.vector
            def _(dve):
                G2 = 2 * GROUPS

                def step(name, ins):
                    ins.then_inc(d[name], 1)
                    dve.wait_ge(d[name], 1)

                dve.wait_ge(s_load, 4 * 16)
                nc.vector.tensor_copy(base_row[:, :], keep["dst"][0:1, :, 0]).then_inc(d["base"], 1)
                nc.vector.tensor_copy(rel, keep["dst"][:, :, :]).then_inc(d["dstf"], 1)
                nc.vector.memset(maxima[:, :, 0:HEADS], LOWEST).then_inc(d["zero_rows"], 1)
                nc.vector.memset(maxima[:, NODE_TILES, HEADS:], 0.0).then_inc(d["zero_rows"], 1)
                nc.vector.memset(shifts[:, NODE_TILES, :], 0.0).then_inc(d["zero_rows"], 1)
                nc.vector.tensor_copy(maxima[:, 0:NODE_TILES, HEADS:], edst).then_inc(d["ed_copies"], 1)
                nc.vector.tensor_copy(shifts[:, 0:NODE_TILES, 0:HEADS], edst).then_inc(d["ed_copies"], 1)
                nc.vector.tensor_reduce(spread[:, G2:G2 + HEADS], esrc, AX, ALU.max).then_inc(d["esrc_max"], 1)
                step("esrc_min", nc.vector.tensor_reduce(least[:, GROUPS:], esrc, AX, ALU.min))
                nc.vector.tensor_scalar_mul(spread[:, G2 + HEADS:], least[:, GROUPS:], -1.0
                                            ).then_inc(d["negated"], 1)
                dve.wait_ge(s_bases, 1)
                dve.wait_ge(d["dstf"], 1)
                step("rel", nc.vector.tensor_tensor(rel, rel, keep["bases"][:, :].unsqueeze(2)
                                                    .to_broadcast(group_dst), ALU.subtract))
                nc.vector.tensor_reduce(spread[:, 0:GROUPS], rel, AX, ALU.max).then_inc(d["rel_max"], 1)
                step("rel_min", nc.vector.tensor_reduce(least[:, 0:GROUPS], rel, AX, ALU.min))
                nc.vector.tensor_scalar_mul(spread[:, GROUPS:G2], least[:, 0:GROUPS], -1.0
                                            ).then_inc(d["negated"], 1)
                nc.vector.tensor_copy(keep["bases_int"][:, :], base_row[:, :]).then_inc(d["base_int"], 1)
                step("row_in", nc.vector.tensor_scalar(row_in_window[:, :], keep["bases"][:, :], row_no[:, 0:1],
                                                       None, ALU.add))
                dve.wait_ge(s_all, 1)
                step("beyond", nc.vector.tensor_scalar(beyond[:, :], reach[:, 0:GROUPS], row_no[:, 0:1],
                                                       float(FAR), ALU.is_lt, ALU.mult))
                step("put", nc.vector.tensor_tensor(put_f[:, :], row_in_window[:, :], beyond[:, :], ALU.add))
                nc.vector.tensor_copy(keep["put"][:, :], put_f[:, :]).then_inc(d["put_int"], 1)
                step("raised", nc.vector.tensor_tensor(
                    raised[:, :, :], edst, reach[:, G2:G2 + HEADS].unsqueeze(1)
                    .to_broadcast([P, NODE_TILES, HEADS]), ALU.add))
                nc.vector.scalar_tensor_tensor(shifts[:, 0:NODE_TILES, HEADS:], raised[:, :, :], SLOPE,
                                               raised[:, :, :], ALU.mult, ALU.max).then_inc(d["shift"], 1)
                step("width", nc.vector.tensor_tensor(width[:, :], reach[:, G2:G2 + HEADS],
                                                      reach[:, G2 + HEADS:], ALU.add))
                nc.vector.tensor_reduce(excess[:, 0:1], reach[:, 0:GROUPS], AX, ALU.max).then_inc(d["excess"], 1)
                nc.vector.tensor_reduce(excess[:, 1:2], reach[:, GROUPS:G2], AX, ALU.max).then_inc(d["excess"], 1)
                nc.vector.tensor_reduce(excess[:, 2:3], width[:, :], AX, ALU.max).then_inc(d["excess"], 1)
                dve.wait_ge(d["excess"], 3)
                nc.vector.tensor_scalar(keep["excess"][:, 0:1], excess[:, 0:1], float(P - 1), None, ALU.is_gt
                                        ).then_inc(d["far"], 1)
                nc.vector.tensor_scalar(keep["excess"][:, 1:2], excess[:, 1:2], 0.0, None, ALU.is_gt
                                        ).then_inc(d["far"], 1)
                nc.vector.tensor_scalar(keep["excess"][:, 2:3], excess[:, 2:3], SAFE_WIDTH, None, ALU.is_gt
                                        ).then_inc(d["far"], 1)
                dve.wait_ge(d["far"], 3)
                step("flag", nc.vector.tensor_reduce(keep["general"][:, :], keep["excess"][:, :], AX, ALU.max))


def attend_windows(nc, top, banks, t, keep):
    with ExitStack() as ctx:
        def sb(name, shape, dt=F32):
            return ctx.enter_context(nc.sbuf_tensor(name, shape, dt))

        def sem(name):
            return top.enter_context(nc.semaphore(name))

        S3 = 3
        node_no = sb("node_no", [P, P])
        src_idx = sb("w_src_idx", [P, S3, GROUP], I32)
        put_idx = sb("w_put_idx", [P, S3, 1], I32)
        gathered = sb("gathered", [P, S3, GROUP, ROW])
        member = sb("member", [P, S3, GROUP, P])
        memberT = sb("memberT", [P, S3, GROUP, P])
        window = sb("window", [P, S3, 2 * HEADS])
        score = sb("w_score", [P, GROUP, HEADS])
        leaky = sb("w_leaky", [P, GROUP, HEADS])
        diff = sb("w_diff", [P, S3, GROUP, HEADS])
        ex = sb("w_ex", [P, S3, GROUP, HEADS])
        coef = sb("w_coef", [P, GROUP, HEADS])
        msg = sb("w_msg", [P, S3, GROUP, D])
        summed = sb("summed", [P, S3, ROW])
        sums = banks[0:3]
        weights = banks[3]
        member_t = banks[4:6]
        edge_dst = banks[6]

        s_no = sem("node_no_loaded")
        s_pool_on = sem("w_pool_went_on")
        s_idx, s_pidx = sem("w_src_idx_set"), sem("w_put_idx_set")
        s_g = [sem(f"w_gathered{i}") for i in range(S3)]
        s_put = [sem(f"w_put{i}") for i in range(S3)]
        s_win = [sem(f"w_window_loaded{i}") for i in range(S3)]
        names = "member member_t memberT edge_dst score leaky diff ex coef msg sums evac".split()
        d = {k: sem("w_" + k) for k in names}

        def filled(g, slot, per):
            return (g - slot) * (per // S3) + per

        def rounds(eng, drain):
            for u in range(3 * S3):
                yield u, u % S3
            with eng.Fori(3, GROUPS // S3) as i:
                for s in range(S3):
                    yield i * S3 + s, s
            for u in range(GROUPS // S3 * S3, GROUPS + drain):
                yield u, u % S3

        def stage(u, slot, lag, do):
            if isinstance(u, int) and not 0 <= u - lag < GROUPS:
                return
            do(u - lag, (slot - lag) % S3)

        def old(g):
            return reused(g, S3)

        with nc.Block() as block:
            @block.sync
            def _(sp):
                sp.dma_start(node_no[:, :], t["node_no"]).then_inc(s_no, 16)
                for g, s in rounds(sp, 0):
                    base = sp.value_load(keep["bases_int"][0:1, bass.ds(g, 1)], min_val=0, max_val=NODES)
                    if old(g):
                        sp.wait_ge(d["edge_dst"], g - 2)
                    sp.dma_start(window[:, s, :], t["shifts"][bass.ds(base, P), :]).then_inc(s_win[s], 48)

            @block.gpsimd
            def _(pool):
                def gather(g, s):
                    wait_alone(pool, s_idx, g + 1, s_pool_on)
                    if old(g):
                        wait_alone(pool, d["msg"], g - 2, s_pool_on)
                    for j in range(GROUP):
                        pool.indirect_dma_start(
                            out=gathered[:, s, j, :], out_offset=None, in_=t["h"][:, :],
                            in_offset=bass.IndirectOffsetOnAxis(ap=src_idx[:, s, j:j + 1], axis=0)
                        ).then_inc(s_g[s], 16)

                def put(g, s):
                    wait_alone(pool, s_pidx, g + 1, s_pool_on)
                    wait_alone(pool, d["evac"], 2 * (g + 1), s_pool_on)
                    if not (isinstance(g, int) and g == 0):
                        before = (s - 1) % S3
                        wait_alone(pool, s_put[before], filled(g - 1, before, 48), s_pool_on)
                    pool.indirect_dma_start(
                        out=t["agg"][:, :], out_offset=bass.IndirectOffsetOnAxis(ap=put_idx[:, s, :], axis=0),
                        in_=summed[:, s, :], in_offset=None, bounds_check=ROWS - 1, oob_is_err=False,
                        compute_op=ALU.add).then_inc(s_put[s], 48)

                for u, slot in rounds(pool, 4):
                    stage(u, slot, 0, gather)
                    stage(u, slot, 4, put)
                last = GROUPS - 1
                pool.wait_ge(s_put[last % S3], filled(last, last % S3, 48))

            @block.vector
            def _(dve):
                def make_member(g, s):
                    if old(g):
                        dve.wait_ge(d["sums"], g - 2)
                    nc.vector.tensor_tensor(
                        member[:, s, :, :], node_no[:, :].unsqueeze(1).to_broadcast([P, GROUP, P]),
                        keep["rel"][:, bass.ds(g * GROUP, GROUP)].unsqueeze(2).to_broadcast([P, GROUP, P]),
                        ALU.is_equal).then_inc(d["member"], 1)

                def scores(g, s):
                    dve.wait_ge(s_g[s], filled(g, s, 16 * GROUP))
                    dve.wait_ge(d["edge_dst"], g + 1)
                    at_dst = edge_dst[:, 0:GROUP * 2 * HEADS].rearrange("p (j c) -> p j c", j=GROUP)
                    nc.vector.tensor_tensor(score[:, :, :], gathered[:, s, :, D:ROW], at_dst[:, :, 0:HEADS],
                                            ALU.add).then_inc(d["score"], 1)
                    dve.wait_ge(d["score"], g + 1)
                    nc.vector.scalar_tensor_tensor(leaky[:, :, :], score[:, :, :], SLOPE, score[:, :, :], ALU.mult,
                                                   ALU.max).then_inc(d["leaky"], 1)
                    dve.wait_ge(d["leaky"], g + 1)
                    if old(g):
                        dve.wait_ge(d["ex"], g - 2)
                    nc.vector.tensor_tensor(diff[:, s, :, :], leaky[:, :, :], at_dst[:, :, HEADS:], ALU.subtract
                                            ).then_inc(d["diff"], 1)

                def messages(g, s):
                    dve.wait_ge(d["ex"], g + 1)
                    nc.vector.tensor_tensor(coef[:, :, :], ex[:, s, :, :],
                                            keep["dist"][:, bass.ds(g * GROUP, GROUP), :], ALU.mult
                                            ).then_inc(d["coef"], 1)
                    dve.wait_ge(d["coef"], g + 1)
                    if old(g):
                        dve.wait_ge(d["sums"], g - 2)
                    shape = [P, GROUP, HEADS, HD]
                    nc.vector.tensor_tensor(
                        msg[:, s, :, :].rearrange("p j (h d) -> p j h d", h=HEADS),
                        gathered[:, s, :, 0:D].rearrange("p j (h d) -> p j h d", h=HEADS),
                        coef[:, :, :].unsqueeze(3).to_broadcast(shape), ALU.mult).then_inc(d["msg"], 1)

                dve.wait_ge(s_no, 16)
                for u, slot in rounds(dve, 1):
                    stage(u, slot, 1, scores)
                    stage(u, slot, 0, make_member)
                    stage(u, slot, 1, messages)

            @block.tensor
            def _(pe):
                def at_edges(g, s):
                    pe.wait_ge(d["memberT"], 2 * (g + 1))
                    pe.wait_ge(s_win[s], filled(g, s, 48))
                    if not (isinstance(g, int) and g == 0):
                        pe.wait_ge(d["diff"], g)
                    for j in range(GROUP):
                        at = j * 2 * HEADS
                        last = nc.tensor.matmul(edge_dst[:, at:at + 2 * HEADS], memberT[:, s, j, :],
                                                window[:, s, :], start=True, stop=True)
                    last.then_inc(d["edge_dst"], 1)

                def transpose(g, s):
                    pe.wait_ge(d["member"], g + 1)
                    if not (isinstance(g, int) and g == 0):
                        pe.wait_ge(d["memberT"], 2 * g)
                    for j in range(GROUP):
                        last = nc.tensor.transpose(member_t[j // 4][:, j % 4 * P:(j % 4 + 1) * P],
                                                   member[:, s, j, :], keep["ident"][:, :])
                    last.then_inc(d["member_t"], 1)

                def add_up(g, s, part):
                    if part == 0:
                        pe.wait_ge(d["msg"], g + 1)
                        if old(g):
                            pe.wait_ge(d["evac"], 2 * (g - 2))
                    half = GROUP // 2
                    for j in range(part * half, (part + 1) * half):
                        first, final = j == 0, j == GROUP - 1
                        nc.tensor.matmul(sums[s][:, :], member[:, s, j, :], msg[:, s, j, :], start=first,
                                         stop=final)
                    if part == 1:
                        if not (isinstance(g, int) and g == 0):
                            pe.wait_ge(d["evac"], 2 * g)
                        for j in range(GROUP):
                            last = nc.tensor.matmul(weights[:, 0:HEADS], member[:, s, j, :], ex[:, s, j, :],
                                                    start=(j == 0), stop=(j == GROUP - 1))
                        last.then_inc(d["sums"], 1)

                for u, slot in rounds(pe, 2):
                    stage(u, slot, 1, at_edges)
                    stage(u, slot, 2, lambda g, s: add_up(g, s, 0))
                    stage(u, slot, 0, transpose)
                    stage(u, slot, 2, lambda g, s: add_up(g, s, 1))

            @block.scalar
            def _(act):
                def copy(out, in_):
                    return nc.scalar.activation(out, in_, ACT.Copy)

                def set_src(g, s):
                    if old(g):
                        act.wait_ge(s_g[s], filled(g - S3, s, 16 * GROUP))
                    copy(src_idx[:, s, :], keep["src"][:, bass.ds(g, 1), :].rearrange("p o j -> p (o j)")
                         ).then_inc(s_idx, 1)

                def exps(g, s):
                    act.wait_ge(d["diff"], g + 1)
                    if old(g):
                        act.wait_ge(d["sums"], g - 2)
                    nc.scalar.activation(ex[:, s, :, :], diff[:, s, :, :], ACT.Exp).then_inc(d["ex"], 1)

                def turn_member(g, s):
                    act.wait_ge(d["member_t"], g + 1)
                    if old(g):
                        act.wait_ge(d["edge_dst"], g - 2)
                    copy(memberT[:, s, 0:4, :], member_t[0][:, :].rearrange("p (j c) -> p j c", j=4)
                         ).then_inc(d["memberT"], 1)
                    copy(memberT[:, s, 4:GROUP, :],
                         member_t[1][:, 0:(GROUP - 4) * P].rearrange("p (j c) -> p j c", j=GROUP - 4)
                         ).then_inc(d["memberT"], 1)

                def evacuate(g, s):
                    act.wait_ge(d["sums"], g + 1)
                    if old(g):
                        act.wait_ge(s_put[s], filled(g - S3, s, 48))
                    copy(summed[:, s, 0:D], sums[s][:, :]).then_inc(d["evac"], 1)
                    copy(summed[:, s, D:ROW], weights[:, 0:HEADS]).then_inc(d["evac"], 1)
                    copy(put_idx[:, s, :], keep["put"][:, bass.ds(g, 1)]).then_inc(s_pidx, 1)

                set_src(0, 0)
                for u, slot in rounds(act, 3):
                    stage(u, slot, -1, set_src)
                    stage(u, slot, 1, exps)
                    stage(u, slot, 0, turn_member)
                    stage(u, slot, 3, evacuate)


def finish(nc, top, banks, t, keep):
    with ExitStack() as ctx:
        def sb(name, shape, dt=F32):
            return ctx.enter_context(nc.sbuf_tensor(name, shape, dt))

        def sem(name):
            return top.enter_context(nc.semaphore(name))

        C = CHUNK
        w1 = sb("w1", [FEATS, 5, P])
        w2 = sb("w2", [P, 13, P])
        w3 = sb("w3", [P, 5, 8])
        b2 = sb("b2", [P, 5])
        b3 = sb("b3", [P, 8])
        countdown = sb("countdown", [P, 64])
        digits = sb("digits", [P, 2, 16])
        x = sb("x_in", [P, 2, C, D])
        agg = sb("agg_in", [P, 2, C, ROW])
        y = sb("y", [P, C, D])
        res = sb("res", [P, 2, C, D])
        wsum = sb("wsum", [P, C, HEADS])
        rsum = sb("rsum", [P, C, HEADS])
        stats = sb("fstats", [P, C, 6])
        mean_var = sb("fmean_var", [P, C, 2])
        var_eps = sb("fvar_eps", [P, C])
        std = sb("fstd", [P, C])
        rstd = sb("frstd", [P, C])
        hits = sb("hits", [P, C, 64])
        best = sb("best", [P, C, 4])
        first = sb("first", [P, C, 4])
        feats = sb("feats", [P, 2, C, FEATS])
        flags = sb("flags", [P, C, 3])
        both = sb("both", [P, 2, C, 2])
        picks = sb("picks", [P, 2, C, 2])
        active = sb("active", [P, 2, C])
        active2 = sb("active2", [P, 2, C])
        featsT = sb("featsT", [FEATS, C * P])
        h1 = sb("h1", [P, 5, C * P])
        h2 = sb("h2", [P, 5, C * P])
        v3 = sb("v3", [P, C, 8])
        added = sb("added", [P, C, 3])
        subbed = sb("subbed", [P, C, 3])
        value = sb("value", [P, C, 3])
        clipped = sb("clipped", [P, C, 3])
        shifted = sb("shifted", [P, C, 3])
        rounded = sb("rounded", [P, C, 3])
        hot = sb("hot", [P, C, 2, 16])
        carry = sb("carry", [P, C])
        feats_t = banks[0]
        layer = banks[1:7]
        y3 = banks[7]

        s_dve_on = sem("fin_dve_went_on")
        s_w = sem("mlp_weights_loaded")
        s_ones = sem("feats_ones_set")
        s_in = [sem("chunk_loaded0"), sem("chunk_loaded1")]
        s_out = [sem("out_stored0"), sem("out_stored1")]
        per_chunk = ("wsum rsum x1 var_eps std rstd res best first feats_ops feats_nibbles flags both m_add all "
                     "m_sub active active2 feats_t featsT mm h1 h2 y3 v3 added subbed value clipped shifted "
                     "rounded carry carried").split()
        per_tile = "scaled stats mean_var y hits hot placed".split()
        d = {k: sem("fin_" + k) for k in per_chunk + per_tile}

        def chunks(eng):
            yield 0, 0, C
            yield 1, 1, C
            with eng.Fori(1, CHUNKS // 2) as i:
                yield 2 * i, 0, C
                yield 2 * i + 1, 1, C
            yield CHUNKS, 0, NODE_TILES - CHUNKS * C

        with nc.Block() as block:
            @block.sync
            def _(sp):
                for name, tile in (("w1", w1), ("w2", w2), ("w3", w3), ("b2", b2), ("b3", b3),
                                   ("countdown", countdown), ("digits", digits)):
                    whole = tile[:, :, :] if len(tile.shape) == 3 else tile[:, :]
                    sp.dma_start(whole, t[name]).then_inc(s_w, 16)

                def store(c, s, k):
                    sp.wait_ge(d["placed"], c * C + k)
                    sp.wait_ge(d["carried"], c + 1)
                    if k == C:
                        sp.dma_start(t["out"][bass.ds(c * (C * P), C * P), :].rearrange("(k p) n -> p k n", p=P),
                                     res[:, s, :, :]).then_inc(s_out[s], 16)
                    else:
                        rows = N - CHUNKS * C * P
                        sp.dma_start(t["out"][N - rows:N, :], res[0:rows, s, 0, :]).then_inc(s_out[s], 16)

                for c, s, k in chunks(sp):
                    if reused(c):
                        sp.wait_ge(d["res"], c - 1)
                    rows = bass.ds(c * (C * P), k * P)
                    sp.dma_start(x[:, s, 0:k, :], t["x"][rows, :].rearrange("(k p) n -> p k n", p=P)
                                 ).then_inc(s_in[s], 16)
                    sp.dma_start(agg[:, s, 0:k, :], t["agg"][rows, :].rearrange("(k p) n -> p k n", p=P)
                                 ).then_inc(s_in[s], 16)
                    if reused(c):
                        store(c - 2, s, C)
                store(CHUNKS - 1, 1, C)
                store(CHUNKS, 0, NODE_TILES - CHUNKS * C)
                sp.wait_ge(s_out[0], dma_count(CHUNKS, 0))
                sp.wait_ge(s_out[1], dma_count(CHUNKS - 1, 1))

            @block.gpsimd
            def _(pool):
                for c, s, k in chunks(pool):
                    pool.wait_ge(d["y"], c * C + k)
                    if reused(c):
                        pool.wait_ge(s_out[s], dma_count(c - 2, s))
                    nc.gpsimd.tensor_tensor(res[:, s, 0:k, :], x[:, s, 0:k, :], y[:, 0:k, :], ALU.add
                                            ).then_inc(d["res"], 1)

            @block.scalar
            def _(act):
                def relus(c, k):
                    w = k * P
                    act.wait_ge(d["feats_t"], c + 1)
                    if reused(c, 1):
                        act.wait_ge(d["mm"], 10 * c)
                    nc.scalar.activation(featsT[:, 0:w], feats_t[0:FEATS, 0:w], ACT.Copy).then_inc(d["featsT"], 1)
                    for g in range(5):
                        act.wait_ge(d["mm"], 10 * c + g + 1)
                        nc.scalar.activation(h1[:, g, 0:w], layer[g][:, 0:w], ACT.Relu).then_inc(d["h1"], 1)
                    for g in range(5):
                        act.wait_ge(d["mm"], 10 * c + 5 + g + 1)
                        if reused(c, 1):
                            act.wait_ge(d["y3"], c)
                        nc.scalar.activation(h2[:, g, 0:w], layer[(5 + g) % 6][:, 0:w], ACT.Relu,
                                             bias=b2[:, g:g + 1]).then_inc(d["h2"], 1)

                act.wait_ge(s_w, 7 * 16)
                for c, s, k in chunks(act):
                    act.wait_ge(d["var_eps"], c + 1)
                    nc.scalar.activation(std[:, 0:k], var_eps[:, 0:k], ACT.Sqrt).then_inc(d["std"], 1)
                    if isinstance(c, int) and c == 0:
                        continue
                    relus(c - 1, C)
                relus(CHUNKS, NODE_TILES - CHUNKS * C)

            @block.tensor
            def _(pe):
                pe.wait_ge(s_w, 7 * 16)
                for c, s, k in chunks(pe):
                    w = k * P
                    pe.wait_ge(s_ones, 2)
                    pe.wait_ge(d["feats_ops"], c + 1)
                    pe.wait_ge(d["feats_nibbles"], c + 1)
                    if reused(c, 1):
                        pe.wait_ge(d["featsT"], c)
                    for j in range(k):
                        last = nc.tensor.transpose(feats_t[0:FEATS, j * P:(j + 1) * P], feats[:, s, j, :],
                                                   keep["ident"][:, :])
                    last.then_inc(d["feats_t"], 1)
                    pe.wait_ge(d["featsT"], c + 1)
                    if reused(c, 1):
                        pe.wait_ge(d["h2"], 5 * c)
                    for g in range(5):
                        nc.tensor.matmul(layer[g][:, 0:w], w1[:, g, :], featsT[:, 0:w], start=True,
                                         stop=True).then_inc(d["mm"], 1)
                    pe.wait_ge(d["h1"], 5 * (c + 1))
                    for g in range(4):
                        bank = layer[(5 + g) % 6]
                        nc.tensor.matmul(bank[:, 0:w], w2[:, g, :], h1[:, g, 0:w], start=True, stop=False)
                        nc.tensor.matmul(bank[:, 0:w], w2[:, 4 + g, :], h1[:, 4, 0:w], start=False,
                                         stop=True).then_inc(d["mm"], 1)
                    bank = layer[9 % 6]
                    for g in range(5):
                        last = nc.tensor.matmul(bank[:, 0:w], w2[:, 8 + g, :], h1[:, g, 0:w], start=(g == 0),
                                                stop=(g == 4))
                    last.then_inc(d["mm"], 1)
                    pe.wait_ge(d["h2"], 5 * (c + 1))
                    if reused(c, 1):
                        pe.wait_ge(d["v3"], c)
                    for j in range(k):
                        for g in range(5):
                            last = nc.tensor.matmul(y3[:, 8 * j:8 * j + 8], h2[:, g, j * P:(j + 1) * P],
                                                    w3[:, g, :], start=(g == 0), stop=(g == 4))
                    last.then_inc(d["y3"], 1)

            @block.vector
            def _(dve):
                def front(c, s, k):
                    def need(name):
                        dve.wait_ge(d[name], c + 1)

                    def need_tiles(name):
                        dve.wait_ge(d[name], c * C + k)

                    loaded = 2 * dma_count(c, s) if isinstance(c, int) else (c - s) * 16 + 32
                    dve.wait_ge(s_in[s], loaded)
                    xk, ak = x[:, s, 0:k, :], agg[:, s, 0:k, :]
                    nc.vector.tensor_scalar_max(wsum[:, 0:k, :], ak[:, :, D:ROW], TINY).then_inc(d["wsum"], 1)
                    need("wsum")
                    nc.vector.reciprocal(rsum[:, 0:k, :], wsum[:, 0:k, :]).then_inc(d["rsum"], 1)
                    need("rsum")
                    for j in range(k):
                        heads = agg[:, s, j, 0:D].rearrange("p (h d) -> p h d", h=HEADS)
                        nc.vector.tensor_tensor(heads, heads, rsum[:, j, :].unsqueeze(2)
                                                .to_broadcast([P, HEADS, HD]), ALU.mult).then_inc(d["scaled"], 1)
                    need_tiles("scaled")
                    nc.vector.tensor_tensor(xk, xk, ak[:, :, 0:D], ALU.add).then_inc(d["x1"], 1)
                    need("x1")
                    for j in range(k):
                        nc.vector.bn_stats(stats[:, j, :], x[:, s, j, :]).then_inc(d["stats"], 1)
                    wait_alone(dve, d["stats"], c * C + k, s_dve_on)
                    for j in range(k):
                        nc.vector.bn_aggr(mean_var[:, j, :], stats[:, j, :]).then_inc(d["mean_var"], 1)
                    need_tiles("mean_var")
                    nc.vector.tensor_scalar_add(var_eps[:, 0:k], mean_var[:, 0:k, 1], EPS).then_inc(d["var_eps"], 1)
                    need("std")
                    nc.vector.reciprocal(rstd[:, 0:k], std[:, 0:k]).then_inc(d["rstd"], 1)
                    need("rstd")
                    if reused(c, 1):
                        dve.wait_ge(d["res"], c)
                    for j in range(k):
                        nc.vector.tensor_scalar(y[:, j, :], x[:, s, j, :], mean_var[:, j, 0:1], rstd[:, j:j + 1],
                                                ALU.subtract, ALU.mult).then_inc(d["y"], 1)
                    need_tiles("y")
                    if reused(c):
                        dve.wait_ge(d["feats_t"], c - 1)
                    nc.vector.tensor_copy(feats[:, s, 0:k, 4:6], y[:, 0:k, X_OP_ADD:X_OP_SUB + 1]
                                          ).then_inc(d["feats_ops"], 1)
                    for j in range(k):
                        nc.vector.scalar_tensor_tensor(hits[:, j, :], y[:, j, 16:80], 0.5, countdown[:, :],
                                                       ALU.is_gt, ALU.mult).then_inc(d["hits"], 1)
                    nc.vector.tensor_scalar(flags[:, 0:k, :], y[:, 0:k, 0:3], 0.5, None, ALU.is_gt
                                            ).then_inc(d["flags"], 1)
                    need_tiles("hits")
                    nc.vector.tensor_reduce(best[:, 0:k, :], hits[:, 0:k, :].rearrange("p k (f j) -> p k f j", j=16),
                                            AX, ALU.max).then_inc(d["best"], 1)
                    need("best")
                    nc.vector.tensor_scalar(first[:, 0:k, :], best[:, 0:k, :], -1.0, 16.0, ALU.mult, ALU.add
                                            ).then_inc(d["first"], 1)
                    need("first")
                    nc.vector.scalar_tensor_tensor(feats[:, s, 0:k, 0:4], best[:, 0:k, :], 0.0, first[:, 0:k, :],
                                                   ALU.is_gt, ALU.mult).then_inc(d["feats_nibbles"], 1)
                    need("flags")
                    mark, add, sub = (flags[:, 0:k, i] for i in range(3))
                    nc.vector.tensor_tensor(picks[:, s, 0:k, 0], mark, add, ALU.mult).then_inc(d["m_add"], 1)
                    nc.vector.tensor_tensor(both[:, s, 0:k, 0], mark, sub, ALU.mult).then_inc(d["both"], 1)
                    need("both")
                    nc.vector.tensor_tensor(both[:, s, 0:k, 1], both[:, s, 0:k, 0], add, ALU.mult
                                            ).then_inc(d["all"], 1)
                    need("all")
                    nc.vector.tensor_tensor(picks[:, s, 0:k, 1], both[:, s, 0:k, 0], both[:, s, 0:k, 1],
                                            ALU.subtract).then_inc(d["m_sub"], 1)
                    need("m_sub")
                    need("m_add")
                    nc.vector.tensor_tensor(active[:, s, 0:k], picks[:, s, 0:k, 0], picks[:, s, 0:k, 1], ALU.add
                                            ).then_inc(d["active"], 1)
                    need("active")
                    nc.vector.tensor_scalar_mul(active2[:, s, 0:k], active[:, s, 0:k], 2.0).then_inc(d["active2"], 1)

                def tail(c, s, k):
                    def need(name):
                        dve.wait_ge(d[name], c + 1)

                    need("y3")
                    nc.vector.tensor_tensor(v3[:, 0:k, :], y3[:, 0:8 * k].rearrange("p (k o) -> p k o", o=8),
                                            b3[:, :].unsqueeze(1).to_broadcast([P, k, 8]), ALU.add
                                            ).then_inc(d["v3"], 1)
                    need("v3")
                    nc.vector.tensor_tensor(added[:, 0:k, :], v3[:, 0:k, 0:3],
                                            picks[:, s, 0:k, 0:1].to_broadcast([P, k, 3]), ALU.mult
                                            ).then_inc(d["added"], 1)
                    nc.vector.tensor_tensor(subbed[:, 0:k, :], v3[:, 0:k, 3:6],
                                            picks[:, s, 0:k, 1:2].to_broadcast([P, k, 3]), ALU.mult
                                            ).then_inc(d["subbed"], 1)
                    need("added")
                    need("subbed")
                    nc.vector.tensor_tensor(value[:, 0:k, :], added[:, 0:k, :], subbed[:, 0:k, :], ALU.add
                                            ).then_inc(d["value"], 1)
                    need("value")
                    nc.vector.tensor_scalar(clipped[:, 0:k, :], value[:, 0:k, :], 0.0, 15.0, ALU.max, ALU.min
                                            ).then_inc(d["clipped"], 1)
                    need("clipped")
                    nc.vector.tensor_scalar_add(shifted[:, 0:k, :], clipped[:, 0:k, :], ROUNDER
                                                ).then_inc(d["shifted"], 1)
                    need("shifted")
                    nc.vector.tensor_scalar_add(rounded[:, 0:k, :], shifted[:, 0:k, :], -ROUNDER
                                                ).then_inc(d["rounded"], 1)
                    need("rounded")
                    need("res")
                    for j in range(k):
                        nc.vector.tensor_tensor(hot[:, j, :, :], digits[:, :, :],
                                                rounded[:, j, 0:2].unsqueeze(2).to_broadcast([P, 2, 16]),
                                                ALU.is_equal).then_inc(d["hot"], 1)
                    nc.vector.scalar_tensor_tensor(carry[:, 0:k], rounded[:, 0:k, 2], 0.5, active[:, s, 0:k],
                                                   ALU.is_gt, ALU.mult).then_inc(d["carry"], 1)
                    dve.wait_ge(d["hot"], c * C + k)
                    for j in range(k):
                        place = res[:, s, j, 128:160]
                        nc.vector.scalar_tensor_tensor(place, hot[:, j, :, :].rearrange("p a b -> p (a b)"),
                                                       active2[:, s, j:j + 1], place, ALU.mult, ALU.add
                                                       ).then_inc(d["placed"], 1)
                    need("carry")
                    nc.vector.tensor_tensor(res[:, s, 0:k, 160], res[:, s, 0:k, 160], carry[:, 0:k], ALU.add
                                            ).then_inc(d["carried"], 1)

                dve.wait_ge(s_w, 7 * 16)
                nc.vector.memset(feats[:, :, :, 6:7], 1.0).then_inc(s_ones, 1)
                nc.vector.memset(feats[:, :, :, 7:8], 0.0).then_inc(s_ones, 1)
                for c, s, k in chunks(dve):
                    front(c, s, k)
                    if isinstance(c, int) and c == 0:
                        continue
                    tail(c - 1, 1 - s, C)
                tail(CHUNKS, 0, NODE_TILES - CHUNKS * C)


ROUNDER = 1.5 * 2.0 ** 23

SHAPES = {
    "x": (NODES, D), "wt": (D, D), "bias": (1, D), "w_src": (P, D), "w_dst": (P, D), "ident": (P, P),
    "src": (P, GROUPS, GROUP), "dst": (P, GROUPS, GROUP), "row_no": (P, 1), "node_no": (P, P), "dist": (P, EDGE_TILES, HEADS), "before": (P, P),
    "w1": (FEATS, 5, P), "w2": (P, 13, P), "w3": (P, 5, 8), "b2": (P, 5), "b3": (P, 8),
    "countdown": (P, 64), "digits": (P, 2, 16),
}


def program(nc, t):
    with ExitStack() as top:
        def sb(name, shape, dt=F32):
            return top.enter_context(nc.sbuf_tensor("k_" + name, shape, dt))

        keep = {
            "src": sb("src", [P, GROUPS, GROUP], I32),
            "dst": sb("dst", [P, GROUPS, GROUP], I32),
            "dist": sb("dist", [P, EDGE_TILES, HEADS]),
            "rel": sb("rel", [P, EDGE_TILES]),
            "bases": sb("bases", [P, GROUPS]),
            "bases_int": sb("bases_int", [1, GROUPS], I32),
            "put": sb("put", [P, GROUPS], I32),
            "excess": sb("excess", [P, 3]),
            "general": sb("general", [P, 1], I32),
            "ident": top.enter_context(nc.sbuf_tensor("ident", [P, P], F32)),
            "esrc": top.enter_context(nc.sbuf_tensor("esrc", [P, NODE_TILES * HEADS], F32)),
            "edst": top.enter_context(nc.sbuf_tensor("edst", [P, NODE_TILES * HEADS], F32)),
        }
        banks = [top.enter_context(nc.psum_tensor(f"bank{i}", [P, 512], F32)) for i in range(8)]
        t["h"] = nc.dram_tensor("table_h", (ROWS, ROW), F32).ap()
        t["agg"] = nc.dram_tensor("table_agg", (ROWS, ROW), F32).ap()
        t["maxima"] = nc.dram_tensor("table_maxima", (ROWS, 2 * HEADS), F32).ap()
        t["shifts"] = nc.dram_tensor("table_shifts", (ROWS, 2 * HEADS), F32).ap()
        project(nc, top, banks, t, keep)
        prepare(nc, top, banks, t, keep)
        _, (general,) = nc.values_load_multi_w_load_instructions(keep["general"][0:1, 0:1], min_val=0, max_val=1)
        with nc.If(general):
            attend_any(nc, top, banks, t, keep)
        with nc.Else():
            attend_windows(nc, top, banks, t, keep)
        finish(nc, top, banks, t, keep)


def layout(x, src, dst, edge_attr_8, L0_gnn_W, L0_gnn_b, L0_gnn_w_att_src, L0_gnn_w_att_dst,
           L0_ffn_Wa, L0_ffn_ba, L0_ffn_Ws, L0_ffn_bs):
    a = {}
    a["x"] = np.zeros((NODES, D), np.float32)
    a["x"][:N] = x
    a["wt"] = L0_gnn_W.T
    a["bias"] = L0_gnn_b[None]
    a["w_src"] = np.broadcast_to(L0_gnn_w_att_src.reshape(1, D), (P, D))
    a["w_dst"] = np.broadcast_to(L0_gnn_w_att_dst.reshape(1, D), (P, D))
    a["ident"] = np.eye(P, dtype=np.float32)
    a["before"] = np.tril(np.ones((P, P), np.float32), -1)
    for name, ends in (("src", src), ("dst", dst)):
        padded = np.full(EDGE_TILES * P, NOWHERE, np.int32)
        padded[:E] = ends
        a[name] = padded.reshape(GROUPS, GROUP, P).transpose(2, 0, 1)
    a["row_no"] = np.arange(P, dtype=np.float32)[:, None]
    a["node_no"] = np.broadcast_to(np.arange(P, dtype=np.float32), (P, P))
    dist = np.zeros((EDGE_TILES * P, HEADS), np.float32)
    dist[:E] = edge_attr_8
    a["dist"] = dist.reshape(EDGE_TILES, P, HEADS).transpose(1, 0, 2)

    w1 = np.zeros((FEATS, 5, P), np.float32)
    w2 = np.zeros((P, 13, P), np.float32)
    w3 = np.zeros((P, 5, 8), np.float32)
    b2 = np.zeros((P, 5), np.float32)
    b3 = np.zeros((P, 8), np.float32)
    nets = [(L0_ffn_Wa, L0_ffn_ba), (L0_ffn_Ws, L0_ffn_bs)]
    for g, (net, pos) in enumerate(COMBOS):
        w, b = nets[net]
        last = slice(REM * g, REM * (g + 1))
        rows = [(pos, NIB_A), (2 + pos, NIB_B), (4, OP_ADD_IN), (5, OP_SUB_IN)]
        for row, col in rows:
            w1[row, g] = w[0][:P, col]
            w1[row, 4, last] = w[0][P:, col]
        w1[6, g] = b[0][:P]
        w1[6, 4, last] = b[0][P:]
        w2[:, g] = w[1][:P, :P].T
        w2[last, 4 + g] = w[1][:P, P:].T
        w2[:, 8 + g, last] = w[1][P:, :P].T
        w2[last, 12, last] = w[1][P:, P:].T
        b2[:, g] = b[1][:P]
        b2[last, 4] = b[1][P:]
        outs = [(3 * net + pos, RESULT)] + [(3 * net + 2, CARRY_OUT)] * pos
        for out, row in outs:
            w3[:, g, out] = w[2][row, :P]
            w3[last, 4, out] = w[2][row, P:]
            b3[:, out] = b[2][row]
    a.update(w1=w1, w2=w2, w3=w3, b2=b2, b3=b3)
    a["countdown"] = np.broadcast_to(np.tile(16.0 - np.arange(16), 4).astype(np.float32), (P, 64))
    a["digits"] = np.broadcast_to(np.arange(16).astype(np.float32), (P, 2, 16))
    return a


def kernel(**inputs):
    import concourse.bacc as bacc
    from concourse.bass_utils import run_bass_kernel_spmd

    arrays = {"in_" + k: np.ascontiguousarray(v) for k, v in layout(**{k: np.asarray(v) for k, v in inputs.items()}
                                                                     ).items()}
    nc = bacc.Bacc("TRN2", target_bir_lowering=False, num_devices=1)
    t = {}
    for name, shape in SHAPES.items():
        assert arrays["in_" + name].shape == shape, name
        dt = mybir.dt.from_np(arrays["in_" + name].dtype)
        t[name] = nc.dram_tensor("in_" + name, shape, dt, kind="ExternalInput").ap()
    t["out"] = nc.dram_tensor("out", (N, D), F32, kind="ExternalOutput").ap()
    program(nc, t)
    return run_bass_kernel_spmd(nc, [arrays], core_ids=[0]).results[0]["out"]
```

```python
from contextlib import ExitStack

import concourse.bass as bass
import numpy as np
from concourse import mybir

F32 = mybir.dt.float32
I32 = mybir.dt.int32
BF16 = mybir.dt.bfloat16
ALU = mybir.AluOpType
ACT = mybir.ActivationFunctionType
AX = mybir.AxisListType.X

P = 128
N, D, HEADS, E = 6250, 512, 8, 100000
HD = D // HEADS
SLOPE = 0.2
EPS = 1e-5
NODE_TILES = -(-N // P)
NODES = NODE_TILES * P
ROWS = NODES + P
NOWHERE = NODES
DC = D // P
ROW = D + HEADS
GROUP = 7
GROUPS = -(-E // (P * GROUP))
EDGE_TILES = GROUPS * GROUP
TINY = 1e-30
FAR = 1 << 20
LOWEST = -3e38
SAFE_WIDTH = 64.0
RMAX = bass.bass_isa.ReduceOp.max

GE = 160
REM = GE - P
RESULT, CARRY_OUT = 100, 101
NIB_A, NIB_B, OP_ADD_IN, OP_SUB_IN = 0, 1, 35, 36
X_OP_ADD, X_OP_SUB = 105, 106
OPS_AT = 16
PAIRS = OPS_AT + 18
COMBOS = [(0, 0), (0, 1), (1, 0), (1, 1)]
OUTS = 6
CHUNK = 4
CHUNKS = NODE_TILES // CHUNK


def turns(eng, total):
    for n in range(4):
        yield n, n % 2
    with eng.Fori(2, total // 2) as i:
        yield 2 * i, 0
        yield 2 * i + 1, 1
    if total % 2:
        yield total - 1, 0


def reused(turn, slots=2):
    return not (isinstance(turn, int) and turn < slots)


def dma_count(turn, slot, slots=2):
    if isinstance(turn, int):
        return 16 * ((turn - slot) // slots + 1)
    return (turn - slot) * (16 // slots) + 16


def wait_alone(eng, semaphore, value, went_on):
    eng.wait_ge(semaphore, value)
    eng.sem_inc(went_on, 1)


def edge_turns(eng):
    yield 0
    with eng.Fori(1, EDGE_TILES) as n:
        yield n


def split3(vector, wait, d, whole, hi, mid, lo, rest):
    vector.tensor_copy(hi, whole).then_inc(d["hi"], 1)
    wait(d["hi"], 1)
    vector.tensor_tensor(rest, whole, hi, ALU.subtract).then_inc(d["rest"], 1)
    wait(d["rest"], 1)
    vector.tensor_copy(mid, rest).then_inc(d["mid"], 1)
    wait(d["mid"], 1)
    vector.tensor_tensor(rest, rest, mid, ALU.subtract).then_inc(d["rest"], 1)
    wait(d["rest"], 2)
    vector.tensor_copy(lo, rest).then_inc(d["lo"], 1)


def project(nc, top, banks, t, keep):
    with ExitStack() as ctx:
        def sb(name, shape, dt=F32):
            return ctx.enter_context(nc.sbuf_tensor(name, shape, dt))

        def sem(name):
            return top.enter_context(nc.semaphore(name))

        wt = sb("wt", [P, DC, D])
        bias3 = sb("bias3", [3, D])
        bias_part = [sb(f"bias_part{i}", [3, D], BF16) for i in range(3)]
        bias_rest = sb("bias_rest", [3, D])
        bias_sum = [sb(f"bias_sum{i}", [3, D], BF16) for i in range(3)]
        pick3 = sb("pick3", [3, 3])
        ones3 = sb("ones3", [3, P], BF16)
        w_src = sb("w_src", [P, D])
        w_dst = sb("w_dst", [P, D])
        zeros = sb("zeros", [P, ROW])
        xt = sb("xt", [P, 2, D])
        xn = sb("xn", [P, 2, D])
        xnT = sb("xnT", [P, 2, D])
        stats = sb("stats", [P, 2, 6])
        mean_var = sb("mean_var", [P, 2, 2])
        var_eps = sb("var_eps", [P, 2, 1])
        std = sb("std", [P, 2, 1])
        rstd = sb("rstd", [P, 2, 1])
        leak = sb("leak", [P, 2, D])
        hrow = sb("hrow", [P, 2, ROW])
        prod_src = sb("prod_src", [P, D])
        prod_dst = sb("prod_dst", [P, 2, D])
        ps_t, ps_h = banks[0:2], banks[2:4]

        s_const = sem("const_loaded")
        s_edges = sem("edge_arrays_loaded")
        s_set = sem("const_set")
        s_zero = sem("zeros_set")
        s_ztab = sem("zeros_stored")
        s_dve_on = sem("dve_went_on")
        s_x = [sem("x_loaded0"), sem("x_loaded1")]
        s_stats, s_mv, s_ve = sem("stats_ready"), sem("meanvar_ready"), sem("vareps_ready")
        s_std, s_rstd, s_xn = sem("std_ready"), sem("rstd_ready"), sem("xn_ready")
        s_tr, s_xnT = sem("transposed"), sem("xnT_ready")
        s_h, s_leak, s_row = sem("h_ready"), sem("leak_ready"), sem("hrow_ready")
        s_psrc, s_esrc, s_kept = sem("prod_src_ready"), sem("esrc_ready"), sem("esrc_kept")
        s_pdst, s_edst = sem("prod_dst_ready"), sem("edst_ready")
        s_out = [sem("hrow_stored0"), sem("hrow_stored1")]
        s_bias = sem("bias_split")
        parts = {k: sem("bias_" + k) for k in ("hi", "rest", "mid", "lo")}
        CONSTS = 6 * 16
        last = NODE_TILES - 1

        with nc.Block() as block:
            @block.sync
            def _(sp):
                def store(n, s):
                    sp.wait_ge(s_esrc, n + 1)
                    sp.dma_start(t["h"][bass.ds(n * P, P), :], hrow[:, s, :]).then_inc(s_out[s], 16)

                def load(n, s):
                    if reused(n):
                        sp.wait_ge(s_xn, n - 1)
                    sp.dma_start(xt[:, s, :], t["x"][bass.ds(n * P, P), :]).then_inc(s_x[s], 16)

                load(0, 0)
                load(1, 1)
                sp.dma_start(keep["ident"][:, :], t["ident"]).then_inc(s_const, 16)
                sp.dma_start(wt[:, :, :], t["wt"].rearrange("(c p) n -> p c n", p=P)).then_inc(s_const, 16)
                sp.dma_start(bias3[:, :], t["bias3"]).then_inc(s_const, 16)
                sp.dma_start(pick3[:, :], t["pick3"]).then_inc(s_const, 16)
                sp.dma_start(w_src[:, :], t["w_src"]).then_inc(s_const, 16)
                sp.dma_start(w_dst[:, :], t["w_dst"]).then_inc(s_const, 16)
                for name in ("src", "dst", "dist"):
                    sp.dma_start(keep[name][:, :, :], t[name]).then_inc(s_edges, 16)
                sp.wait_ge(s_zero, 1)
                for table in (t["h"], t["agg"]):
                    sp.dma_start(table[NODES:ROWS, :], zeros[:, :]).then_inc(s_ztab, 16)
                for n, s in turns(sp, NODE_TILES):
                    if reused(n):
                        load(n, s)
                    if reused(n, 3):
                        store(n - 3, 1 - s)
                    sp.dma_start(t["agg"][bass.ds(n * P, P), :], zeros[:, :]).then_inc(s_ztab, 16)
                store(last - 2, 0)
                store(last - 1, 1)
                store(last, 0)
                sp.wait_ge(s_out[0], dma_count(last, 0))
                sp.wait_ge(s_out[1], dma_count(last - 1, 1))
                sp.wait_ge(s_ztab, 16 * (NODE_TILES + 2))
                sp.wait_ge(s_edges, 3 * 16)

            @block.gpsimd
            def _(pool):
                nc.gpsimd.memset(zeros[:, :], 0.0).then_inc(s_zero, 1)
                nc.gpsimd.memset(ones3[:, :], 1.0).then_inc(s_set, 1)
                pool.wait_ge(s_const, CONSTS)
                for n, s in turns(pool, NODE_TILES):
                    pool.wait_ge(s_row, n + 1)
                    if reused(n):
                        pool.wait_ge(s_edst, n - 1)
                    nc.gpsimd.tensor_tensor(prod_dst[:, s, :], hrow[:, s, 0:D], w_dst[:, :],
                                            ALU.mult).then_inc(s_pdst, 1)

            @block.vector
            def _(dve):
                def normalise(n, s):
                    dve.wait_ge(s_x[s], dma_count(n, s))
                    nc.vector.bn_stats(stats[:, s, :], xt[:, s, :]).then_inc(s_stats, 1)
                    wait_alone(dve, s_stats, n + 1, s_dve_on)
                    nc.vector.bn_aggr(mean_var[:, s, :], stats[:, s, :]).then_inc(s_mv, 1)
                    dve.wait_ge(s_mv, n + 1)
                    if reused(n):
                        dve.wait_ge(s_std, n - 1)
                    nc.vector.tensor_scalar_add(var_eps[:, s, :], mean_var[:, s, 1:2], EPS).then_inc(s_ve, 1)
                    dve.wait_ge(s_std, n + 1)
                    nc.vector.reciprocal(rstd[:, s, :], std[:, s, :]).then_inc(s_rstd, 1)
                    dve.wait_ge(s_rstd, n + 1)
                    if reused(n):
                        dve.wait_ge(s_tr, n - 1)
                    nc.vector.tensor_scalar(xn[:, s, :], xt[:, s, :], mean_var[:, s, 0:1], rstd[:, s, :],
                                            ALU.subtract, ALU.mult).then_inc(s_xn, 1)

                def scores(n, s):
                    dve.wait_ge(s_leak, n + 1)
                    if reused(n):
                        dve.wait_ge(s_out[s], dma_count(n - 2, s))
                        dve.wait_ge(s_pdst, n - 1)
                        dve.wait_ge(s_kept, n - 1)
                    nc.vector.tensor_tensor(hrow[:, s, 0:D], leak[:, s, :], ps_h[s][:, :], ALU.max).then_inc(s_row, 1)
                    dve.wait_ge(s_row, n + 1)
                    if reused(n, 1):
                        dve.wait_ge(s_esrc, n)
                    nc.vector.tensor_tensor(prod_src[:, :], hrow[:, s, 0:D], w_src[:, :], ALU.mult
                                            ).then_inc(s_psrc, 1)
                    dve.wait_ge(s_psrc, n + 1)
                    nc.vector.tensor_reduce(hrow[:, s, D:ROW], prod_src[:, :].rearrange("p (h d) -> p h d", h=HEADS),
                                            AX, ALU.add).then_inc(s_esrc, 1)
                    dve.wait_ge(s_pdst, n + 1)
                    nc.vector.tensor_reduce(keep["edst"][:, bass.ds(n * HEADS, HEADS)],
                                            prod_dst[:, s, :].rearrange("p (h d) -> p h d", h=HEADS), AX,
                                            ALU.add).then_inc(s_edst, 1)

                dve.wait_ge(s_const, CONSTS)
                split3(nc.vector, dve.wait_ge, parts, bias3[:, :], bias_part[0][:, :], bias_part[1][:, :],
                       bias_part[2][:, :], bias_rest[:, :])
                dve.wait_ge(parts["lo"], 1)
                nc.vector.tensor_scalar(bias_sum[0][:, :], bias_part[0][:, :], pick3[:, 0:1], None, ALU.mult
                                        ).then_inc(s_bias, 1)
                for i in (1, 2):
                    dve.wait_ge(s_bias, i)
                    nc.vector.scalar_tensor_tensor(bias_sum[i][:, :], bias_part[i][:, :], pick3[:, i:i + 1],
                                                   bias_sum[i - 1][:, :], ALU.mult, ALU.add).then_inc(s_bias, 1)
                for n, s in turns(dve, NODE_TILES):
                    normalise(n, s)
                    if reused(n):
                        scores(n - 2, s)
                scores(last - 1, 1)
                scores(last, 0)

            @block.tensor
            def _(pe):
                def gemm(n, s):
                    pe.wait_ge(s_xnT, n + 1)
                    if reused(n):
                        pe.wait_ge(s_row, n - 1)
                    nc.tensor.matmul(ps_h[s][:, :], ones3[:, :], bias_sum[2][:, :], start=True, stop=False)
                    for c in range(DC):
                        mm = nc.tensor.matmul(ps_h[s][:, :], xnT[:, s, c * P:(c + 1) * P], wt[:, c, :],
                                              start=False, stop=(c == DC - 1))
                    mm.then_inc(s_h, 1)

                def transpose(n, s):
                    pe.wait_ge(s_xn, n + 1)
                    if reused(n):
                        pe.wait_ge(s_xnT, n - 1)
                    for c in range(DC):
                        tr = nc.tensor.transpose(ps_t[s][:, c * P:(c + 1) * P], xn[:, s, c * P:(c + 1) * P],
                                                 keep["ident"][:, :])
                    tr.then_inc(s_tr, 1)

                pe.wait_ge(s_const, CONSTS)
                pe.wait_ge(s_set, 1)
                pe.wait_ge(s_bias, 3)
                for n, s in turns(pe, NODE_TILES):
                    transpose(n, s)
                    if reused(n, 1):
                        gemm(n - 1, 1 - s)
                gemm(last, 0)

            @block.scalar
            def _(act):
                def leaky(n, s):
                    act.wait_ge(s_h, n + 1)
                    if reused(n):
                        act.wait_ge(s_row, n - 1)
                    nc.scalar.activation(leak[:, s, :], ps_h[s][:, :], ACT.Copy, scale=SLOPE).then_inc(s_leak, 1)

                def sqrt(n, s):
                    act.wait_ge(s_ve, n + 1)
                    if reused(n):
                        act.wait_ge(s_rstd, n - 1)
                    nc.scalar.activation(std[:, s, :], var_eps[:, s, :], ACT.Sqrt).then_inc(s_std, 1)

                def keep_src(n, s):
                    act.wait_ge(s_esrc, n + 1)
                    nc.scalar.activation(keep["esrc"][:, bass.ds(n * HEADS, HEADS)], hrow[:, s, D:ROW], ACT.Copy
                                         ).then_inc(s_kept, 1)

                sqrt(0, 0)
                for n, s in turns(act, NODE_TILES):
                    act.wait_ge(s_tr, n + 1)
                    if reused(n):
                        act.wait_ge(s_h, n - 1)
                    nc.scalar.activation(xnT[:, s, :], ps_t[s][:, :], ACT.Copy).then_inc(s_xnT, 1)
                    if not (isinstance(n, int) and n == last):
                        sqrt(n + 1, 1 - s)
                    if reused(n):
                        keep_src(n - 2, s)
                    if reused(n, 1):
                        leaky(n - 1, 1 - s)
                leaky(last, 0)
                keep_src(last - 1, 1)
                keep_src(last, 0)


def attend_any(nc, top, banks, t, keep, branch_semaphores):
    with ExitStack() as ctx:
        def sb(name, shape, dt=F32):
            return ctx.enter_context(nc.sbuf_tensor(name, shape, dt))

        def sem(name):
            branch_semaphores.append(top.enter_context(nc.semaphore(name)))
            return branch_semaphores[-1]

        before = sb("before", [P, P])
        src_idx = sb("src_idx", [P, 1], I32)
        dst_idx = sb("dst_idx", [P, 1], I32)
        put_idx = sb("put_idx", [P, 1], I32)
        dcol = sb("dcol", [P, 1])
        dst_wide = sb("dst_wide", [P, P])
        e_wide = sb("e_wide", [P, HEADS, P])
        same = sb("same", [P, P])
        penalty = sb("penalty", [P, P])
        masked = sb("masked", [P, HEADS, P])
        earlier = sb("earlier", [P, P])
        n_earlier = sb("n_earlier", [P, 1])
        grow = sb("grow", [P, ROW])
        arow = sb("arow", [P, ROW])
        anew = sb("anew", [P, ROW])
        mrow = sb("mrow", [P, 2 * HEADS])
        mnew = sb("mnew", [P, 2 * HEADS])
        score = sb("score", [P, HEADS])
        e = sb("e", [P, HEADS])
        tile_max = sb("tile_max", [P, HEADS])
        diffs = sb("diffs", [P, 2 * HEADS])
        exps = sb("exps", [P, 2 * HEADS])
        coef = sb("coef", [P, HEADS])
        msg = sb("msg", [P, D])
        put_f = sb("put_f", [P, 1])
        src = keep["src"][:, :, :].rearrange("p g j -> p (g j)")
        dst = keep["dst"][:, :, :].rearrange("p g j -> p (g j)")
        dist = keep["dist"]
        wide_t = banks[0]
        e_t = [banks[1], banks[2]]
        sums, weights = banks[3], banks[4]

        s_load = sem("edges_loaded")
        s_src, s_dst, s_dc, s_put = sem("src_idx_set"), sem("dst_idx_set"), sem("dcol_set"), sem("put_idx_set")
        s_pool_on = sem("pool_went_on")
        s_g, s_a, s_m = sem("g_gathered"), sem("a_gathered"), sem("m_gathered")
        s_ap, s_mp = sem("a_put"), sem("m_put")
        names = "dst_wide dstT penalty e_wide eT masked mnew diffs exps msg sums anew".split()
        done = {k: sem("any_" + k) for k in names}
        chain = "same earlier n_earlier put_f score e tile_max coef".split()
        s_chain = sem("any_chain")
        s_scaled = sem("any_scaled")

        with nc.Block() as block:
            @block.sync
            def _(sp):
                sp.dma_start(before[:, :], t["before"]).then_inc(s_load, 16)

            @block.gpsimd
            def _(pool):
                def gather(out, table, idx, semaphore):
                    pool.indirect_dma_start(out=out[:, :], out_offset=None, in_=table[:, :],
                                            in_offset=bass.IndirectOffsetOnAxis(ap=idx[:, :], axis=0)
                                            ).then_inc(semaphore, 16)

                def scatter(table, row, semaphore):
                    pool.indirect_dma_start(out=table[:, :],
                                            out_offset=bass.IndirectOffsetOnAxis(ap=put_idx[:, :], axis=0),
                                            in_=row[:, :], in_offset=None, bounds_check=ROWS - 1,
                                            oob_is_err=False).then_inc(semaphore, 16)

                for n in edge_turns(pool):
                    wait_alone(pool, s_src, n + 1, s_pool_on)
                    gather(grow, t["h"], src_idx, s_g)
                    wait_alone(pool, s_dst, n + 1, s_pool_on)
                    gather(arow, t["agg"], dst_idx, s_a)
                    gather(mrow, t["maxima"], dst_idx, s_m)
                    pool.wait_ge(s_put, n + 1)
                    wait_alone(pool, done["anew"], 2 * (n + 1), s_pool_on)
                    scatter(t["agg"], anew, s_ap)
                    scatter(t["maxima"], mnew, s_mp)
                    pool.wait_ge(s_ap, 16 * (n + 1))
                    pool.wait_ge(s_mp, 16 * (n + 1))

            @block.vector
            def _(dve):
                dve.wait_ge(s_load, 16)

                def heads(ap):
                    return ap.rearrange("p (h d) -> p h d", h=HEADS)

                for n in edge_turns(dve):
                    def step(name, ins):
                        ins.then_inc(s_chain, 1)
                        dve.wait_ge(s_chain, n * len(chain) + chain.index(name) + 1)

                    if reused(n, 1):
                        dve.wait_ge(s_mp, 16 * n)
                        dve.wait_ge(s_ap, 16 * n)
                    nc.vector.tensor_copy(src_idx[:, :], src[:, bass.ds(n, 1)]).then_inc(s_src, 1)
                    nc.vector.tensor_copy(dst_idx[:, :], dst[:, bass.ds(n, 1)]).then_inc(s_dst, 1)
                    nc.vector.tensor_copy(dcol[:, :], dst[:, bass.ds(n, 1)]).then_inc(s_dc, 1)
                    dve.wait_ge(s_dc, n + 1)
                    nc.vector.tensor_copy(dst_wide[:, :], dcol[:, 0:1].to_broadcast([P, P])
                                          ).then_inc(done["dst_wide"], 1)
                    dve.wait_ge(done["dstT"], n + 1)
                    step("same", nc.vector.tensor_scalar(same[:, :], wide_t[:, 0:P], dcol[:, 0:1], None,
                                                         ALU.is_equal))
                    nc.vector.tensor_scalar(penalty[:, :], same[:, :], -1.0, -LOWEST, ALU.add,
                                            ALU.mult).then_inc(done["penalty"], 1)
                    step("earlier", nc.vector.tensor_tensor(earlier[:, :], same[:, :], before[:, :], ALU.mult))
                    step("n_earlier", nc.vector.tensor_reduce(n_earlier[:, :], earlier[:, :], AX, ALU.max))
                    step("put_f", nc.vector.scalar_tensor_tensor(put_f[:, :], n_earlier[:, :], float(FAR),
                                                                 dcol[:, :], ALU.mult, ALU.add))
                    nc.vector.tensor_copy(put_idx[:, :], put_f[:, :]).then_inc(s_put, 1)

                    dve.wait_ge(s_g, 16 * (n + 1))
                    dve.wait_ge(s_m, 16 * (n + 1))
                    step("score", nc.vector.tensor_tensor(score[:, :], grow[:, D:ROW], mrow[:, HEADS:2 * HEADS],
                                                          ALU.add))
                    step("e", nc.vector.scalar_tensor_tensor(e[:, :], score[:, :], SLOPE, score[:, :], ALU.mult,
                                                             ALU.max))
                    nc.vector.tensor_copy(e_wide[:, :, :], e[:, :].unsqueeze(2).to_broadcast([P, HEADS, P])
                                          ).then_inc(done["e_wide"], 1)
                    dve.wait_ge(done["eT"], n + 1)
                    dve.wait_ge(done["penalty"], n + 1)
                    half = HEADS // 2
                    for b in range(2):
                        last = nc.vector.tensor_tensor(
                            masked[:, b * half:(b + 1) * half, :],
                            e_t[b][:, :].rearrange("p (h c) -> p h c", h=half),
                            penalty[:, :].unsqueeze(1).to_broadcast([P, half, P]), ALU.add)
                        if b == 0:
                            last.then_inc(done["masked"], 1)
                    last.then_inc(done["masked"], 1)
                    dve.wait_ge(done["masked"], 2 * (n + 1))
                    step("tile_max", nc.vector.tensor_reduce(tile_max[:, :], masked[:, :, :], AX, ALU.max))
                    nc.vector.tensor_copy(mnew[:, HEADS:2 * HEADS], mrow[:, HEADS:2 * HEADS]
                                          ).then_inc(done["mnew"], 1)
                    nc.vector.tensor_tensor(mnew[:, 0:HEADS], mrow[:, 0:HEADS], tile_max[:, :], ALU.max
                                            ).then_inc(done["mnew"], 1)
                    dve.wait_ge(done["mnew"], 2 * (n + 1))
                    nc.vector.tensor_tensor(diffs[:, 0:HEADS], mrow[:, 0:HEADS], mnew[:, 0:HEADS],
                                            ALU.subtract).then_inc(done["diffs"], 1)
                    nc.vector.tensor_tensor(diffs[:, HEADS:2 * HEADS], e[:, :], mnew[:, 0:HEADS],
                                            ALU.subtract).then_inc(done["diffs"], 1)
                    dve.wait_ge(done["exps"], n + 1)
                    step("coef", nc.vector.tensor_tensor(
                        coef[:, :], exps[:, HEADS:2 * HEADS],
                        dist[:, bass.ds(n, 1), :].rearrange("p o h -> p (o h)"), ALU.mult))
                    nc.vector.tensor_tensor(heads(msg[:, :]), heads(grow[:, 0:D]),
                                            coef[:, :].unsqueeze(2).to_broadcast([P, HEADS, HD]), ALU.mult
                                            ).then_inc(done["msg"], 1)
                    dve.wait_ge(s_a, 16 * (n + 1))
                    nc.vector.tensor_tensor(heads(arow[:, 0:D]), heads(arow[:, 0:D]),
                                            exps[:, 0:HEADS].unsqueeze(2).to_broadcast([P, HEADS, HD]),
                                            ALU.mult).then_inc(s_scaled, 1)
                    nc.vector.tensor_tensor(arow[:, D:ROW], arow[:, D:ROW], exps[:, 0:HEADS],
                                            ALU.mult).then_inc(s_scaled, 1)
                    dve.wait_ge(s_scaled, 2 * (n + 1))
                    dve.wait_ge(done["sums"], n + 1)
                    nc.vector.tensor_tensor(anew[:, 0:D], arow[:, 0:D], sums[:, :], ALU.add
                                            ).then_inc(done["anew"], 1)
                    nc.vector.tensor_tensor(anew[:, D:ROW], arow[:, D:ROW], weights[:, 0:HEADS], ALU.add
                                            ).then_inc(done["anew"], 1)

            @block.scalar
            def _(act):
                for n in edge_turns(act):
                    act.wait_ge(done["diffs"], 2 * (n + 1))
                    nc.scalar.activation(exps[:, :], diffs[:, :], ACT.Exp).then_inc(done["exps"], 1)

            @block.tensor
            def _(pe):
                for n in edge_turns(pe):
                    pe.wait_ge(done["dst_wide"], n + 1)
                    nc.tensor.transpose(wide_t[:, 0:P], dst_wide[:, :], keep["ident"][:, :]
                                        ).then_inc(done["dstT"], 1)
                    pe.wait_ge(done["e_wide"], n + 1)
                    for h in range(HEADS):
                        k = h % (HEADS // 2)
                        last = nc.tensor.transpose(e_t[h // (HEADS // 2)][:, k * P:(k + 1) * P], e_wide[:, h, :],
                                                   keep["ident"][:, :])
                    last.then_inc(done["eT"], 1)
                    pe.wait_ge(done["msg"], n + 1)
                    nc.tensor.matmul(sums[:, :], same[:, :], msg[:, :], start=True, stop=True)
                    nc.tensor.matmul(weights[:, 0:HEADS], same[:, :], exps[:, HEADS:2 * HEADS], start=True,
                                     stop=True).then_inc(done["sums"], 1)


def prepare(nc, top, banks, t, keep):
    with ExitStack() as ctx:
        def sb(name, shape, dt=F32):
            return ctx.enter_context(nc.sbuf_tensor(name, shape, dt))

        def sem(name):
            return top.enter_context(nc.semaphore(name))

        group_dst = [P, GROUPS, GROUP]
        base_row = sb("base_row", [1, GROUPS])
        spread = sb("spread", [P, 2 * GROUPS + 2 * HEADS])
        reach = sb("reach", [P, 2 * GROUPS + 2 * HEADS])
        least = sb("least", [P, GROUPS + HEADS])
        over = sb("over", [P, GROUPS - 1])
        steps = sb("steps", [P, GROUPS - 1])
        width = sb("score_width", [P, HEADS])
        excess = sb("excess", [P, 4])
        raised = sb("raised", [P, NODE_TILES, HEADS])
        shifts = sb("shifts", [P, NODE_TILES + 1, 2 * HEADS])
        shifts3 = sb("shifts3", [P, NODE_TILES + 1, 3, 2 * HEADS], BF16)
        shifts_rest = sb("shifts_rest", [P, NODE_TILES + 1, 2 * HEADS])
        maxima = sb("maxima", [P, NODE_TILES + 1, 2 * HEADS])

        s_all, s_tab = sem("prep_reached"), sem("prep_tables_stored")
        s_bases = sem("bases_spread")
        names = "base dstf rel_max esrc_max negated steps base_int excess far shift ed_copies zero_rows".split()
        d = {k: sem("prep_" + k) for k in names}
        s_chain = sem("prep_chain")
        parts = {k: sem("shifts_" + k) for k in ("hi", "rest", "mid", "lo")}
        esrc = keep["esrc"][:, :].rearrange("p (n h) -> p h n", h=HEADS)
        edst = keep["edst"][:, :].rearrange("p (n h) -> p n h", h=HEADS)
        rel = keep["rel"][:, :].rearrange("p (g j) -> p g j", j=GROUP)

        with nc.Block() as block:
            @block.sync
            def _(sp):
                sp.wait_ge(d["ed_copies"], 2)
                sp.wait_ge(d["zero_rows"], 3)
                sp.dma_start(t["maxima"].rearrange("(n p) c -> p n c", p=P), maxima[:, :, :]).then_inc(s_tab, 16)
                sp.wait_ge(parts["lo"], 1)
                sp.dma_start(t["shifts"].rearrange("(n p) c -> p n c", p=P),
                             shifts3[:, :, :, :].rearrange("p n q c -> p n (q c)")).then_inc(s_tab, 16)
                sp.wait_ge(s_tab, 32)

            @block.gpsimd
            def _(pool):
                pool.wait_ge(d["base"], 1)
                nc.gpsimd.partition_broadcast(keep["bases"][:, :], base_row[:, :]).then_inc(s_bases, 1)
                pool.wait_ge(d["rel_max"], 1)
                pool.wait_ge(d["esrc_max"], 1)
                pool.wait_ge(d["negated"], 2)
                nc.gpsimd.partition_all_reduce(reach[:, :], spread[:, :], P, RMAX).then_inc(s_all, 1)

            @block.vector
            def _(dve):
                G2 = 2 * GROUPS

                steps_done = 0

                def step(ins):
                    nonlocal steps_done
                    steps_done += 1
                    ins.then_inc(s_chain, 1)
                    dve.wait_ge(s_chain, steps_done)

                nc.vector.tensor_copy(base_row[:, :], keep["dst"][0:1, :, 0]).then_inc(d["base"], 1)
                nc.vector.tensor_copy(rel, keep["dst"][:, :, :]).then_inc(d["dstf"], 1)
                nc.vector.memset(maxima[:, :, 0:HEADS], LOWEST).then_inc(d["zero_rows"], 1)
                nc.vector.memset(maxima[:, NODE_TILES, HEADS:], 0.0).then_inc(d["zero_rows"], 1)
                nc.vector.memset(shifts[:, NODE_TILES, :], 0.0).then_inc(d["zero_rows"], 1)
                nc.vector.tensor_copy(maxima[:, 0:NODE_TILES, HEADS:], edst).then_inc(d["ed_copies"], 1)
                nc.vector.tensor_copy(shifts[:, 0:NODE_TILES, 0:HEADS], edst).then_inc(d["ed_copies"], 1)
                nc.vector.tensor_reduce(spread[:, G2:G2 + HEADS], esrc, AX, ALU.max).then_inc(d["esrc_max"], 1)
                step(nc.vector.tensor_reduce(least[:, GROUPS:], esrc, AX, ALU.min))
                nc.vector.tensor_scalar_mul(spread[:, G2 + HEADS:], least[:, GROUPS:], -1.0
                                            ).then_inc(d["negated"], 1)
                dve.wait_ge(s_bases, 1)
                dve.wait_ge(d["dstf"], 1)
                step(nc.vector.tensor_tensor(rel, rel, keep["bases"][:, :].unsqueeze(2)
                                                    .to_broadcast(group_dst), ALU.subtract))
                nc.vector.tensor_reduce(spread[:, 0:GROUPS], rel, AX, ALU.max).then_inc(d["rel_max"], 1)
                step(nc.vector.tensor_reduce(least[:, 0:GROUPS], rel, AX, ALU.min))
                nc.vector.tensor_scalar_mul(spread[:, GROUPS:G2], least[:, 0:GROUPS], -1.0
                                            ).then_inc(d["negated"], 1)
                nc.vector.tensor_copy(keep["bases_int"][:, :], base_row[:, :]).then_inc(d["base_int"], 1)
                nc.vector.tensor_tensor(steps[:, :], keep["bases"][:, 1:], keep["bases"][:, 0:GROUPS - 1],
                                        ALU.subtract).then_inc(d["steps"], 1)
                dve.wait_ge(s_all, 1)
                dve.wait_ge(d["steps"], 1)
                step(nc.vector.tensor_tensor(over[:, :], reach[:, 0:GROUPS - 1], steps[:, :], ALU.subtract))
                step(nc.vector.tensor_tensor(
                    raised[:, :, :], edst, reach[:, G2:G2 + HEADS].unsqueeze(1)
                    .to_broadcast([P, NODE_TILES, HEADS]), ALU.add))
                nc.vector.scalar_tensor_tensor(shifts[:, 0:NODE_TILES, HEADS:], raised[:, :, :], SLOPE,
                                               raised[:, :, :], ALU.mult, ALU.max).then_inc(d["shift"], 1)
                dve.wait_ge(d["shift"], 1)
                dve.wait_ge(d["ed_copies"], 2)
                dve.wait_ge(d["zero_rows"], 3)
                split3(nc.vector, dve.wait_ge, parts, shifts[:, :, :], shifts3[:, :, 0, :], shifts3[:, :, 1, :],
                       shifts3[:, :, 2, :], shifts_rest[:, :, :])
                step(nc.vector.tensor_tensor(width[:, :], reach[:, G2:G2 + HEADS],
                                                      reach[:, G2 + HEADS:], ALU.add))
                measures = (over[:, :], reach[:, 0:GROUPS], reach[:, GROUPS:G2], width[:, :])
                for i, measure in enumerate(measures):
                    nc.vector.tensor_reduce(excess[:, i:i + 1], measure, AX, ALU.max).then_inc(d["excess"], 1)
                dve.wait_ge(d["excess"], len(measures))
                for i, limit in enumerate((0.0, float(P - 1), 0.0, SAFE_WIDTH)):
                    nc.vector.tensor_scalar(keep["excess"][:, i:i + 1], excess[:, i:i + 1], limit, None, ALU.is_gt
                                            ).then_inc(d["far"], 1)
                dve.wait_ge(d["far"], len(measures))
                step(nc.vector.tensor_reduce(keep["general"][:, :], keep["excess"][:, :], AX, ALU.max))


def attend_windows(nc, top, banks, t, keep, branch_semaphores):
    with ExitStack() as ctx:
        def sb(name, shape, dt=F32):
            return ctx.enter_context(nc.sbuf_tensor(name, shape, dt))

        def sem(name):
            return branch_semaphores.pop() if branch_semaphores else top.enter_context(nc.semaphore(name))

        S3 = 3
        ident16 = sb("ident16", [P, P], BF16)
        node_no = sb("node_no", [P, P])
        src_idx = sb("w_src_idx", [P, S3, GROUP], I32)
        gathered = sb("gathered", [P, S3, GROUP, ROW])
        member16 = sb("member16", [P, S3, GROUP, P], BF16)
        member = sb("member", [P, S3, GROUP, P])
        memberT = sb("memberT", [P, S3, GROUP, P], BF16)
        window = sb("window", [P, S3, 6 * HEADS], BF16)
        at_dst = sb("at_dst", [P, GROUP, 2 * HEADS])
        score = sb("w_score", [P, GROUP, HEADS])
        leaky = sb("w_leaky", [P, GROUP, HEADS])
        diff = sb("w_diff", [P, S3, GROUP, HEADS])
        ex = sb("w_ex", [P, S3, GROUP, HEADS])
        ex3 = sb("w_ex3", [P, S3, GROUP, 3, HEADS], BF16)
        ex_rest = sb("w_ex_rest", [P, GROUP, HEADS])
        coef = sb("w_coef", [P, GROUP, HEADS])
        msg = sb("w_msg", [P, S3, GROUP, D])
        summed = sb("summed", [P, S3, ROW])
        carry = sb("w_carry", [1, ROW])
        sums = banks[0:3]
        weights = banks[3]
        member_t = banks[4][:, :].bitcast(BF16)
        edge_dst = banks[6]

        s_no = sem("node_no_loaded")
        s_pool_on = sem("w_pool_went_on")
        s_i16 = sem("ident16_set")
        s_idx = sem("w_src_idx_set")
        s_g = [sem(f"w_gathered{i}") for i in range(S3)]
        s_put = [sem(f"w_stored{i}") for i in range(S3)]
        s_carry = sem("w_carry_copied")
        s_win = [sem(f"w_window_loaded{i}") for i in range(S3)]
        names = ("member16 member member_t memberT edge_dst at_dst score leaky diff ex ex_hi ex_rest ex_mid ex_lo "
                 "coef msg sums evac evac_w carried").split()
        d = {k: sem("w_" + k) for k in names}

        def filled(g, slot, per):
            return (g - slot) * (per // S3) + per

        def rounds(eng, drain):
            for u in range(3 * S3):
                yield u, u % S3
            with eng.Fori(3, GROUPS // S3) as i:
                for s in range(S3):
                    yield i * S3 + s, s
            for u in range(GROUPS // S3 * S3, GROUPS + drain):
                yield u, u % S3

        def stage(u, slot, lag, do):
            if isinstance(u, int) and not 0 <= u - lag < GROUPS:
                return
            do(u - lag, (slot - lag) % S3)

        def old(g):
            return reused(g, S3)

        with nc.Block() as block:
            @block.sync
            def _(sp):
                sp.dma_start(node_no[:, :], t["node_no"]).then_inc(s_no, 16)

                def load_window(g, s):
                    base = sp.value_load(keep["bases_int"][0:1, bass.ds(g, 1)], min_val=0, max_val=NODES)
                    if old(g):
                        sp.wait_ge(d["edge_dst"], g - 2)
                    sp.dma_start(window[:, s, :], t["shifts"][bass.ds(base, P), :]).then_inc(s_win[s], 48)

                def store(g, s):
                    base = sp.value_load(keep["bases_int"][0:1, bass.ds(g, 1)], min_val=0, max_val=NODES)
                    if isinstance(g, int) and g == 0:
                        sp.wait_ge(d["evac"], 1)
                        sp.wait_ge(d["evac_w"], 1)
                    else:
                        sp.wait_ge(d["carried"], g)
                    sp.dma_start(t["agg"][bass.ds(base, P), :], summed[:, s, :]).then_inc(s_put[s], 48)

                def load_carry(g, s):
                    if isinstance(g, int) and g == 0:
                        return
                    base = sp.value_load(keep["bases_int"][0:1, bass.ds(g, 1)], min_val=0, max_val=NODES)
                    if reused(g):
                        sp.wait_ge(d["carried"], g - 1)
                    before = (s - 1) % S3
                    sp.wait_ge(s_put[before], filled(g - 1, before, 48))
                    sp.dma_start(carry[:, :], t["agg"][bass.ds(base, 1), :]).then_inc(s_carry, 16)

                for u, slot in rounds(sp, 4):
                    stage(u, slot, 0, load_window)
                    stage(u, slot, 4, load_carry)
                    stage(u, slot, 4, store)
                for g in range(GROUPS - S3, GROUPS):
                    sp.wait_ge(s_put[g % S3], filled(g, g % S3, 48))

            @block.gpsimd
            def _(pool):
                for g, s in rounds(pool, 0):
                    wait_alone(pool, s_idx, g + 1, s_pool_on)
                    if old(g):
                        wait_alone(pool, d["msg"], g - 2, s_pool_on)
                    for j in range(GROUP):
                        pool.indirect_dma_start(
                            out=gathered[:, s, j, :], out_offset=None, in_=t["h"][:, :],
                            in_offset=bass.IndirectOffsetOnAxis(ap=src_idx[:, s, j:j + 1], axis=0)
                        ).then_inc(s_g[s], 48)

            @block.vector
            def _(dve):
                def make_member(g, s):
                    if old(g):
                        dve.wait_ge(d["sums"], g - 2)
                    nc.vector.tensor_tensor(
                        member16[:, s, :, :], node_no[:, :].unsqueeze(1).to_broadcast([P, GROUP, P]),
                        keep["rel"][:, bass.ds(g * GROUP, GROUP)].unsqueeze(2).to_broadcast([P, GROUP, P]),
                        ALU.is_equal).then_inc(d["member16"], 1)

                def scores(g, s):
                    dve.wait_ge(s_g[s], filled(g, s, 48 * GROUP))
                    dve.wait_ge(d["edge_dst"], g + 1)
                    nc.vector.tensor_reduce(
                        at_dst[:, :, :], edge_dst[:, 0:GROUP * 6 * HEADS]
                        .rearrange("p (j q c) -> p j c q", j=GROUP, q=3), AX, ALU.add).then_inc(d["at_dst"], 1)
                    dve.wait_ge(d["at_dst"], g + 1)
                    nc.vector.tensor_tensor(score[:, :, :], gathered[:, s, :, D:ROW], at_dst[:, :, 0:HEADS],
                                            ALU.add).then_inc(d["score"], 1)
                    dve.wait_ge(d["score"], g + 1)
                    nc.vector.scalar_tensor_tensor(leaky[:, :, :], score[:, :, :], SLOPE, score[:, :, :], ALU.mult,
                                                   ALU.max).then_inc(d["leaky"], 1)
                    dve.wait_ge(d["leaky"], g + 1)
                    if old(g):
                        dve.wait_ge(d["ex"], g - 2)
                    nc.vector.tensor_tensor(diff[:, s, :, :], leaky[:, :, :], at_dst[:, :, HEADS:], ALU.subtract
                                            ).then_inc(d["diff"], 1)

                def messages(g, s):
                    dve.wait_ge(d["ex"], g + 1)
                    nc.vector.tensor_tensor(coef[:, :, :], ex[:, s, :, :],
                                            keep["dist"][:, bass.ds(g * GROUP, GROUP), :], ALU.mult
                                            ).then_inc(d["coef"], 1)
                    dve.wait_ge(d["coef"], g + 1)
                    if old(g):
                        dve.wait_ge(d["sums"], g - 2)
                    shape = [P, GROUP, HEADS, HD]
                    nc.vector.tensor_tensor(
                        msg[:, s, :, :].rearrange("p j (h d) -> p j h d", h=HEADS),
                        gathered[:, s, :, 0:D].rearrange("p j (h d) -> p j h d", h=HEADS),
                        coef[:, :, :].unsqueeze(3).to_broadcast(shape), ALU.mult).then_inc(d["msg"], 1)

                def weights_parts(g, s):
                    dve.wait_ge(d["ex_hi"], g + 1)
                    nc.vector.tensor_tensor(ex_rest[:, :, :], ex[:, s, :, :], ex3[:, s, :, 0, :], ALU.subtract
                                            ).then_inc(d["ex_rest"], 1)

                def weights_last_part(g, s):
                    dve.wait_ge(d["ex_mid"], g + 1)
                    nc.vector.tensor_tensor(ex3[:, s, :, 2, :], ex_rest[:, :, :], ex3[:, s, :, 1, :], ALU.subtract
                                            ).then_inc(d["ex_lo"], 1)

                def evacuate_weights(g, s):
                    dve.wait_ge(d["sums"], g + 1)
                    if old(g):
                        dve.wait_ge(s_put[s], filled(g - S3, s, 48))
                    nc.vector.tensor_reduce(summed[:, s, D:ROW], weights[:, 0:3 * HEADS]
                                            .rearrange("p (q h) -> p h q", q=3), AX, ALU.add
                                            ).then_inc(d["evac_w"], 1)

                def carry_in(g, s):
                    if isinstance(g, int) and g == 0:
                        return
                    dve.wait_ge(d["evac"], g + 1)
                    dve.wait_ge(d["evac_w"], g + 1)
                    dve.wait_ge(s_carry, 16 * g)
                    nc.vector.tensor_tensor(summed[0:1, s, :], summed[0:1, s, :], carry[:, :], ALU.add
                                            ).then_inc(d["carried"], 1)

                dve.wait_ge(s_no, 16)
                for u, slot in rounds(dve, 4):
                    stage(u, slot, 4, carry_in)
                    stage(u, slot, 1, scores)
                    stage(u, slot, 0, make_member)
                    stage(u, slot, 1, weights_parts)
                    stage(u, slot, 1, messages)
                    stage(u, slot, 1, weights_last_part)
                    stage(u, slot, 3, evacuate_weights)

            @block.tensor
            def _(pe):
                def at_edges(g, s):
                    pe.wait_ge(d["memberT"], g + 1)
                    pe.wait_ge(s_win[s], filled(g, s, 48))
                    if not (isinstance(g, int) and g == 0):
                        pe.wait_ge(d["at_dst"], g)
                    for j in range(GROUP):
                        at = j * 6 * HEADS
                        last = nc.tensor.matmul(edge_dst[:, at:at + 6 * HEADS], memberT[:, s, j, :],
                                                window[:, s, :], start=True, stop=True)
                    last.then_inc(d["edge_dst"], 1)

                def transpose(g, s):
                    pe.wait_ge(d["member16"], g + 1)
                    if not (isinstance(g, int) and g == 0):
                        pe.wait_ge(d["memberT"], g)
                    for j in range(GROUP):
                        last = nc.tensor.transpose(member_t[:, j * P:(j + 1) * P], member16[:, s, j, :],
                                                   ident16[:, :])
                    last.then_inc(d["member_t"], 1)

                def add_up(g, s, part):
                    if part == 0:
                        pe.wait_ge(d["msg"], g + 1)
                        pe.wait_ge(d["member"], g + 1)
                        if old(g):
                            pe.wait_ge(d["evac"], g - 2)
                    half = GROUP // 2
                    for j in range(half) if part == 0 else range(half, GROUP):
                        first, final = j == 0, j == GROUP - 1
                        nc.tensor.matmul(sums[s][:, :], member[:, s, j, :], msg[:, s, j, :], start=first,
                                         stop=final)
                    if part == 1:
                        if not (isinstance(g, int) and g == 0):
                            pe.wait_ge(d["evac_w"], g)
                        pe.wait_ge(d["ex_lo"], g + 1)
                        for j in range(GROUP):
                            last = nc.tensor.matmul(weights[:, 0:3 * HEADS], member16[:, s, j, :],
                                                    ex3[:, s, j, :, :].rearrange("p q h -> p (q h)"),
                                                    start=(j == 0), stop=(j == GROUP - 1))
                        last.then_inc(d["sums"], 1)

                pe.wait_ge(s_i16, 1)
                for u, slot in rounds(pe, 2):
                    stage(u, slot, 1, at_edges)
                    stage(u, slot, 2, lambda g, s: add_up(g, s, 0))
                    stage(u, slot, 0, transpose)
                    stage(u, slot, 2, lambda g, s: add_up(g, s, 1))

            @block.scalar
            def _(act):
                def copy(out, in_):
                    return nc.scalar.activation(out, in_, ACT.Copy)

                def set_src(g, s):
                    if old(g):
                        act.wait_ge(s_g[s], filled(g - S3, s, 48 * GROUP))
                    copy(src_idx[:, s, :], keep["src"][:, bass.ds(g, 1), :].rearrange("p o j -> p (o j)")
                         ).then_inc(s_idx, 1)

                def exps(g, s):
                    act.wait_ge(d["diff"], g + 1)
                    if old(g):
                        act.wait_ge(d["sums"], g - 2)
                    nc.scalar.activation(ex[:, s, :, :], diff[:, s, :, :], ACT.Exp).then_inc(d["ex"], 1)
                    act.wait_ge(d["ex"], g + 1)
                    copy(ex3[:, s, :, 0, :], ex[:, s, :, :]).then_inc(d["ex_hi"], 1)

                def exps_middle(g, s):
                    act.wait_ge(d["ex_rest"], g + 1)
                    copy(ex3[:, s, :, 1, :], ex_rest[:, :, :]).then_inc(d["ex_mid"], 1)

                def widen_member(g, s):
                    act.wait_ge(d["member16"], g + 1)
                    if old(g):
                        act.wait_ge(d["sums"], g - 2)
                    copy(member[:, s, :, :], member16[:, s, :, :]).then_inc(d["member"], 1)

                def turn_member(g, s):
                    act.wait_ge(d["member_t"], g + 1)
                    if old(g):
                        act.wait_ge(d["edge_dst"], g - 2)
                    copy(memberT[:, s, :, :], member_t[:, 0:GROUP * P].rearrange("p (j c) -> p j c", j=GROUP)
                         ).then_inc(d["memberT"], 1)

                def evacuate(g, s):
                    act.wait_ge(d["sums"], g + 1)
                    if old(g):
                        act.wait_ge(s_put[s], filled(g - S3, s, 48))
                    copy(summed[:, s, 0:D], sums[s][:, :]).then_inc(d["evac"], 1)

                copy(ident16[:, :], keep["ident"][:, :]).then_inc(s_i16, 1)
                set_src(0, 0)
                for u, slot in rounds(act, 3):
                    stage(u, slot, -1, set_src)
                    stage(u, slot, 1, exps)
                    stage(u, slot, 0, widen_member)
                    stage(u, slot, 1, exps_middle)
                    stage(u, slot, 0, turn_member)
                    stage(u, slot, 3, evacuate)


def finish(nc, top, banks, t, keep):
    with ExitStack() as ctx:
        def sb(name, shape, dt=F32):
            return ctx.enter_context(nc.sbuf_tensor(name, shape, dt))

        def sem(name):
            return top.enter_context(nc.semaphore(name))

        C = CHUNK
        w1 = sb("w1", [PAIRS, 5, P])
        w1_part = [sb(f"w1_part{i}", [PAIRS, 5, P], BF16) for i in range(3)]
        w1_rest = sb("w1_rest", [PAIRS, 5, P])
        w1_sum = [sb(f"w1_sum{i}", [PAIRS, 5, P], BF16) for i in range(3)]
        w1_pick = sb("w1_pick", [PAIRS, 3])
        w2 = sb("w2", [P, 13, P])
        w3 = sb("w3", [P, 5, 8])
        b2 = sb("b2", [P, 5])
        b3 = sb("b3", [P, 8])
        countdown = sb("countdown", [P, 64])
        digits = sb("digits", [P, 2, 16])
        x = sb("x_in", [P, 2, C, D])
        agg = sb("agg_in", [P, 2, C, ROW])
        y = sb("y", [P, 2, C, D])
        res = sb("res", [P, 2, C, D])
        wsum = sb("wsum", [P, C, HEADS])
        rsum = sb("rsum", [P, C, HEADS])
        stats = sb("fstats", [P, C, 6])
        mean_var = sb("fmean_var", [P, C, 2])
        var_eps = sb("fvar_eps", [P, C])
        std = sb("fstd", [P, C])
        rstd = sb("frstd", [P, C])
        hits = sb("hits", [P, C, 64])
        best = sb("best", [P, C, 4])
        first = sb("first", [P, C, 4])
        feats = sb("feats", [P, 2, C, PAIRS], BF16)
        ops_rest = sb("ops_rest", [P, C, 2])
        ident16 = sb("fident16", [P, P], BF16)
        flags = sb("flags", [P, C, 3])
        both = sb("both", [P, 2, C, 2])
        picks = sb("picks", [P, 2, C, 2])
        active = sb("active", [P, 2, C])
        active2 = sb("active2", [P, 2, C])
        featsT = sb("featsT", [PAIRS, C * P], BF16)
        h1 = sb("h1", [P, 5, C * P])
        h2 = sb("h2", [P, 5, C * P])
        v3 = sb("v3", [P, C, 8])
        added = sb("added", [P, C, 3])
        subbed = sb("subbed", [P, C, 3])
        value = sb("value", [P, C, 3])
        clipped = sb("clipped", [P, C, 3])
        shifted = sb("shifted", [P, C, 3])
        rounded = sb("rounded", [P, C, 3])
        hot = sb("hot", [P, C, 2, 16])
        carry = sb("carry", [P, C])
        feats_t = banks[0][:, :].bitcast(BF16)
        layer = banks[1:7]
        y3 = banks[7]

        s_dve_on, s_sp_on, s_pe_on = sem("fin_dve_went_on"), sem("fin_sp_went_on"), sem("fin_pe_went_on")
        s_w = sem("mlp_weights_loaded")
        s_ones = sem("feats_ones_set")
        s_in = [sem("chunk_loaded0"), sem("chunk_loaded1")]
        s_out = [sem("out_stored0"), sem("out_stored1")]
        parts = {k: sem("w1_" + k) for k in ("hi", "rest", "mid", "lo")}
        s_w1, s_i16 = sem("w1_split"), sem("fin_ident16_set")
        per_chunk = ("wsum rsum x1 var_eps std rstd res best first ops_hi ops_rest ops_mid ops_rest2 ops_lo "
                     "feats_nibbles flags both m_add all "
                     "m_sub active active2 feats_t featsT mm h1 h2 y3 v3 added subbed value clipped shifted "
                     "rounded carry carried").split()
        per_tile = "scaled stats mean_var y hits hot placed".split()
        d = {k: sem("fin_" + k) for k in per_chunk + per_tile}

        def chunks(eng):
            for c in range(4):
                yield c, c % 2, C
            with eng.Fori(2, CHUNKS // 2) as i:
                yield 2 * i, 0, C
                yield 2 * i + 1, 1, C
            yield CHUNKS, 0, NODE_TILES - CHUNKS * C

        LAST = NODE_TILES - CHUNKS * C
        ORDER1 = (4, 0, 1, 2, 3)

        def is_last(c):
            return isinstance(c, int) and c == CHUNKS

        with nc.Block() as block:
            @block.sync
            def _(sp):
                for name, tile in (("w1", w1), ("w1_pick", w1_pick), ("w2", w2), ("w3", w3), ("b2", b2), ("b3", b3),
                                   ("countdown", countdown), ("digits", digits)):
                    whole = tile[:, :, :] if len(tile.shape) == 3 else tile[:, :]
                    sp.dma_start(whole, t[name]).then_inc(s_w, 16)

                def load(c, s, k):
                    if reused(c):
                        wait_alone(sp, d["res"], c - 1, s_sp_on)
                    rows = bass.ds(c * (C * P), k * P)
                    sp.dma_start(x[:, s, 0:k, :], t["x"][rows, :].rearrange("(k p) n -> p k n", p=P)
                                 ).then_inc(s_in[s], 16)
                    sp.dma_start(agg[:, s, 0:k, :], t["agg"][rows, :].rearrange("(k p) n -> p k n", p=P)
                                 ).then_inc(s_in[s], 16)

                def store(c, s, k):
                    wait_alone(sp, d["placed"], c * C + k, s_sp_on)
                    wait_alone(sp, d["carried"], c + 1, s_sp_on)
                    if k == C:
                        sp.dma_start(t["out"][bass.ds(c * (C * P), C * P), :].rearrange("(k p) n -> p k n", p=P),
                                     res[:, s, :, :]).then_inc(s_out[s], 16)
                    else:
                        rows = N - CHUNKS * C * P
                        sp.dma_start(t["out"][N - rows:N, :], res[0:rows, s, 0, :]).then_inc(s_out[s], 16)

                for c, s, k in chunks(sp):
                    load(c, s, k)
                    if reused(c, 3):
                        store(c - 3, 1 - s, C)
                store(CHUNKS - 2, 0, C)
                store(CHUNKS - 1, 1, C)
                store(CHUNKS, 0, NODE_TILES - CHUNKS * C)
                sp.wait_ge(s_out[0], dma_count(CHUNKS, 0))
                sp.wait_ge(s_out[1], dma_count(CHUNKS - 1, 1))

            @block.gpsimd
            def _(pool):
                def choose(c, s, k):
                    def need(name):
                        pool.wait_ge(d[name], c + 1)

                    need("flags")
                    mark, add, sub = (flags[:, 0:k, i] for i in range(3))
                    nc.gpsimd.tensor_tensor(picks[:, s, 0:k, 0], mark, add, ALU.mult).then_inc(d["m_add"], 1)
                    nc.gpsimd.tensor_tensor(both[:, s, 0:k, 0], mark, sub, ALU.mult).then_inc(d["both"], 1)
                    need("both")
                    nc.gpsimd.tensor_tensor(both[:, s, 0:k, 1], both[:, s, 0:k, 0], add, ALU.mult
                                            ).then_inc(d["all"], 1)
                    need("all")
                    nc.gpsimd.tensor_tensor(picks[:, s, 0:k, 1], both[:, s, 0:k, 0], both[:, s, 0:k, 1],
                                            ALU.subtract).then_inc(d["m_sub"], 1)
                    need("m_sub")
                    need("m_add")
                    nc.gpsimd.tensor_tensor(active[:, s, 0:k], picks[:, s, 0:k, 0], picks[:, s, 0:k, 1], ALU.add
                                            ).then_inc(d["active"], 1)
                    need("active")
                    nc.gpsimd.tensor_tensor(active2[:, s, 0:k], active[:, s, 0:k], active[:, s, 0:k], ALU.add).then_inc(d["active2"], 1)

                for c, s, k in chunks(pool):
                    pool.wait_ge(d["y"], c * C + k)
                    if reused(c):
                        pool.wait_ge(s_out[s], dma_count(c - 2, s))
                    nc.gpsimd.tensor_tensor(res[:, s, 0:k, :], x[:, s, 0:k, :], y[:, s, 0:k, :], ALU.add
                                            ).then_inc(d["res"], 1)
                    choose(c, s, k)

            @block.scalar
            def _(act):
                def sqrt(c, k):
                    act.wait_ge(d["var_eps"], c + 1)
                    nc.scalar.activation(std[:, 0:k], var_eps[:, 0:k], ACT.Sqrt).then_inc(d["std"], 1)

                def features(c, k):
                    w = k * P
                    act.wait_ge(d["feats_t"], c + 1)
                    if reused(c, 1):
                        act.wait_ge(d["mm"], 10 * (c - 1) + 5)
                    nc.scalar.activation(featsT[:, 0:w], feats_t[0:PAIRS, 0:w], ACT.Copy).then_inc(d["featsT"], 1)

                def relu1(c, k):
                    w = k * P
                    for i, g in enumerate(ORDER1):
                        act.wait_ge(d["mm"], 10 * c + i + 1)
                        nc.scalar.activation(h1[:, g, 0:w], layer[g][:, 0:w], ACT.Relu).then_inc(d["h1"], 1)

                def relu2(c, k, groups):
                    w = k * P
                    for g in groups:
                        act.wait_ge(d["mm"], 10 * c + 5 + g + 1)
                        if reused(c, 1):
                            act.wait_ge(d["y3"], c)
                        nc.scalar.activation(h2[:, g, 0:w], layer[(5 + g) % 6][:, 0:w], ACT.Relu,
                                             bias=b2[:, g:g + 1]).then_inc(d["h2"], 1)

                act.wait_ge(s_w, 8 * 16)
                nc.scalar.activation(ident16[:, :], keep["ident"][:, :], ACT.Copy).then_inc(s_i16, 1)
                sqrt(0, C)
                features(0, C)
                for c, s, k in chunks(act):
                    relu1(c, k)
                    if not is_last(c):
                        if isinstance(c, int) and c == CHUNKS - 1:
                            sqrt(c + 1, LAST)
                        else:
                            sqrt(c + 1, C)
                    relu2(c, k, (0, 1, 2))
                    if not is_last(c):
                        features(c + 1, LAST if isinstance(c, int) and c == CHUNKS - 1 else C)
                    relu2(c, k, (3, 4))

            @block.tensor
            def _(pe):
                def transpose(c, s, k):
                    for name in ("ops_hi", "ops_mid", "ops_lo"):
                        pe.wait_ge(d[name], c + 1)
                    if reused(c, 1):
                        pe.wait_ge(d["featsT"], c)
                    wait_alone(pe, d["feats_nibbles"], c + 1, s_pe_on)
                    for j in range(k):
                        last = nc.tensor.transpose(feats_t[0:PAIRS, j * P:(j + 1) * P], feats[:, s, j, :],
                                                   ident16[:, :])
                    last.then_inc(d["feats_t"], 1)

                def layer1(c, k):
                    w = k * P
                    pe.wait_ge(d["featsT"], c + 1)
                    for g in ORDER1:
                        if reused(c, 1) and g < 4:
                            pe.wait_ge(d["h2"], 5 * (c - 1) + g + 2)
                        nc.tensor.matmul(layer[g][:, 0:w], w1_sum[2][:, g, :], featsT[:, 0:w], start=True,
                                         stop=True).then_inc(d["mm"], 1)

                def layer2(c, k, groups):
                    w = k * P
                    for g in groups:
                        pe.wait_ge(d["h1"], 5 * c + min(g + 2, 5))
                        bank = layer[(5 + g) % 6]
                        if g < 4:
                            pairs = ((g, g), (4 + g, 4))
                        else:
                            pairs = tuple((8 + i, i) for i in range(5))
                        for i, (weights, units) in enumerate(pairs):
                            last = nc.tensor.matmul(bank[:, 0:w], w2[:, weights, :], h1[:, units, 0:w],
                                                    start=(i == 0), stop=(i == len(pairs) - 1))
                        last.then_inc(d["mm"], 1)

                def layer3(c, k, tiles):
                    if tiles[0] == 0:
                        pe.wait_ge(d["h2"], 5 * (c + 1))
                        if reused(c, 1):
                            pe.wait_ge(d["v3"], c)
                    for j in tiles:
                        for g in range(5):
                            last = nc.tensor.matmul(y3[:, 8 * j:8 * j + 8], h2[:, g, j * P:(j + 1) * P],
                                                    w3[:, g, :], start=(g == 0), stop=(g == 4))
                    if tiles[-1] == k - 1:
                        last.then_inc(d["y3"], 1)

                pe.wait_ge(s_w, 8 * 16)
                pe.wait_ge(s_ones, 2)
                pe.wait_ge(s_i16, 1)
                pe.wait_ge(s_w1, 3)
                transpose(0, 0, C)
                for c, s, k in chunks(pe):
                    layer1(c, k)
                    if reused(c, 1):
                        layer3(c - 1, C, (0, 1))
                    layer2(c, k, (0,))
                    if reused(c, 1):
                        layer3(c - 1, C, (2,))
                    layer2(c, k, (1,))
                    if reused(c, 1):
                        layer3(c - 1, C, (3,))
                    layer2(c, k, (2,))
                    if not is_last(c):
                        transpose(c + 1, 1 - s, LAST if isinstance(c, int) and c == CHUNKS - 1 else C)
                    layer2(c, k, (3, 4))
                layer3(CHUNKS, LAST, range(LAST))

            @block.vector
            def _(dve):
                def front(c, s, k):
                    def need(name):
                        dve.wait_ge(d[name], c + 1)

                    def need_tiles(name):
                        dve.wait_ge(d[name], c * C + k)

                    loaded = 2 * dma_count(c, s) if isinstance(c, int) else (c - s) * 16 + 32
                    dve.wait_ge(s_in[s], loaded)
                    xk, ak = x[:, s, 0:k, :], agg[:, s, 0:k, :]
                    nc.vector.tensor_scalar_max(wsum[:, 0:k, :], ak[:, :, D:ROW], TINY).then_inc(d["wsum"], 1)
                    need("wsum")
                    nc.vector.reciprocal(rsum[:, 0:k, :], wsum[:, 0:k, :]).then_inc(d["rsum"], 1)
                    need("rsum")
                    for j in range(k):
                        heads = agg[:, s, j, 0:D].rearrange("p (h d) -> p h d", h=HEADS)
                        nc.vector.tensor_tensor(heads, heads, rsum[:, j, :].unsqueeze(2)
                                                .to_broadcast([P, HEADS, HD]), ALU.mult).then_inc(d["scaled"], 1)
                    need_tiles("scaled")
                    nc.vector.tensor_tensor(xk, xk, ak[:, :, 0:D], ALU.add).then_inc(d["x1"], 1)
                    need("x1")
                    for j in range(k):
                        nc.vector.bn_stats(stats[:, j, :], x[:, s, j, :]).then_inc(d["stats"], 1)
                    wait_alone(dve, d["stats"], c * C + k, s_dve_on)
                    for j in range(k):
                        nc.vector.bn_aggr(mean_var[:, j, :], stats[:, j, :]).then_inc(d["mean_var"], 1)
                    need_tiles("mean_var")
                    nc.vector.tensor_scalar_add(var_eps[:, 0:k], mean_var[:, 0:k, 1], EPS).then_inc(d["var_eps"], 1)
                    need("std")
                    nc.vector.reciprocal(rstd[:, 0:k], std[:, 0:k]).then_inc(d["rstd"], 1)
                    need("rstd")
                    if reused(c):
                        dve.wait_ge(d["res"], c - 1)
                    for j in range(k):
                        nc.vector.tensor_scalar(y[:, s, j, :], x[:, s, j, :], mean_var[:, j, 0:1], rstd[:, j:j + 1],
                                                ALU.subtract, ALU.mult).then_inc(d["y"], 1)
                    need_tiles("y")
                    if reused(c):
                        dve.wait_ge(d["feats_t"], c - 1)
                    def ops(part):
                        return feats[:, s, 0:k, OPS_AT:].rearrange("p k (i w o) -> p k i w o", i=3, w=3)[:, :, part]

                    def spread(in_):
                        return in_.unsqueeze(2).to_broadcast([P, k, 3, 2])

                    codes = y[:, s, 0:k, X_OP_ADD:X_OP_SUB + 1]
                    nc.vector.tensor_copy(ops(0), spread(codes)).then_inc(d["ops_hi"], 1)
                    need("ops_hi")
                    nc.vector.tensor_tensor(ops_rest[:, 0:k, :], codes, ops(0)[:, :, 0, :], ALU.subtract
                                            ).then_inc(d["ops_rest"], 1)
                    need("ops_rest")
                    nc.vector.tensor_copy(ops(1), spread(ops_rest[:, 0:k, :])).then_inc(d["ops_mid"], 1)
                    need("ops_mid")
                    nc.vector.tensor_tensor(ops_rest[:, 0:k, :], ops_rest[:, 0:k, :], ops(1)[:, :, 0, :],
                                            ALU.subtract).then_inc(d["ops_rest2"], 1)
                    need("ops_rest2")
                    nc.vector.tensor_copy(ops(2), spread(ops_rest[:, 0:k, :])).then_inc(d["ops_lo"], 1)
                    for j in range(k):
                        nc.vector.scalar_tensor_tensor(hits[:, j, :], y[:, s, j, 16:80], 0.5, countdown[:, :],
                                                       ALU.is_gt, ALU.mult).then_inc(d["hits"], 1)
                    if reused(c, 1):
                        dve.wait_ge(d["active2"], c)
                    nc.vector.tensor_scalar(flags[:, 0:k, :], y[:, s, 0:k, 0:3], 0.5, None, ALU.is_gt
                                            ).then_inc(d["flags"], 1)
                    need_tiles("hits")
                    nc.vector.tensor_reduce(best[:, 0:k, :], hits[:, 0:k, :].rearrange("p k (f j) -> p k f j", j=16),
                                            AX, ALU.max).then_inc(d["best"], 1)
                    need("best")
                    nc.vector.tensor_scalar(first[:, 0:k, :], best[:, 0:k, :], -1.0, 16.0, ALU.mult, ALU.add
                                            ).then_inc(d["first"], 1)
                    need("first")
                    for j in range(k):
                        ins = nc.vector.scalar_tensor_tensor(
                            feats[:, s, j, 0:12].rearrange("p (w f) -> p w f", w=3),
                            best[:, j, :].unsqueeze(1).to_broadcast([P, 3, 4]), 0.0,
                            first[:, j, :].unsqueeze(1).to_broadcast([P, 3, 4]), ALU.is_gt, ALU.mult)
                    ins.then_inc(d["feats_nibbles"], 1)

                def tail(c, s, k):
                    def need(name):
                        dve.wait_ge(d[name], c + 1)

                    need("active2")
                    need("y3")
                    nc.vector.tensor_tensor(v3[:, 0:k, :], y3[:, 0:8 * k].rearrange("p (k o) -> p k o", o=8),
                                            b3[:, :].unsqueeze(1).to_broadcast([P, k, 8]), ALU.add
                                            ).then_inc(d["v3"], 1)
                    need("v3")
                    nc.vector.tensor_tensor(added[:, 0:k, :], v3[:, 0:k, 0:3],
                                            picks[:, s, 0:k, 0:1].to_broadcast([P, k, 3]), ALU.mult
                                            ).then_inc(d["added"], 1)
                    nc.vector.tensor_tensor(subbed[:, 0:k, :], v3[:, 0:k, 3:6],
                                            picks[:, s, 0:k, 1:2].to_broadcast([P, k, 3]), ALU.mult
                                            ).then_inc(d["subbed"], 1)
                    need("added")
                    need("subbed")
                    nc.vector.tensor_tensor(value[:, 0:k, :], added[:, 0:k, :], subbed[:, 0:k, :], ALU.add
                                            ).then_inc(d["value"], 1)
                    need("value")
                    nc.vector.tensor_scalar(clipped[:, 0:k, :], value[:, 0:k, :], 0.0, 15.0, ALU.max, ALU.min
                                            ).then_inc(d["clipped"], 1)
                    need("clipped")
                    nc.vector.tensor_scalar_add(shifted[:, 0:k, :], clipped[:, 0:k, :], ROUNDER
                                                ).then_inc(d["shifted"], 1)
                    need("shifted")
                    nc.vector.tensor_scalar_add(rounded[:, 0:k, :], shifted[:, 0:k, :], -ROUNDER
                                                ).then_inc(d["rounded"], 1)
                    need("rounded")
                    need("res")
                    for j in range(k):
                        nc.vector.tensor_tensor(hot[:, j, :, :], digits[:, :, :],
                                                rounded[:, j, 0:2].unsqueeze(2).to_broadcast([P, 2, 16]),
                                                ALU.is_equal).then_inc(d["hot"], 1)
                    nc.vector.scalar_tensor_tensor(carry[:, 0:k], rounded[:, 0:k, 2], 0.5, active[:, s, 0:k],
                                                   ALU.is_gt, ALU.mult).then_inc(d["carry"], 1)
                    dve.wait_ge(d["hot"], c * C + k)
                    for j in range(k):
                        place = res[:, s, j, 128:160]
                        nc.vector.scalar_tensor_tensor(place, hot[:, j, :, :].rearrange("p a b -> p (a b)"),
                                                       active2[:, s, j:j + 1], place, ALU.mult, ALU.add
                                                       ).then_inc(d["placed"], 1)
                    need("carry")
                    nc.vector.tensor_tensor(res[:, s, 0:k, 160], res[:, s, 0:k, 160], carry[:, 0:k], ALU.add
                                            ).then_inc(d["carried"], 1)

                dve.wait_ge(s_w, 8 * 16)
                nc.vector.memset(feats[:, :, :, 12:15], 1.0).then_inc(s_ones, 1)
                nc.vector.memset(feats[:, :, :, 15:16], 0.0).then_inc(s_ones, 1)
                split3(nc.vector, dve.wait_ge, parts, w1[:, :, :], w1_part[0][:, :, :], w1_part[1][:, :, :],
                       w1_part[2][:, :, :], w1_rest[:, :, :])
                dve.wait_ge(parts["lo"], 1)
                nc.vector.tensor_scalar(w1_sum[0][:, :, :], w1_part[0][:, :, :], w1_pick[:, 0:1], None, ALU.mult
                                        ).then_inc(s_w1, 1)
                for i in (1, 2):
                    dve.wait_ge(s_w1, i)
                    nc.vector.scalar_tensor_tensor(w1_sum[i][:, :, :], w1_part[i][:, :, :], w1_pick[:, i:i + 1],
                                                   w1_sum[i - 1][:, :, :], ALU.mult, ALU.add).then_inc(s_w1, 1)
                front(0, 0, C)
                for c, s, k in chunks(dve):
                    if not is_last(c):
                        after = LAST if isinstance(c, int) and c == CHUNKS - 1 else C
                        front(c + 1, 1 - s, after)
                    if reused(c, 1):
                        tail(c - 1, 1 - s, C)
                tail(CHUNKS, 0, LAST)


ROUNDER = 1.5 * 2.0 ** 23

SHAPES = {
    "x": (NODES, D), "wt": (D, D), "bias3": (3, D), "pick3": (3, 3), "w_src": (P, D), "w_dst": (P, D), "ident": (P, P),
    "src": (P, GROUPS, GROUP), "dst": (P, GROUPS, GROUP), "node_no": (P, P), "dist": (P, EDGE_TILES, HEADS), "before": (P, P),
    "w1": (PAIRS, 5, P), "w1_pick": (PAIRS, 3), "w2": (P, 13, P), "w3": (P, 5, 8), "b2": (P, 5), "b3": (P, 8),
    "countdown": (P, 64), "digits": (P, 2, 16),
}


def program(nc, t):
    with ExitStack() as top:
        def sb(name, shape, dt=F32):
            return top.enter_context(nc.sbuf_tensor("k_" + name, shape, dt))

        keep = {
            "src": sb("src", [P, GROUPS, GROUP], I32),
            "dst": sb("dst", [P, GROUPS, GROUP], I32),
            "dist": sb("dist", [P, EDGE_TILES, HEADS]),
            "rel": sb("rel", [P, EDGE_TILES]),
            "bases": sb("bases", [P, GROUPS]),
            "bases_int": sb("bases_int", [1, GROUPS], I32),
            "excess": sb("excess", [P, 4]),
            "general": sb("general", [P, 1], I32),
            "ident": top.enter_context(nc.sbuf_tensor("ident", [P, P], F32)),
            "esrc": top.enter_context(nc.sbuf_tensor("esrc", [P, NODE_TILES * HEADS], F32)),
            "edst": top.enter_context(nc.sbuf_tensor("edst", [P, NODE_TILES * HEADS], F32)),
        }
        banks = [top.enter_context(nc.psum_tensor(f"bank{i}", [P, 512], F32)) for i in range(8)]
        t["h"] = nc.dram_tensor("table_h", (ROWS, ROW), F32).ap()
        t["agg"] = nc.dram_tensor("table_agg", (ROWS, ROW), F32).ap()
        t["maxima"] = nc.dram_tensor("table_maxima", (ROWS, 2 * HEADS), F32).ap()
        t["shifts"] = nc.dram_tensor("table_shifts", (ROWS, 6 * HEADS), BF16).ap()
        project(nc, top, banks, t, keep)
        prepare(nc, top, banks, t, keep)
        _, (general,) = nc.values_load_multi_w_load_instructions(keep["general"][0:1, 0:1], min_val=0, max_val=1)
        branch_semaphores = []
        with nc.If(general):
            attend_any(nc, top, banks, t, keep, branch_semaphores)
        with nc.Else():
            attend_windows(nc, top, banks, t, keep, branch_semaphores)
        finish(nc, top, banks, t, keep)


def layout(x, src, dst, edge_attr_8, L0_gnn_W, L0_gnn_b, L0_gnn_w_att_src, L0_gnn_w_att_dst,
           L0_ffn_Wa, L0_ffn_ba, L0_ffn_Ws, L0_ffn_bs):
    a = {}
    a["x"] = np.zeros((NODES, D), np.float32)
    a["x"][:N] = x
    a["wt"] = L0_gnn_W.T
    a["bias3"] = np.broadcast_to(L0_gnn_b, (3, D))
    a["pick3"] = np.eye(3, dtype=np.float32)
    a["w_src"] = np.broadcast_to(L0_gnn_w_att_src.reshape(1, D), (P, D))
    a["w_dst"] = np.broadcast_to(L0_gnn_w_att_dst.reshape(1, D), (P, D))
    a["ident"] = np.eye(P, dtype=np.float32)
    a["before"] = np.tril(np.ones((P, P), np.float32), -1)
    for name, ends in (("src", src), ("dst", dst)):
        padded = np.full(EDGE_TILES * P, NOWHERE, np.int32)
        padded[:E] = ends
        a[name] = padded.reshape(GROUPS, GROUP, P).transpose(2, 0, 1)
    a["node_no"] = np.broadcast_to(np.arange(P, dtype=np.float32), (P, P))
    dist = np.zeros((EDGE_TILES * P, HEADS), np.float32)
    dist[:E] = edge_attr_8
    a["dist"] = dist.reshape(EDGE_TILES, P, HEADS).transpose(1, 0, 2)

    w1 = np.zeros((PAIRS, 5, P), np.float32)
    w1_pick = np.zeros((PAIRS, 3), np.float32)
    w2 = np.zeros((P, 13, P), np.float32)
    w3 = np.zeros((P, 5, 8), np.float32)
    b2 = np.zeros((P, 5), np.float32)
    b3 = np.zeros((P, 8), np.float32)
    nets = [(L0_ffn_Wa, L0_ffn_ba), (L0_ffn_Ws, L0_ffn_bs)]
    for g, (net, pos) in enumerate(COMBOS):
        w, b = nets[net]
        last = slice(REM * g, REM * (g + 1))
        for part in range(3):
            rows = [(4 * part + pos, w[0][:, NIB_A]), (4 * part + 2 + pos, w[0][:, NIB_B]), (12 + part, b[0])]
            for i in range(3):
                at = OPS_AT + 6 * i + 2 * part
                rows += [(at, w[0][:, OP_ADD_IN]), (at + 1, w[0][:, OP_SUB_IN])]
            for row, units in rows:
                w1[row, g] = units[:P]
                w1[row, 4, last] = units[P:]
                w1_pick[row, part] = 1
        w2[:, g] = w[1][:P, :P].T
        w2[last, 4 + g] = w[1][:P, P:].T
        w2[:, 8 + g, last] = w[1][P:, :P].T
        w2[last, 12, last] = w[1][P:, P:].T
        b2[:, g] = b[1][:P]
        b2[last, 4] = b[1][P:]
        outs = [(3 * net + pos, RESULT)] + [(3 * net + 2, CARRY_OUT)] * pos
        for out, row in outs:
            w3[:, g, out] = w[2][row, :P]
            w3[last, 4, out] = w[2][row, P:]
            b3[:, out] = b[2][row]
    a.update(w1=w1, w1_pick=w1_pick, w2=w2, w3=w3, b2=b2, b3=b3)
    a["countdown"] = np.broadcast_to(np.tile(16.0 - np.arange(16), 4).astype(np.float32), (P, 64))
    a["digits"] = np.broadcast_to(np.arange(16).astype(np.float32), (P, 2, 16))
    return a


def kernel(**inputs):
    import concourse.bacc as bacc
    from concourse.bass_utils import run_bass_kernel_spmd

    arrays = {"in_" + k: np.ascontiguousarray(v) for k, v in layout(**{k: np.asarray(v) for k, v in inputs.items()}
                                                                     ).items()}
    nc = bacc.Bacc("TRN2", target_bir_lowering=False, num_devices=1)
    t = {}
    for name, shape in SHAPES.items():
        assert arrays["in_" + name].shape == shape, name
        dt = mybir.dt.from_np(arrays["in_" + name].dtype)
        t[name] = nc.dram_tensor("in_" + name, shape, dt, kind="ExternalInput").ap()
    t["out"] = nc.dram_tensor("out", (N, D), F32, kind="ExternalOutput").ap()
    program(nc, t)
    return run_bass_kernel_spmd(nc, [arrays], core_ids=[0]).results[0]["out"]
```
